# Optimizing a Trainium2 kernel written in Bass

```python
import numpy as np
import jax
import jax.numpy as jnp

def _softmax(x, axis=-1):
    return jax.nn.softmax(x, axis=axis)

def _gelu(x):
    return jax.nn.gelu(x, approximate=True)

def _silu(x):
    return jax.nn.silu(x)

def _sigmoid(x):
    return jax.nn.sigmoid(x)

def _layernorm(x, axis=-1, eps=1e-05):
    m = jnp.mean(x, axis=axis, keepdims=True)
    v = jnp.var(x, axis=axis, keepdims=True)
    return (x - m) / jnp.sqrt(v + eps)

def _scatter_add(tgt, idx, src, axis=0):
    return tgt.at[idx].add(src)

def _segment_sum(src, seg, n):
    return jax.ops.segment_sum(src, seg, n)
kernel_name = 'mk_xattn_seq_d4_seqx_r4_88f8f2'

def setup_inputs(seed: int=0):
    np.random.seed(seed)
    _w = jnp.asarray

    def _rec_inputs():
        import jax
        import jax.numpy as jnp
        _rk = jax.random.key(seed)
        x = 7.22e-05 + 1 * jax.random.normal(jax.random.fold_in(_rk, 1), (32, 128, 1024), jnp.float32)
        _lenS = 128 - jax.random.randint(jax.random.fold_in(_rk, 7), (32,), 0, max(1, 128 // 4) + 1, jnp.int32)
        _lenS2 = 128 - jax.random.randint(jax.random.fold_in(_rk, 8), (32,), 0, max(1, 128 // 4) + 1, jnp.int32)
        _ctx_4096P = jax.random.normal(jax.random.fold_in(_rk, 11), (32, 16, 1024), jnp.float32)
        _ctx_4096c = jax.random.dirichlet(jax.random.fold_in(_rk, 511), 0.3 * jnp.ones((16,), jnp.float32), (32, 128))
        _ctx_4096t = jnp.einsum('bsk,bkd->bsd', _ctx_4096c, _ctx_4096P)
        _ctx_4096t = _ctx_4096t * jax.lax.rsqrt(jnp.mean(jnp.square(_ctx_4096t)) + 1e-12) * 0.953939
        ctx_4096 = 4.13588e-05 + 0.999923 * (_ctx_4096t + 0.3 * jax.random.normal(jax.random.fold_in(_rk, 611), (32, 128, 1024), jnp.float32))
        _validS = jnp.arange(128)[None, :] < _lenS[:, None]
        _validS2 = jnp.arange(128)[None, :] < _lenS2[:, None]
        _causal = jnp.tril(jnp.ones((128, 128), dtype=bool))
        mask_Bx1x4096_ff1 = jnp.where(jnp.ones((32, 1, 1024), dtype=bool), 1.0, 0.0).astype(jnp.float32)
        return (x, ctx_4096, mask_Bx1x4096_ff1)
    x, ctx_4096, mask_Bx1x4096_ff1 = _rec_inputs()

    def _L0_xattn_setup():
        import jax, jax.numpy as jnp
        import numpy as np
        NUM_HEADS = 8
        CHUNK = 64
        EPS = 1e-05
        NEG = -1000000000.0

        def _chunk_attn(q, k, v, masks, W_in, b_in, W_out, b_out):
            N, C, T = q.shape
            H, Dh = (NUM_HEADS, C // NUM_HEADS)
            nc = T // CHUNK
            Wq, Wk, Wv = jnp.split(W_in, 3, axis=0)
            bq, bk, bv = jnp.split(b_in, 3, axis=0)

            def proj(t, W, b):
                t = t.transpose(0, 2, 1) @ W.T + b
                return t.reshape(N, nc, CHUNK, H, Dh)
            qh = proj(q, Wq, bq)
            kh = proj(k, Wk, bk)
            vh = proj(v, Wv, bv)
            scale = 1.0 / jnp.sqrt(jnp.asarray(Dh, q.dtype))
            scores = jnp.einsum('bnqhd,bnkhd->bnhqk', qh, kh) * scale
            km = masks[:, 0, :].reshape(N, nc, CHUNK)
            scores = scores + jnp.where(km[:, :, None, None, :] > 0, 0.0, NEG)
            attn = jax.nn.softmax(scores, axis=-1)
            out = jnp.einsum('bnhqk,bnkhd->bnqhd', attn, vh).reshape(N, T, C)
            out = out @ W_out.T + b_out
            out = out.transpose(0, 2, 1) * masks
            return out
        key = jax.random.key(seed)
        ks = jax.random.split(key, 8)
        N, C, T = (4, 128, 1024)
        x = jax.random.normal(ks[0], (N, C, T), dtype=jnp.float32)
        q = jax.random.normal(ks[1], (N, C, T), dtype=jnp.float32)
        k = jax.random.normal(ks[2], (N, C, T), dtype=jnp.float32)
        v = jax.random.normal(ks[3], (N, C, T), dtype=jnp.float32)
        masks = jnp.ones((N, 1, T), dtype=jnp.float32)
        s = 1.0 / np.sqrt(C)
        W_in = jax.random.normal(ks[4], (3 * C, C), dtype=jnp.float32) * s
        b_in = jnp.zeros((3 * C,), dtype=jnp.float32)
        W_out = jax.random.normal(ks[5], (C, C), dtype=jnp.float32) * s
        b_out = jnp.zeros((C,), dtype=jnp.float32)
        return {'x': x, 'q': q, 'k': k, 'v': v, 'masks': masks, 'W_in': W_in, 'b_in': b_in, 'W_out': W_out, 'b_out': b_out}
    _L0_xattn_all = _L0_xattn_setup()
    _L0_xattn_in = {k: v for k, v in _L0_xattn_all.items() if k in ('W_in', 'b_in', 'W_out', 'b_out')}
    del _L0_xattn_all

    def _L1_xattn_setup():
        import jax, jax.numpy as jnp
        import numpy as np
        H = 1024
        NH = 32
        NKV = 8
        HD = H // NH
        R = 16
        SCALING = 32.0 / 16.0

        def _lora_linear(x, W, A, B):
            return x @ W + SCALING * (x @ A @ B)
        key = jax.random.key(seed)
        ks = jax.random.split(key, 16)
        d = {'hidden_states': jax.random.normal(ks[0], (4, 256, H), jnp.float32), 'traces': jax.random.normal(ks[1], (4, 256, H), jnp.float32), 'Wq': jax.random.normal(ks[2], (H, H), jnp.float32) * 0.02, 'Aq': jax.random.normal(ks[3], (H, R), jnp.float32) * 0.02, 'Bq': jax.random.normal(ks[4], (R, H), jnp.float32) * 0.02, 'Wk': jax.random.normal(ks[5], (H, NKV * HD), jnp.float32) * 0.02, 'Ak': jax.random.normal(ks[6], (H, R), jnp.float32) * 0.02, 'Bk': jax.random.normal(ks[7], (R, NKV * HD), jnp.float32) * 0.02, 'Wv': jax.random.normal(ks[8], (H, NKV * HD), jnp.float32) * 0.02, 'Av': jax.random.normal(ks[9], (H, R), jnp.float32) * 0.02, 'Bv': jax.random.normal(ks[10], (R, NKV * HD), jnp.float32) * 0.02, 'Wo': jax.random.normal(ks[11], (H, H), jnp.float32) * 0.02, 'Ao': jax.random.normal(ks[12], (H, R), jnp.float32) * 0.02, 'Bo': jax.random.normal(ks[13], (R, H), jnp.float32) * 0.02}
        return d
    _L1_xattn_all = _L1_xattn_setup()
    _L1_xattn_in = {k: v for k, v in _L1_xattn_all.items() if k in ('Wq', 'Aq', 'Bq', 'Wk', 'Ak', 'Bk', 'Wv', 'Av', 'Bv', 'Wo', 'Ao', 'Bo')}
    del _L1_xattn_all

    def _L2_xattn_setup():
        import jax, jax.numpy as jnp
        import numpy as np
        NUM_HEADS = 8
        CHUNK = 64
        EPS = 1e-05
        NEG = -1000000000.0

        def _chunk_attn(q, k, v, masks, W_in, b_in, W_out, b_out):
            N, C, T = q.shape
            H, Dh = (NUM_HEADS, C // NUM_HEADS)
            nc = T // CHUNK
            Wq, Wk, Wv = jnp.split(W_in, 3, axis=0)
            bq, bk, bv = jnp.split(b_in, 3, axis=0)

            def proj(t, W, b):
                t = t.transpose(0, 2, 1) @ W.T + b
                return t.reshape(N, nc, CHUNK, H, Dh)
            qh = proj(q, Wq, bq)
            kh = proj(k, Wk, bk)
            vh = proj(v, Wv, bv)
            scale = 1.0 / jnp.sqrt(jnp.asarray(Dh, q.dtype))
            scores = jnp.einsum('bnqhd,bnkhd->bnhqk', qh, kh) * scale
            km = masks[:, 0, :].reshape(N, nc, CHUNK)
            scores = scores + jnp.where(km[:, :, None, None, :] > 0, 0.0, NEG)
            attn = jax.nn.softmax(scores, axis=-1)
            out = jnp.einsum('bnhqk,bnkhd->bnqhd', attn, vh).reshape(N, T, C)
            out = out @ W_out.T + b_out
            out = out.transpose(0, 2, 1) * masks
            return out
        key = jax.random.key(seed)
        ks = jax.random.split(key, 8)
        N, C, T = (4, 128, 1024)
        x = jax.random.normal(ks[0], (N, C, T), dtype=jnp.float32)
        q = jax.random.normal(ks[1], (N, C, T), dtype=jnp.float32)
        k = jax.random.normal(ks[2], (N, C, T), dtype=jnp.float32)
        v = jax.random.normal(ks[3], (N, C, T), dtype=jnp.float32)
        masks = jnp.ones((N, 1, T), dtype=jnp.float32)
        s = 1.0 / np.sqrt(C)
        W_in = jax.random.normal(ks[4], (3 * C, C), dtype=jnp.float32) * s
        b_in = jnp.zeros((3 * C,), dtype=jnp.float32)
        W_out = jax.random.normal(ks[5], (C, C), dtype=jnp.float32) * s
        b_out = jnp.zeros((C,), dtype=jnp.float32)
        return {'x': x, 'q': q, 'k': k, 'v': v, 'masks': masks, 'W_in': W_in, 'b_in': b_in, 'W_out': W_out, 'b_out': b_out}
    _L2_xattn_all = _L2_xattn_setup()
    _L2_xattn_in = {k: v for k, v in _L2_xattn_all.items() if k in ('W_in', 'b_in', 'W_out', 'b_out')}
    del _L2_xattn_all

    def _L3_xattn_setup():
        import jax, jax.numpy as jnp
        import numpy as np
        B, N, C, K = (8, 1024, 64, 30)
        EPS_BN = 1e-05
        TINY = 1e-20

        def _knn(p, k):
            xx = jnp.sum(p * p, axis=1)
            pd = 2.0 * jnp.einsum('bdn,bdm->bnm', p, p) - xx[:, :, None] - xx[:, None, :]
            return jax.lax.top_k(pd, k)[1]

        def _bn(h, g, b):
            mu = jnp.mean(h, axis=(0, 1, 2), keepdims=True)
            var = jnp.var(h, axis=(0, 1, 2), keepdims=True)
            return (h - mu) * jax.lax.rsqrt(var + EPS_BN) * g + b

        def _forward(x_loc, x, W1, g1, b1, W2, g2, b2, W3, g3, b3, k):
            Bsz = x.shape[0]
            idx = _knn(x_loc, k)
            bidx = jnp.arange(Bsz)[:, None, None]
            pts = x_loc.transpose(0, 2, 1)
            rel = pts[bidx, idx] - pts[:, :, None, :]
            xr, yr, zr = (rel[..., 0], rel[..., 1], rel[..., 2])
            sxy2 = xr * xr + yr * yr
            r2 = sxy2 + zr * zr
            rho = jnp.sqrt(jnp.maximum(r2, TINY))
            sxy = jnp.sqrt(jnp.maximum(sxy2, TINY))
            deg_r = r2 < TINY
            deg_p = sxy2 < TINY
            theta = jnp.arctan2(jnp.where(deg_r, 0.0, zr), jnp.where(deg_r, 1.0, sxy))
            phi = jnp.arctan2(jnp.where(deg_p, 0.0, yr), jnp.where(deg_p, 1.0, xr))
            sph = jnp.stack([rho, theta, phi], axis=-1)
            feat = jnp.concatenate([sph, sph - jnp.mean(sph, axis=-1, keepdims=True)], axis=-1)
            lrelu = lambda h: jax.nn.leaky_relu(h, 0.2)
            h = lrelu(_bn(feat @ W1.T, g1, b1))
            h = lrelu(_bn(h @ W2.T, g2, b2))
            h = lrelu(_bn(h @ W3.T, g3, b3))
            att = jax.nn.softmax(h[..., 0], axis=-1)
            xk = x.transpose(0, 2, 1)[bidx, idx]
            agg = jnp.einsum('bnkc,bnk->bnc', xk, att)
            return x + agg.transpose(0, 2, 1)
        key = jax.random.key(seed)
        ks = jax.random.split(key, 12)
        return {'x_loc': jax.random.normal(ks[0], (B, 3, N), jnp.float32), 'x': jax.random.normal(ks[1], (B, C, N), jnp.float32), 'W1': jax.random.normal(ks[2], (6, 6), jnp.float32) * 0.4, 'g1': 1.0 + 0.1 * jax.random.normal(ks[3], (6,), jnp.float32), 'b1': 0.1 * jax.random.normal(ks[4], (6,), jnp.float32), 'W2': jax.random.normal(ks[5], (3, 6), jnp.float32) * 0.4, 'g2': 1.0 + 0.1 * jax.random.normal(ks[6], (3,), jnp.float32), 'b2': 0.1 * jax.random.normal(ks[7], (3,), jnp.float32), 'W3': jax.random.normal(ks[8], (1, 3), jnp.float32) * 0.4, 'g3': 1.0 + 0.1 * jax.random.normal(ks[9], (1,), jnp.float32), 'b3': 0.1 * jax.random.normal(ks[10], (1,), jnp.float32), 'k': K}
    _L3_xattn_all = _L3_xattn_setup()
    _L3_xattn_in = {k: v for k, v in _L3_xattn_all.items() if k in ('W1', 'g1', 'b1', 'W2', 'g2', 'b2', 'W3', 'g3', 'b3')}
    del _L3_xattn_all
    return {'x': x, 'ctx_4096': ctx_4096, 'mask_Bx1x4096_ff1': mask_Bx1x4096_ff1, 'L0_xattn_W_in': _L0_xattn_in['W_in'], 'L0_xattn_b_in': _L0_xattn_in['b_in'], 'L0_xattn_W_out': _L0_xattn_in['W_out'], 'L0_xattn_b_out': _L0_xattn_in['b_out'], 'L1_xattn_Wq': _L1_xattn_in['Wq'], 'L1_xattn_Aq': _L1_xattn_in['Aq'], 'L1_xattn_Bq': _L1_xattn_in['Bq'], 'L1_xattn_Wk': _L1_xattn_in['Wk'], 'L1_xattn_Ak': _L1_xattn_in['Ak'], 'L1_xattn_Bk': _L1_xattn_in['Bk'], 'L1_xattn_Wv': _L1_xattn_in['Wv'], 'L1_xattn_Av': _L1_xattn_in['Av'], 'L1_xattn_Bv': _L1_xattn_in['Bv'], 'L1_xattn_Wo': _L1_xattn_in['Wo'], 'L1_xattn_Ao': _L1_xattn_in['Ao'], 'L1_xattn_Bo': _L1_xattn_in['Bo'], 'L2_xattn_W_in': _L2_xattn_in['W_in'], 'L2_xattn_b_in': _L2_xattn_in['b_in'], 'L2_xattn_W_out': _L2_xattn_in['W_out'], 'L2_xattn_b_out': _L2_xattn_in['b_out'], 'L3_xattn_W1': _L3_xattn_in['W1'], 'L3_xattn_g1': _L3_xattn_in['g1'], 'L3_xattn_b1': _L3_xattn_in['b1'], 'L3_xattn_W2': _L3_xattn_in['W2'], 'L3_xattn_g2': _L3_xattn_in['g2'], 'L3_xattn_b2': _L3_xattn_in['b2'], 'L3_xattn_W3': _L3_xattn_in['W3'], 'L3_xattn_g3': _L3_xattn_in['g3'], 'L3_xattn_b3': _L3_xattn_in['b3']}

def reference(x, ctx_4096, mask_Bx1x4096_ff1, L0_xattn_W_in, L0_xattn_b_in, L0_xattn_W_out, L0_xattn_b_out, L1_xattn_Wq, L1_xattn_Aq, L1_xattn_Bq, L1_xattn_Wk, L1_xattn_Ak, L1_xattn_Bk, L1_xattn_Wv, L1_xattn_Av, L1_xattn_Bv, L1_xattn_Wo, L1_xattn_Ao, L1_xattn_Bo, L2_xattn_W_in, L2_xattn_b_in, L2_xattn_W_out, L2_xattn_b_out, L3_xattn_W1, L3_xattn_g1, L3_xattn_b1, L3_xattn_W2, L3_xattn_g2, L3_xattn_b2, L3_xattn_W3, L3_xattn_g3, L3_xattn_b3):
    import jax
    import jax.numpy as jnp

    def _L0_xattn_ref(x, q, k, v, masks, W_in, b_in, W_out, b_out):
        import jax, jax.numpy as jnp
        import numpy as np
        NUM_HEADS = 8
        CHUNK = 64
        EPS = 1e-05
        NEG = -1000000000.0

        def _chunk_attn(q, k, v, masks, W_in, b_in, W_out, b_out):
            N, C, T = q.shape
            H, Dh = (NUM_HEADS, C // NUM_HEADS)
            nc = T // CHUNK
            Wq, Wk, Wv = jnp.split(W_in, 3, axis=0)
            bq, bk, bv = jnp.split(b_in, 3, axis=0)

            def proj(t, W, b):
                t = t.transpose(0, 2, 1) @ W.T + b
                return t.reshape(N, nc, CHUNK, H, Dh)
            qh = proj(q, Wq, bq)
            kh = proj(k, Wk, bk)
            vh = proj(v, Wv, bv)
            scale = 1.0 / jnp.sqrt(jnp.asarray(Dh, q.dtype))
            scores = jnp.einsum('bnqhd,bnkhd->bnhqk', qh, kh) * scale
            km = masks[:, 0, :].reshape(N, nc, CHUNK)
            scores = scores + jnp.where(km[:, :, None, None, :] > 0, 0.0, NEG)
            attn = jax.nn.softmax(scores, axis=-1)
            out = jnp.einsum('bnhqk,bnkhd->bnqhd', attn, vh).reshape(N, T, C)
            out = out @ W_out.T + b_out
            out = out.transpose(0, 2, 1) * masks
            return out
        out = _chunk_attn(q, k, v, masks, W_in, b_in, W_out, b_out) + x
        mu = jnp.mean(out, axis=2, keepdims=True)
        var = jnp.mean(jnp.square(out - mu), axis=2, keepdims=True)
        return (out - mu) * jax.lax.rsqrt(var + EPS)

    def _L1_xattn_ref(hidden_states, traces, Wq, Aq, Bq, Wk, Ak, Bk, Wv, Av, Bv, Wo, Ao, Bo):
        import jax, jax.numpy as jnp
        import numpy as np
        H = 1024
        NH = 32
        NKV = 8
        HD = H // NH
        R = 16
        SCALING = 32.0 / 16.0

        def _lora_linear(x, W, A, B):
            return x @ W + SCALING * (x @ A @ B)
        bsz, q_len, _ = hidden_states.shape
        t_len = traces.shape[1]
        groups = NH // NKV
        q = _lora_linear(hidden_states, Wq, Aq, Bq).reshape(bsz, q_len, NH, HD)
        q = jnp.transpose(q, (0, 2, 1, 3))
        k = _lora_linear(traces, Wk, Ak, Bk).reshape(bsz, t_len, NKV, HD)
        v = _lora_linear(traces, Wv, Av, Bv).reshape(bsz, t_len, NKV, HD)
        k = jnp.transpose(k, (0, 2, 1, 3))
        v = jnp.transpose(v, (0, 2, 1, 3))
        k = jnp.repeat(k, groups, axis=1)
        v = jnp.repeat(v, groups, axis=1)
        scores = jnp.einsum('bhqd,bhtd->bhqt', q, k) / jnp.sqrt(jnp.asarray(HD, q.dtype))
        attn = jax.nn.softmax(scores, axis=-1)
        context = jnp.einsum('bhqt,bhtd->bhqd', attn, v)
        context = jnp.transpose(context, (0, 2, 1, 3)).reshape(bsz, q_len, H)
        out = _lora_linear(context, Wo, Ao, Bo)
        return hidden_states + out

    def _L2_xattn_ref(x, q, k, v, masks, W_in, b_in, W_out, b_out):
        import jax, jax.numpy as jnp
        import numpy as np
        NUM_HEADS = 8
        CHUNK = 64
        EPS = 1e-05
        NEG = -1000000000.0

        def _chunk_attn(q, k, v, masks, W_in, b_in, W_out, b_out):
            N, C, T = q.shape
            H, Dh = (NUM_HEADS, C // NUM_HEADS)
            nc = T // CHUNK
            Wq, Wk, Wv = jnp.split(W_in, 3, axis=0)
            bq, bk, bv = jnp.split(b_in, 3, axis=0)

            def proj(t, W, b):
                t = t.transpose(0, 2, 1) @ W.T + b
                return t.reshape(N, nc, CHUNK, H, Dh)
            qh = proj(q, Wq, bq)
            kh = proj(k, Wk, bk)
            vh = proj(v, Wv, bv)
            scale = 1.0 / jnp.sqrt(jnp.asarray(Dh, q.dtype))
            scores = jnp.einsum('bnqhd,bnkhd->bnhqk', qh, kh) * scale
            km = masks[:, 0, :].reshape(N, nc, CHUNK)
            scores = scores + jnp.where(km[:, :, None, None, :] > 0, 0.0, NEG)
            attn = jax.nn.softmax(scores, axis=-1)
            out = jnp.einsum('bnhqk,bnkhd->bnqhd', attn, vh).reshape(N, T, C)
            out = out @ W_out.T + b_out
            out = out.transpose(0, 2, 1) * masks
            return out
        out = _chunk_attn(q, k, v, masks, W_in, b_in, W_out, b_out) + x
        mu = jnp.mean(out, axis=2, keepdims=True)
        var = jnp.mean(jnp.square(out - mu), axis=2, keepdims=True)
        return (out - mu) * jax.lax.rsqrt(var + EPS)

    def _L3_xattn_ref(x_loc, x, W1, g1, b1, W2, g2, b2, W3, g3, b3, k):
        import jax, jax.numpy as jnp
        import numpy as np
        B, N, C, K = (8, 1024, 64, 30)
        EPS_BN = 1e-05
        TINY = 1e-20

        def _knn(p, k):
            xx = jnp.sum(p * p, axis=1)
            pd = 2.0 * jnp.einsum('bdn,bdm->bnm', p, p) - xx[:, :, None] - xx[:, None, :]
            return jax.lax.top_k(pd, k)[1]

        def _bn(h, g, b):
            mu = jnp.mean(h, axis=(0, 1, 2), keepdims=True)
            var = jnp.var(h, axis=(0, 1, 2), keepdims=True)
            return (h - mu) * jax.lax.rsqrt(var + EPS_BN) * g + b

        def _forward(x_loc, x, W1, g1, b1, W2, g2, b2, W3, g3, b3, k):
            Bsz = x.shape[0]
            idx = _knn(x_loc, k)
            bidx = jnp.arange(Bsz)[:, None, None]
            pts = x_loc.transpose(0, 2, 1)
            rel = pts[bidx, idx] - pts[:, :, None, :]
            xr, yr, zr = (rel[..., 0], rel[..., 1], rel[..., 2])
            sxy2 = xr * xr + yr * yr
            r2 = sxy2 + zr * zr
            rho = jnp.sqrt(jnp.maximum(r2, TINY))
            sxy = jnp.sqrt(jnp.maximum(sxy2, TINY))
            deg_r = r2 < TINY
            deg_p = sxy2 < TINY
            theta = jnp.arctan2(jnp.where(deg_r, 0.0, zr), jnp.where(deg_r, 1.0, sxy))
            phi = jnp.arctan2(jnp.where(deg_p, 0.0, yr), jnp.where(deg_p, 1.0, xr))
            sph = jnp.stack([rho, theta, phi], axis=-1)
            feat = jnp.concatenate([sph, sph - jnp.mean(sph, axis=-1, keepdims=True)], axis=-1)
            lrelu = lambda h: jax.nn.leaky_relu(h, 0.2)
            h = lrelu(_bn(feat @ W1.T, g1, b1))
            h = lrelu(_bn(h @ W2.T, g2, b2))
            h = lrelu(_bn(h @ W3.T, g3, b3))
            att = jax.nn.softmax(h[..., 0], axis=-1)
            xk = x.transpose(0, 2, 1)[bidx, idx]
            agg = jnp.einsum('bnkc,bnk->bnc', xk, att)
            return x + agg.transpose(0, 2, 1)
        return _forward(x_loc, x, W1, g1, b1, W2, g2, b2, W3, g3, b3, k)
    x = _L0_xattn_ref(x, ctx_4096, ctx_4096, ctx_4096, mask_Bx1x4096_ff1, L0_xattn_W_in, L0_xattn_b_in, L0_xattn_W_out, L0_xattn_b_out)
    x = _L1_xattn_ref(x, ctx_4096, L1_xattn_Wq, L1_xattn_Aq, L1_xattn_Bq, L1_xattn_Wk, L1_xattn_Ak, L1_xattn_Bk, L1_xattn_Wv, L1_xattn_Av, L1_xattn_Bv, L1_xattn_Wo, L1_xattn_Ao, L1_xattn_Bo)
    x = _L2_xattn_ref(x, ctx_4096, ctx_4096, ctx_4096, mask_Bx1x4096_ff1, L2_xattn_W_in, L2_xattn_b_in, L2_xattn_W_out, L2_xattn_b_out)
    x = _L3_xattn_ref(ctx_4096, x, L3_xattn_W1, L3_xattn_g1, L3_xattn_b1, L3_xattn_W2, L3_xattn_g2, L3_xattn_b2, L3_xattn_W3, L3_xattn_g3, L3_xattn_b3, 30)
    return x

_drawn_inputs = setup_inputs


def setup_inputs(seed=0):
    import zlib

    import numpy as np

    out = dict(_drawn_inputs(seed))
    spreads = {'L0_xattn_b_in': (0.0, 0.368),
     'L0_xattn_b_out': (0.0, 0.536),
     'L2_xattn_b_in': (0.0, 0.335),
     'L2_xattn_b_out': (0.0, 0.531)}
    factors = {'L1_xattn_Aq': 8.0,
     'L1_xattn_Bq': 8.0,
     'L1_xattn_Ak': 8.0,
     'L1_xattn_Bk': 8.0,
     'L3_xattn_g1': 8.0,
     'L3_xattn_b1': 8.0,
     'L3_xattn_g2': 8.0,
     'L3_xattn_b2': 8.0,
     'L3_xattn_W3': 4.743}
    for name, (base, spread) in spreads.items():
        noise = np.random.default_rng([zlib.crc32(name.encode()), seed]).standard_normal(out[name].shape)
        drawn = base * np.exp(spread * noise) if base else spread * noise
        out[name] = jnp.asarray(drawn.astype(out[name].dtype))
    for name, factor in factors.items():
        out[name] = (out[name] * factor).astype(out[name].dtype)
    return out
```

```python
import numpy as np
import concourse.bass as bass
from concourse import mybir
from contextlib import ExitStack

B, C, T = 32, 128, 1024
H0, CHUNK = 8, 64
D0 = C // H0
NH, NKV = 32, 8
HD = T // NH
R = 16
LORA = 32.0 / 16.0
KNN = 30
EPS = 1e-5
NEG = -1.0e9
TINY = 1e-20
P = 128
NT = T // P
KC = T // P
ROW = C + 4
ROUNDS = 4
PAIRS = NT * KNN
DVE_STEPS = 125


def program(nc, x_in, ctx_in, mask_in, w_in, b_qkv, w_out, wq, wk, wv, wo, at, bq, bk, bv, bo,
            mlp_w, consts, out, NB=B):
    f32, u32 = mybir.dt.float32, mybir.dt.uint32
    ALU, ACT, AX = mybir.AluOpType, mybir.ActivationFunctionType, mybir.AxisListType
    TOTAL = NB * PAIRS

    stack = ExitStack()
    with stack:
        def sb(name, shape, dt=f32):
            return stack.enter_context(nc.sbuf_tensor(name, shape, dt))

        def sem(name):
            return stack.enter_context(nc.semaphore(name))

        table = [nc.dram_tensor(f"gather_table{n}", [T, ROW], f32).ap() for n in range(2)]
        x3_dram = nc.dram_tensor("x3_scratch", [NB, P, T], f32).ap()
        sph_dram = nc.dram_tensor("sph_scratch", [NB + 1, P, 3, PAIRS], f32).ap()
        rows_dram = [nc.dram_tensor(f"neighbour_rows{t}", [NB, P, KNN * ROW], f32).ap() for t in range(NT)]

        arena = sb("arena", [P, 3 * B * PAIRS])
        o = 0
        Wq = arena[:, o:o + KC * T].rearrange("p (k n) -> p k n", k=KC); o += KC * T
        Wo = arena[:, o:o + KC * T].rearrange("p (k n) -> p k n", k=KC); o += KC * T
        Wk = arena[:, o:o + KC * 256].rearrange("p (k n) -> p k n", k=KC); o += KC * 256
        Wv = arena[:, o:o + KC * 256].rearrange("p (k n) -> p k n", k=KC); o += KC * 256
        tab = arena[:, o:o + NT * ROW].rearrange("p (t r) -> p t r", t=NT); o += NT * ROW
        xxrow = arena[:, o:o + T]; o += T
        ctx = sb("ctx", [P, T])
        X0 = sb("X0", [P, T])
        X1 = sb("X1", [P, T])
        reg = sb("reg", [P, 4 * T])
        q_sb, kT, V2 = reg[:, 0:T], reg[:, T:2 * T], reg[:, 2 * T:4 * T].rearrange("p (c n) -> p c n", c=16)
        hT = reg[:, 2 * T:3 * T].rearrange("p (k n) -> p k n", k=KC)
        V1 = reg[:, 3 * T:3 * T + 256]
        kexp = sb("kexp", [P, 2048])
        OT = sb("OT", [P, T])
        ctxT = sb("ctxT", [P, NT, P])
        S = [sb(f"S{n}", [P, T]) for n in range(2)]
        ET = sb("ET", [P, T])
        pd = [sb(f"pd{n}", [P, T]) for n in range(2)]
        gbuf = [sb(f"gbuf{n}", [P, KNN, ROW]) for n in range(2)]
        mb = sb("mb", [P, 512])
        maskT = sb("maskT", [P, T])
        m8 = sb("m8", [P, 8 * ROUNDS])
        idx = sb("idx", [P, NT, 8 * ROUNDS], u32)
        idxp = sb("idxp", [P, NT, 8 * ROUNDS], u32)
        crd = sb("crd", [P, NT, KNN, 4])
        own = sb("own", [P, NT, 4])
        rel = OT[:, 0:3 * PAIRS].rearrange("p (a n) -> p a n", a=3)
        tmp = [kexp[:, 2 * PAIRS * n:2 * PAIRS * (n + 1)].rearrange("p (a n) -> p a n", a=2) for n in range(4)]
        sph = sb("sph", [P, 3, PAIRS])
        WL = [sb(f"WL{n}", [P, 4 * P]) for n in range(2)]
        bL = sb("bL", [P, 2, 4])
        bqs = sb("bqs", [P, 2])
        bof = sb("bof", [P, 2])
        con = sb("con", [P, consts.shape[1]])
        ident = con[:, 0:128]
        parity = con[:, 128:256]
        headmask = con[:, 256:264]
        quadmask = con[:, 264:268]
        neghalf = con[:, 268:269]
        negone = con[:, 269:270]
        eps = con[:, 270:271]
        ones_row = con[0:1, 271:399]
        mean_w = con[:, 399:527]
        xxcol = sb("xxcol", [P, NT])
        mx = sb("mx", [P, 16])
        sm = sb("sm", [P, 16])
        bst = sb("bst", [P, 2, 6])
        mv = sb("mv", [P, 2])
        std = sb("std", [P, 1])
        rstd = sb("rstd", [P, 1])
        small = sb("small", [P, 256])
        att_mx = X1[:, 0:NB * NT]
        loraA = gbuf[0][0:R, :, :].rearrange("p a b -> p (a b)")[:, 0:3072]
        loraO = gbuf[1][0:R, :, :].rearrange("p a b -> p (a b)")[:, 0:1024]
        loraB = gbuf[1][0:R, :, :].rearrange("p a b -> p (a b)")[:, 1024:3584]

        def pb(name, n):
            return stack.enter_context(nc.psum_tensor(name, [P, 512 * n], f32))
        SC = [pb("SCA", 2), pb("SCB", 2)]
        TP = pb("TP", 2)
        PD = pb("PD", 1)
        MISC = pb("MISC", 1)

        w_ld, lora_ps, lora_done, bo_ps, prep_done = (sem(n) for n in (
            "w_ld", "lora_ps", "lora_done", "bo_ps", "prep_done"))
        ctx_ld, x_ld, mask_ld, x3_st, table_st, sph_st = (sem(n) for n in (
            "ctx_ld", "x_ld", "mask_ld", "x3_st", "table_st", "sph_st"))
        rows_in = [sem(f"rows_in{n}") for n in range(2)]
        rows_st = [sem(f"rows_st{n}") for n in range(2)]
        ctxT_ready, xx_ready, pd_ready, q_ready, k_ready, v_ready, v1_ready, hT_ready = (sem(n) for n in (
            "ctxT_ready", "xx_ready", "pd_ready", "q_ready", "k_ready", "v_ready", "v1_ready", "hT_ready"))
        scores_ready, probsT_ready, av_ready, oproj_ready, x3T_ready = (sem(n) for n in (
            "scores_ready", "probsT_ready", "av_ready", "oproj_ready", "x3T_ready"))
        sq_done, xx_evac, ctxT_evac, pd_evac, q_evac, k_evac, v1_evac, hT_evac = (sem(n) for n in (
            "sq_done", "xx_evac", "ctxT_evac", "pd_evac", "q_evac", "k_evac", "v1_evac", "hT_evac"))
        kexp_done, exp_done, et_evac, ot_evac, std_done, tab_done, sqrt_done, atan_done = (sem(n) for n in (
            "kexp_done", "exp_done", "et_evac", "ot_evac", "std_done", "tab_done", "sqrt_done", "atan_done"))
        dve_step, v2_evac, front_done, probs_done, topk_done, oproj_used, xl_done, var_done = (sem(n) for n in (
            "dve_step", "v2_evac", "front_done", "probs_done", "topk_done", "oproj_used", "xl_done", "var_done"))
        idxp_done, own_saved, rel_done, sq_in, atan_in, sph_done, crd_done = (sem(n) for n in (
            "idxp_done", "own_saved", "rel_done", "sq_in", "atan_in", "sph_done", "crd_done"))
        rows_ld = [sem(f"rows_ld{n}") for n in range(4)]
        mlp_ld, lin_done, h_used, stat_in, stat_ps, tstd_done, coef_done, att_in, att_exp, att_done = (sem(n) for n in (
            "mlp_ld", "lin_done", "h_used", "stat_in", "stat_ps", "tstd_done", "coef_done", "att_in", "att_exp", "att_done"))
        x3_ld, weighted, agg_ready, agg_used, out_st = (sem(n) for n in (
            "x3_ld", "weighted", "agg_ready", "agg_used", "out_st"))

        CW = min(960, TOTAL)
        NCH = TOTAL // CW
        SUB = CW // 2
        chan = [arena[:, c * TOTAL:(c + 1) * TOTAL] for c in range(3)]
        hid = [gbuf[j // 4][:, :, :].rearrange("p k r -> p (k r)")[:, (j % 4) * CW:(j % 4 + 1) * CW] for j in range(6)]
        hstat = reg[:, 0:6 * 6 * 2 * NCH].rearrange("p (j n) -> p j n", j=6)
        free = arena[:, TOTAL:3 * TOTAL] if NB == B else arena[:, 3 * TOTAL:3 * TOTAL + 2 * KNN * ROW]
        NBUF = 4
        rbuf = [gbuf[0][:, :, :], gbuf[1][:, :, :]] + [
            free[:, n * KNN * ROW:(n + 1) * KNN * ROW].rearrange("p (k r) -> p k r", k=KNN) for n in range(2)]
        w1, g1, b1 = small[:, 0:36].rearrange("p (j f) -> p j f", j=6), small[:, 36:42], small[:, 42:48]
        w2, g2, b2 = small[:, 48:66], small[:, 66:69], small[:, 69:72]
        w3, g3, b3 = small[:, 72:75], small[:, 75:76], small[:, 76:77]
        weff = small[:, 80:98]
        wnorm = small[:, 98:116]
        wsum = small[:, 116:122]
        hmv = small[:, 124:136].rearrange("p (j s) -> p j s", j=6)
        stat = small[:, 136:142]
        mean = small[:, 142:148]
        tstd = small[:, 148:154]
        gain = small[:, 154:160]
        shift = small[:, 160:166]
        zero = small[:, 166:167]
        dev = small[:, 168:174]

        def spherical_act(act, i, _):
            A = nc.scalar.activation
            act.wait_ge(sq_in, i + 1)
            A(tmp[0][:, :, :], tmp[0][:, :, :], ACT.Sqrt).then_inc(sqrt_done, 1)
            act.wait_ge(atan_in, i + 1)
            A(tmp[2][:, :, :], tmp[2][:, :, :], ACT.Arctan).then_inc(atan_done, 1)

        ROUNDS_AT = [3, 3, 3, 3, 2, 2, 2, 2, 3, 3, 3, 3]
        PD_AT = {2: 2, 3: 3, 4: 4, 6: 5, 8: 6, 10: 7}
        BLK = stack.enter_context(nc.Block())
        waited = sem("waited")

        def settle(eng):
            eng.sem_inc(waited, 1)

        WCHUNKS = [(W, kc, c0, 256 if W in (Wk, Wv) else 512)
                   for W in (Wq, Wk, Wv, Wo) for kc in range(KC)
                   for c0 in (range(0, 256, 256) if W in (Wk, Wv) else range(0, T, 512))]
        A_OF = {id(Wq): loraA[:, 0:1024], id(Wk): loraA[:, 1024:2048], id(Wv): loraA[:, 2048:3072], id(Wo): loraO}
        B_OF = {id(Wq): loraB[:, 0:1024], id(Wk): loraB[:, 1024:1280], id(Wv): loraB[:, 1280:1536],
                id(Wo): loraB[:, 1536:2560]}
        N_WLD = 16 * (4 + 4 + 3 + 4 + 2 + 1)

        @BLK.sync
        def _(sp):
            for W, d in ((Wq, wq), (Wk, wk), (Wv, wv), (Wo, wo)):
                sp.dma_start(W, d.rearrange("(k p) n -> p k n", p=P)).then_inc(w_ld, 16)
            for n in range(4):
                sp.dma_start((loraA[:, 1024 * n:1024 * n + 1024] if n < 3 else loraO), at[n, :, :]).then_inc(w_ld, 16)
            for (lo, hi), d in (((0, 1024), bq), ((1024, 1280), bk), ((1280, 1536), bv), ((1536, 2560), bo)):
                sp.dma_start(loraB[:, lo:hi], d).then_inc(w_ld, 16)
            for n in range(2):
                sp.dma_start(WL[n][:, 0:384], w_in[n, :, :]).then_inc(w_ld, 16)
            sp.dma_start(WL[0][:, 384:512], w_out[0, :, :]).then_inc(w_ld, 16)
            sp.dma_start(WL[1][:, 384:512], w_out[1, :, :]).then_inc(w_ld, 16)
            sp.dma_start(bL[:, :, :], b_qkv).then_inc(w_ld, 16)
            sp.dma_start(con[:, :], consts).then_inc(w_ld, 16)
            with sp.Fori(0, NB) as i:
                sp.wait_ge(sph_done, i + 2)
                sp.dma_start(sph_dram[i, :, :, :], sph[:, :, :]).then_inc(sph_st, 16)
                for t in range(NT):
                    sp.wait_ge(rows_in[t % 2], i * (NT // 2 * KNN * 16) + (t // 2 + 1) * KNN * 16)
                    sp.dma_start(rows_dram[t][i, :, :],
                                 gbuf[t % 2][:, :, :].rearrange("p k r -> p (k r)")).then_inc(rows_st[t % 2], 16)
            sp.wait_ge(sph_done, NB + 2)
            sp.dma_start(sph_dram[NB, :, :, :], sph[:, :, :]).then_inc(sph_st, 16)
            for n in range(2):
                sp.wait_ge(rows_st[n], 16 * NB * NT // 2 + 16)
            sp.wait_ge(sph_st, 16 * (NB + 2))
            sp.wait_ge(x3_st, 16 * (NB + 1))
            sp.wait_ge(table_st, 16 * (NB + 1))
            sp.wait_ge(sph_done, NB + 2)
            for c in range(3):
                sp.dma_start(chan[c].rearrange("p (b n) -> p b n", b=NB),
                             sph_dram[1:NB + 1, :, c, :].rearrange("b p n -> p b n")).then_inc(mlp_ld, 16)
            sp.dma_start(small[:, 0:mlp_w.shape[0]], mlp_w.partition_broadcast(P)).then_inc(mlp_ld, 16)
            sp.wait_ge(att_done, 1)
            with sp.Fori(0, NB) as i:
                sp.wait_ge(agg_ready, i * NT + NBUF)
                sp.dma_start(X0[:, :], x3_dram[i, :, :]).then_inc(x3_ld, 16)
                for t in range(NT):
                    sp.wait_ge(agg_ready, i * NT + t + 1)
                    sp.dma_start(rbuf[t % NBUF].rearrange("p k r -> p (k r)"),
                                 rows_dram[t][i, :, :]).then_inc(rows_ld[t % NBUF], 16)
            sp.wait_ge(out_st, 16 * (NB + 1))

        @BLK.gpsimd
        def _(pool):
            nc.gpsimd.memset(crd[:, :, :, :], 0.0).then_inc(crd_done, 1)
            pool.sem_inc(crd_done, 1)
            for n in range(2):
                pool.sem_inc(rows_st[n], 16)
            pool.wait_ge(prep_done, 1)
            with pool.Fori(0, NB // 2) as pair:
                for odd in range(2):
                    i = pair * 2 + odd
                    pool.wait_ge(table_st, i * 16 + 32)
                    pool.wait_ge(idxp_done, i + 1)
                    for t in range(NT):
                        n = t % 2
                        pool.wait_ge(rows_st[n], i * (16 * NT // 2) + 16 * (t // 2) + 16)
                        pool.wait_ge(crd_done, i * NT + t + 1)
                        settle(pool)
                        for k in range(KNN):
                            nc.gpsimd.indirect_dma_start(
                                gbuf[n][:, k, :], None, table[odd],
                                bass.IndirectOffsetOnAxis(ap=idxp[:, t, k:k + 1], axis=0)).then_inc(rows_in[n], 16)
                        if t == 0:
                            pool.wait_ge(rel_done, i + 1)
                        if t >= 1:
                            pool.wait_ge(rows_in[1 - n], i * (NT // 2 * KNN * 16) + ((t - 1) // 2 + 1) * KNN * 16)
                            settle(pool)
                            nc.gpsimd.tensor_copy(crd[:, t - 1, :, :], gbuf[1 - n][:, :, C:ROW]).then_inc(crd_done, 1)
                    pool.wait_ge(rows_in[1], i * (NT // 2 * KNN * 16) + NT // 2 * KNN * 16)
                    settle(pool)
                    nc.gpsimd.tensor_copy(crd[:, NT - 1, :, :], gbuf[1][:, :, C:ROW]).then_inc(crd_done, 1)

        @BLK.tensor
        def _(pe):
            mm = nc.tensor.matmul
            pe.wait_ge(w_ld, N_WLD)
            for n, (W, kc, c0, w) in enumerate(WCHUNKS):
                if n >= 2:
                    pe.wait_ge(lora_done, n - 1)
                mm(SC[n % 2][:, 0:w], A_OF[id(W)][:, kc * P:(kc + 1) * P], B_OF[id(W)][:, c0:c0 + w],
                   start=True, stop=True).then_inc(lora_ps, 1)
            for n in range(2):
                last = mm(MISC[:, n:n + 1], WL[n][:, 384:512], bL[:, n, 2:3], start=True, stop=True)
            last.then_inc(bo_ps, 1)
            pe.wait_ge(prep_done, 1)

            with pe.Fori(0, NB) as i:
                def distances(t):
                    for h in range(2):
                        if 2 * t + h:
                            pe.wait_ge(pd_evac, i * 16 + 2 * t + h)
                        mm(PD[:, :], ctx[:, t * P:(t + 1) * P], ctx[:, h * 512:(h + 1) * 512], start=True, stop=False)
                        mm(PD[:, :], ones_row, xxrow[0:1, h * 512:(h + 1) * 512], start=False, stop=True)\
                            .then_inc(pd_ready, 1)

                def groups(l, scores, values):
                    pe.wait_ge(q_evac, i * 3 + l + 1)
                    scores(0)
                    for g in range(4):
                        n = 4 * l + g
                        if n in PD_AT:
                            distances(PD_AT[n])
                        if g < 3:
                            scores(g + 1)
                        pe.wait_ge(probs_done, i * 12 + n + 1)
                        for b in range(2):
                            for j in range(4):
                                last = nc.tensor.transpose(TP[:, b * 512 + j * P:b * 512 + (j + 1) * P],
                                                           S[g % 2][:, b * 512 + j * P:b * 512 + (j + 1) * P], ident)
                        last.then_inc(probsT_ready, 1)
                        pe.wait_ge(et_evac, i * 12 + n + 1)
                        if n:
                            pe.wait_ge(ot_evac, i * 12 + n)
                        values(g)
                    pe.wait_ge(ot_evac, i * 12 + 4 * l + 4)

                def score_bank(l, g):
                    n = 4 * l + g
                    if g == 1:
                        pe.wait_ge(k_evac, i * 3 + l + 1)
                    if g >= 2:
                        pe.wait_ge(front_done, i * 12 + n - 1)
                    pe.wait_ge(kexp_done, i * 12 + n + 1)

                def chunk_attention(l):
                    w = WL[l // 2]
                    if l:
                        pe.wait_ge(oproj_used, i * 3 + l)
                    for h in range(2):
                        last = mm(SC[0][:, h * 512:(h + 1) * 512], w[:, 0:128], ctx[:, h * 512:(h + 1) * 512],
                                  start=True, stop=True)
                    last.then_inc(q_ready, 1)
                    for h in range(2):
                        last = mm(SC[1][:, h * 512:(h + 1) * 512], w[:, 128:256], ctx[:, h * 512:(h + 1) * 512],
                                  start=True, stop=True)
                    last.then_inc(k_ready, 1)
                    for half in range(2):
                        if half:
                            pe.wait_ge(v2_evac, i * 4 + l + 1)
                        for c in range(8):
                            n = half * 8 + c
                            for h in range(2):
                                last = mm(TP[64 * h:64 * h + 64, c * P:(c + 1) * P],
                                          ctx[:, n * CHUNK:(n + 1) * CHUNK], w[:, 256:384], start=True, stop=True)
                        last.then_inc(v_ready, 1)
                    pe.wait_ge(v2_evac, i * 4 + l + 2)

                    def scores(g):
                        score_bank(l, g)
                        for j in range(4):
                            c = 4 * g + j
                            last = mm(SC[g % 2][64 * (j % 2):64 * (j % 2) + 64, (j // 2) * 512:(j // 2 + 1) * 512],
                                      q_sb[:, c * CHUNK:(c + 1) * CHUNK],
                                      kexp.rearrange("p (h t) -> p h t", h=H0)[:, :, j * CHUNK:(j + 1) * CHUNK],
                                      start=True, stop=True)
                        last.then_inc(scores_ready, 1)

                    def values(g):
                        for b in range(2):
                            for half in range(2):
                                for j in range(4):
                                    last = mm(MISC[32 * j:32 * j + 32, (2 * b + half) * 64:(2 * b + half + 1) * 64],
                                              V2[:, 4 * g + 2 * b + half, 32 * j:32 * j + 32],
                                              ET[:, b * 512 + j * P + 64 * half:b * 512 + j * P + 64 * half + 64],
                                              start=True, stop=True)
                        last.then_inc(av_ready, 1)

                    groups(l, scores, values)
                    for h in range(2):
                        last = mm(SC[0][:, h * 512:(h + 1) * 512], w[:, 384:512], OT[:, h * 512:(h + 1) * 512],
                                  start=True, stop=True)
                    last.then_inc(oproj_ready, 1)

                pe.wait_ge(ctx_ld, i * 16 + 16)
                for t in range(NT):
                    last = nc.tensor.transpose(SC[0][:, t * P:(t + 1) * P], ctx[:, t * P:(t + 1) * P], ident)
                last.then_inc(ctxT_ready, 1)
                pe.wait_ge(sq_done, i + 1)
                for h in range(2):
                    mm(TP[0:1, h * 512:(h + 1) * 512], neghalf, ET[:, h * 512:(h + 1) * 512], start=True, stop=True)
                for t in range(NT):
                    last = mm(MISC[:, t:t + 1], ET[:, t * P:(t + 1) * P], negone, start=True, stop=True)
                last.then_inc(xx_ready, 1)
                pe.wait_ge(xx_evac, i * 2 + 2)
                distances(0)
                distances(1)
                pe.wait_ge(ctxT_evac, i + 1)

                chunk_attention(0)

                for c in range(2):
                    for kc in range(KC):
                        last = mm(SC[1][:, c * P:(c + 1) * P], Wk[:, kc, c * P:(c + 1) * P], ctxT[:, kc, :],
                                  start=(kc == 0), stop=(kc == KC - 1))
                last.then_inc(k_ready, 1)
                for kc in range(KC):
                    last = mm(MISC[:, 0:256], ctxT[:, kc, :], Wv[:, kc, :], start=(kc == 0), stop=(kc == KC - 1))
                last.then_inc(v1_ready, 1)
                pe.wait_ge(xl_done, i * 3 + 1)
                for kc in range(KC):
                    last = nc.tensor.transpose(TP[:, kc * P:(kc + 1) * P], X1[:, kc * P:(kc + 1) * P], ident)
                last.then_inc(hT_ready, 1)
                pe.wait_ge(hT_evac, i + 1)
                for c in range(KC):
                    for kc in range(KC):
                        last = mm(SC[0][:, c * P:(c + 1) * P], Wq[:, kc, c * P:(c + 1) * P], hT[:, kc, :],
                                  start=(kc == 0), stop=(kc == KC - 1))
                last.then_inc(q_ready, 1)
                pe.wait_ge(v1_evac, i + 1)

                def scores1(g):
                    score_bank(1, g)
                    for b in range(2):
                        c = 2 * g + b
                        last = mm(SC[g % 2][:, b * 512:(b + 1) * 512], q_sb[:, c * P:(c + 1) * P],
                                  kexp[:, (c // 4) * 512:(c // 4 + 1) * 512], start=True, stop=True)
                    last.then_inc(scores_ready, 1)

                def values1(g):
                    for b in range(2):
                        c = 2 * g + b
                        for j in range(4):
                            h = c // 4 * 4 + j
                            last = mm(MISC[32 * j:32 * j + 32, b * P:(b + 1) * P], V1[:, h * HD:(h + 1) * HD],
                                      ET[:, b * 512 + j * P:b * 512 + (j + 1) * P], start=True, stop=True)
                    last.then_inc(av_ready, 1)

                groups(1, scores1, values1)
                for h in range(2):
                    for c in range(KC):
                        last = mm(SC[0][:, h * 512:(h + 1) * 512], OT[:, c * P:(c + 1) * P],
                                  Wo[:, c, h * 512:(h + 1) * 512], start=(c == 0), stop=(c == KC - 1))
                last.then_inc(oproj_ready, 1)

                chunk_attention(2)
                pe.wait_ge(xl_done, i * 3 + 3)
                for t in range(NT):
                    last = nc.tensor.transpose(TP[:, t * P:(t + 1) * P], X0[:, t * P:(t + 1) * P], ident)
                last.then_inc(x3T_ready, 1)

            for n in range(6):
                pe.wait_ge(stat_in, n + 1)
                w = 6 if n < 2 else 3 if n < 4 else 1
                mm(PD[:, 0:w], mean_w, stat[:, 0:w], start=True, stop=True).then_inc(stat_ps, 1)
            pe.sem_inc(agg_ready, NBUF)
            with pe.Fori(0, NB) as i:
                for t in range(NT):
                    pe.wait_ge(weighted, i * NT + t + 1)
                    pe.wait_ge(agg_used, i * NT + t + 1)
                    for k in range(KNN):
                        mm(SC[t % 2][:, 0:P], rbuf[t % NBUF][:, k, 0:C], ident, start=(k == 0), stop=False)
                    if t == 0:
                        pe.wait_ge(x3_ld, i * 16 + 16)
                    mm(SC[t % 2][:, 0:P], ident, X0[:, t * P:(t + 1) * P], start=False, stop=True)\
                        .then_inc(agg_ready, 1)

        @BLK.scalar
        def _(act):
            A = nc.scalar.activation
            act.sem_inc(x3_st, 16)
            act.sem_inc(table_st, 16)
            act.wait_ge(w_ld, N_WLD)
            for n in range(2):
                A(bqs[:, n:n + 1], bL[:, n, 0:1], ACT.Copy, scale=0.25)
            with act.Fori(0, NB // 2) as pair:
                for odd in range(2):
                    i = pair * 2 + odd

                    def distances(t):
                        for h in range(2):
                            act.wait_ge(pd_ready, i * 16 + 2 * t + h + 1)
                            if t >= 2 and h == 0:
                                act.wait_ge(topk_done, i * NT + t - 1)
                            A(pd[t % 2][:, h * 512:(h + 1) * 512], PD[:, :], ACT.Identity,
                              bias=xxcol[:, t:t + 1], scale=2.0).then_inc(pd_evac, 1)

                    def groups(l, expand, scale):
                        expand(0)
                        for g in range(4):
                            n = 4 * l + g
                            if n in PD_AT:
                                distances(PD_AT[n])
                            if g < 3:
                                if l != 1:
                                    act.wait_ge(scores_ready, i * 12 + n + 1)
                                expand(g + 1)
                            act.wait_ge(front_done, i * 12 + n + 1)
                            A(S[g % 2][:, :], S[g % 2][:, :], ACT.Exp, scale=scale).then_inc(exp_done, 1)
                            act.wait_ge(probsT_ready, i * 12 + n + 1)
                            A(ET[:, :], TP[:, :], ACT.Copy).then_inc(et_evac, 1)
                            act.wait_ge(av_ready, i * 12 + n + 1)
                            A(OT[:, g * 256:(g + 1) * 256], MISC[:, 0:256], ACT.Copy).then_inc(ot_evac, 1)

                    def chunk_attention(l):
                        b = l // 2
                        act.wait_ge(q_ready, i * 3 + l + 1)
                        A(q_sb, SC[0][:, :], ACT.Identity, bias=bqs[:, b:b + 1], scale=0.25).then_inc(q_evac, 1)
                        act.wait_ge(k_ready, i * 3 + l + 1)
                        A(kT, SC[1][:, :], ACT.Identity, bias=bL[:, b, 1:2]).then_inc(k_evac, 1)
                        act.wait_ge(k_evac, i * 3 + l + 1)

                        def expand(g):
                            for h in range(H0):
                                last = A(kexp[:, h * 256:(h + 1) * 256], kT[:, g * 256:(g + 1) * 256], ACT.Copy,
                                         scale=headmask[:, h:h + 1])
                            last.then_inc(kexp_done, 1)

                        groups(l, expand, 1.0)
                        act.wait_ge(var_done, i * 2 + b + 1)
                        A(std[:, :], mv[:, 1:2], ACT.Sqrt, bias=eps).then_inc(std_done, 1)

                    act.dma_start(ctx[:, :], ctx_in[i, :, :]).then_inc(ctx_ld, 16)
                    mrow = mask_in[i, :, :]
                    halves = mrow.rearrange("a (c h k) -> a c h k", h=2, k=CHUNK)
                    for h in range(2):
                        act.dma_start(mb[64 * h:64 * h + 64, :].rearrange("p (c k) -> p c k", k=CHUNK),
                                      halves[0, :, h, :].partition_broadcast(64)).then_inc(mask_ld, 16)
                    act.dma_start(maskT[:, :], mrow[0, :].partition_broadcast(P)).then_inc(mask_ld, 16)
                    act.wait_ge(ctx_ld, i * 16 + 16)
                    A(ET[:, :], ctx[:, :], ACT.Square).then_inc(sq_done, 1)
                    act.wait_ge(x3_st, i * 16 + 16)
                    act.dma_start(X0[:, :], x_in[i, :, :]).then_inc(x_ld, 16)
                    act.wait_ge(ctxT_ready, i + 1)
                    act.wait_ge(own_saved, i + 1)
                    A(ctxT[:, :, :].rearrange("p t c -> p (t c)"), SC[0][:, :], ACT.Copy).then_inc(ctxT_evac, 1)
                    act.wait_ge(xx_ready, i + 1)
                    A(xxrow[0:1, :], TP[0:1, :], ACT.Copy).then_inc(xx_evac, 1)
                    A(xxcol[:, :], MISC[:, 0:NT], ACT.Copy).then_inc(xx_evac, 1)
                    act.wait_ge(xx_evac, i * 2 + 2)
                    distances(0)
                    distances(1)
                    act.wait_ge(sph_done, i + 1)

                    chunk_attention(0)

                    act.wait_ge(k_ready, i * 3 + 2)
                    halves = kexp.rearrange("p (c j t) -> p c j t", c=4, j=4)[:, 0:2, :, :]
                    for j in range(4):
                        last = A(halves[:, :, j, :], SC[1][:, 0:256].rearrange("p (c t) -> p c t", c=2), ACT.Copy,
                                 scale=quadmask[:, j:j + 1])
                    last.then_inc(k_evac, 1)
                    act.wait_ge(v1_ready, i + 1)
                    A(V1, MISC[:, 0:256], ACT.Copy).then_inc(v1_evac, 1)
                    act.wait_ge(hT_ready, i + 1)
                    A(hT.rearrange("p k n -> p (k n)"), TP[:, :], ACT.Copy).then_inc(hT_evac, 1)
                    act.wait_ge(q_ready, i * 3 + 2)
                    A(q_sb, SC[0][:, :], ACT.Copy).then_inc(q_evac, 1)
                    act.wait_ge(k_evac, i * 3 + 2)

                    def expand1(g):
                        act.sem_inc(kexp_done, 1)

                    groups(1, expand1, float(HD) ** -0.5)

                    chunk_attention(2)

                    act.wait_ge(xl_done, i * 3 + 3)
                    act.dma_start(x3_dram[i, :, :], X0[:, :]).then_inc(x3_st, 16)
                    act.wait_ge(table_st, i * 16 + 16)
                    act.wait_ge(x3T_ready, i + 1)
                    A(tab[:, :, 0:C], TP[:, :].rearrange("p (t c) -> p t c", t=NT), ACT.Copy).then_inc(tab_done, 1)
                    A(tab[:, :, C:ROW], ctxT[:, :, 0:4], ACT.Copy).then_inc(tab_done, 1)
                    act.wait_ge(tab_done, i * 2 + 2)
                    act.dma_start(table[odd].rearrange("(t p) r -> p t r", p=P), tab).then_inc(table_st, 16)

                    spherical_act(act, i, 0)
            spherical_act(act, NB, 0)

            act.wait_ge(mlp_ld, 64)
            n = 0
            act.wait_ge(coef_done, 1)
            for p in range(2):
                if p:
                    act.wait_ge(stat_ps, 2)
                    A(tstd[:, 0:6], PD[:, 0:6], ACT.Sqrt, bias=eps).then_inc(tstd_done, 1)
                    act.wait_ge(coef_done, 2)
                for c in range(NCH):
                    for j in range(6):
                        if n >= 6:
                            act.wait_ge(h_used, n - 5)
                        w = weff if p == 0 else wnorm
                        A(hid[j], chan[0][:, c * CW:(c + 1) * CW], ACT.Identity, scale=w[:, 3 * j:3 * j + 1],
                          bias=(zero if p == 0 else shift[:, j:j + 1])).then_inc(lin_done, 1)
                        n += 1
            act.wait_ge(stat_ps, 4)
            A(tstd[:, 0:3], PD[:, 0:3], ACT.Sqrt, bias=eps).then_inc(tstd_done, 1)
            act.wait_ge(coef_done, 3)
            for c in range(NCH):
                for m in range(3):
                    act.wait_ge(h_used, n - (5 if c == 0 else 2))
                    A(hid[m], chan[m][:, c * CW:(c + 1) * CW], ACT.Identity, scale=gain[:, m:m + 1],
                      bias=shift[:, m:m + 1]).then_inc(lin_done, 1)
                    n += 1
            act.wait_ge(stat_ps, 6)
            A(tstd[:, 0:1], PD[:, 0:1], ACT.Sqrt, bias=eps).then_inc(tstd_done, 1)
            act.wait_ge(coef_done, 4)
            A(chan[1], chan[0], ACT.Identity, scale=gain[:, 0:1], bias=shift[:, 0:1]).then_inc(lin_done, 1)
            act.wait_ge(att_in, 1)
            A(chan[0], chan[0], ACT.Exp).then_inc(att_exp, 1)
            act.sem_inc(agg_used, 2)
            act.sem_inc(out_st, 16)
            with act.Fori(0, NB) as i:
                act.wait_ge(out_st, i * 16 + 16)
                for t in range(NT):
                    act.wait_ge(agg_ready, i * NT + t + 1 + NBUF)
                    A(X1[:, t * P:(t + 1) * P], SC[t % 2][:, 0:P], ACT.Copy).then_inc(agg_used, 1)
                act.wait_ge(agg_used, i * NT + NT + 2)
                act.dma_start(out[i, :, :], X1[:, :]).then_inc(out_st, 16)

        @BLK.vector
        def _(dve):
            V = nc.vector
            dve.sem_inc(own_saved, 1)
            dve.sem_inc(sph_done, 1)
            V.memset(own[:, :, :], 0.0)
            dve.wait_ge(w_ld, N_WLD)
            for n, (W, kc, c0, w) in enumerate(WCHUNKS):
                dve.wait_ge(lora_ps, n + 1)
                V.scalar_tensor_tensor(W[:, kc, c0:c0 + w], SC[n % 2][:, 0:w], LORA, W[:, kc, c0:c0 + w],
                                       ALU.mult, ALU.add).then_inc(lora_done, 1)
            dve.wait_ge(lora_done, len(WCHUNKS))
            dve.wait_ge(bo_ps, 1)
            V.tensor_tensor(bof[:, :], MISC[:, 0:2], bL[:, :, 3], ALU.add).then_inc(prep_done, 1)
            dve.wait_ge(prep_done, 1)

            def spherical(i, step):
                dve.wait_ge(crd_done, i * NT + 2)
                for c in range(3):
                    last = V.tensor_tensor(rel[:, c, :].rearrange("p (t k) -> p t k", t=NT), crd[:, :, :, c],
                                           own[:, :, c].unsqueeze(2).broadcast_to([P, NT, KNN]), ALU.subtract)
                last.then_inc(rel_done, 1)
                dve.wait_ge(rel_done, i + 1)
                r_xy, den, t2, t3 = tmp
                step(V.tensor_tensor(t2[:, :, :], rel[:, 0:2, :], rel[:, 0:2, :], ALU.mult))
                V.tensor_tensor(t3[:, 0, :], rel[:, 2, :], rel[:, 2, :], ALU.mult)
                step(V.tensor_tensor(den[:, 0, :], t2[:, 0, :], t2[:, 1, :], ALU.add))
                step(V.tensor_tensor(den[:, 1, :], den[:, 0, :], t3[:, 0, :], ALU.add))
                V.tensor_scalar(t3[:, :, :], den[:, :, :], TINY, None, ALU.is_ge)
                V.tensor_scalar(r_xy[:, :, :], den[:, :, :], TINY, None, ALU.max).then_inc(sq_in, 1)
                dve.wait_ge(sqrt_done, i + 1)
                dve.wait_ge(sph_st, i * 16 + 16)
                V.tensor_copy(sph[:, 0, :], r_xy[:, 1, :])
                V.scalar_tensor_tensor(den[:, 0, :], rel[:, 0, :], -1.0, rel[:, 0, :], ALU.mult, ALU.max)
                V.tensor_copy(den[:, 1, :], r_xy[:, 0, :])
                step(V.scalar_tensor_tensor(t2[:, :, :], rel[:, 1:3, :], -1.0, rel[:, 1:3, :], ALU.mult, ALU.max))
                num = t2
                step(V.tensor_tensor(r_xy[:, :, :], num[:, :, :], den[:, :, :], ALU.max))
                step(V.tensor_scalar(r_xy[:, :, :], r_xy[:, :, :], 1e-30, None, ALU.max))
                step(V.reciprocal(r_xy[:, :, :], r_xy[:, :, :]))
                big = S[0][:, 0:2 * PAIRS].rearrange("p (a n) -> p a n", a=2)
                corr = S[1][:, 0:2 * PAIRS].rearrange("p (a n) -> p a n", a=2)
                V.tensor_tensor(big, num[:, :, :], den[:, :, :], ALU.is_gt)
                step(V.tensor_tensor(num[:, :, :], num[:, :, :], den[:, :, :], ALU.min))
                V.tensor_tensor(num[:, :, :], num[:, :, :], r_xy[:, :, :], ALU.mult).then_inc(atan_in, 1)
                dve.wait_ge(atan_in, i + 1)
                V.tensor_scalar(r_xy[:, :, :], rel[:, 1:3, :], 0.0, -2.0, ALU.is_lt, ALU.mult)
                step(V.tensor_scalar(den[:, 0, :], rel[:, 0, :], 0.0, None, ALU.is_lt))
                step(V.tensor_scalar(r_xy[:, :, :], r_xy[:, :, :], 1.0, None, ALU.add))
                dve.wait_ge(atan_done, i + 1)
                a = num
                step(V.tensor_scalar(corr, a[:, :, :], -2.0, float(np.pi / 2), ALU.mult, ALU.add))
                step(V.tensor_tensor(corr, corr, big, ALU.mult))
                step(V.tensor_tensor(a[:, :, :], a[:, :, :], corr, ALU.add))
                step(V.tensor_scalar(corr[:, 0, :], a[:, 0, :], -2.0, float(np.pi), ALU.mult, ALU.add))
                step(V.tensor_tensor(corr[:, 0, :], corr[:, 0, :], den[:, 0, :], ALU.mult))
                step(V.tensor_tensor(a[:, 0, :], a[:, 0, :], corr[:, 0, :], ALU.add))
                step(V.tensor_tensor(a[:, :, :], a[:, :, :], r_xy[:, :, :], ALU.mult))
                V.tensor_tensor(sph[:, 1, :], a[:, 1, :], t3[:, 1, :], ALU.mult)
                step(V.tensor_tensor(sph[:, 2, :], a[:, 0, :], t3[:, 0, :], ALU.mult))
                dve.sem_inc(sph_done, 1)

            dve.sem_inc(sph_st, 16)
            with dve.Fori(0, NB) as i:
                chain = [0]

                def step(ins):
                    chain[0] += 1
                    ins.then_inc(dve_step, 1)
                    dve.wait_ge(dve_step, i * DVE_STEPS + chain[0])

                rounds = [0]

                def search_round():
                    t, r = divmod(rounds[0], ROUNDS)
                    rounds[0] += 1
                    buf = pd[t % 2]
                    if r == 0:
                        dve.wait_ge(pd_evac, i * 16 + 2 * t + 2)
                    m = m8[:, 8 * r:8 * r + 8]
                    settle(dve)
                    step(V.max(m, buf[:, :]))
                    settle(dve)
                    last = V.max_index(idx[:, t, 8 * r:8 * r + 8], m, buf[:, :])
                    if r < ROUNDS - 1:
                        step(V.match_replace(buf[:, :], m, buf[:, :], -3.0e38))
                    else:
                        last.then_inc(topk_done, 1)

                def groups(l, front, keys):
                    for g in range(4):
                        n = 4 * l + g
                        s = S[g % 2]
                        dve.wait_ge(scores_ready, i * 12 + n + 1)
                        if n >= 2:
                            dve.wait_ge(probsT_ready, i * 12 + n - 1)
                        front(g, s)
                        dve.wait_ge(front_done, i * 12 + n + 1)
                        search_round()
                        dve.wait_ge(exp_done, i * 12 + n + 1)
                        rows = T // keys
                        e = s[:, :].rearrange("p (r k) -> p r k", k=keys)
                        step(V.reduce_sum(sm[:, 0:rows], e, AX.X))
                        step(V.reciprocal(sm[:, 0:rows], sm[:, 0:rows]))
                        V.tensor_tensor(e, e, sm[:, 0:rows].unsqueeze(2).broadcast_to([P, rows, keys]), ALU.mult)\
                            .then_inc(probs_done, 1)
                        for _ in range(ROUNDS_AT[n] - 1):
                            search_round()

                def chunk_attention(l, x_res, y):
                    b = l // 2
                    for half in range(2):
                        dve.wait_ge(v_ready, i * 4 + l + half + 1)
                        V.tensor_tensor(V2[:, half * 8:half * 8 + 8, :], TP[:, :].rearrange("p (c n) -> p c n", c=8),
                                        parity.unsqueeze(1).broadcast_to([P, 8, P]), ALU.mult).then_inc(v2_evac, 1)

                    def front(g, s):
                        rows = s[:, :].rearrange("p (b h k) -> p b h k", b=2, h=H0)
                        bias = mb[:, g * 128:(g + 1) * 128].rearrange("p (b k) -> p b k", b=2)
                        for b_ in range(2):
                            last = V.tensor_tensor(rows[:, b_, :, :],
                                                   SC[g % 2][:, b_ * 512:(b_ + 1) * 512].rearrange("p (h k) -> p h k", h=H0),
                                                   bias[:, b_, :].unsqueeze(1).broadcast_to([P, H0, CHUNK]), ALU.add)
                        step(last)
                        e = s[:, :].rearrange("p (r k) -> p r k", k=CHUNK)
                        step(V.reduce_max(mx[:, :], e, AX.X))
                        V.tensor_tensor(e, e, mx[:, :].unsqueeze(2).broadcast_to([P, 16, CHUNK]), ALU.subtract)\
                            .then_inc(front_done, 1)

                    groups(l, front, CHUNK)
                    dve.wait_ge(oproj_ready, i * 3 + l + 1)
                    V.scalar_tensor_tensor(y[:, :], SC[0][:, :], bof[:, b:b + 1], maskT[:, :], ALU.add, ALU.mult)\
                        .then_inc(oproj_used, 1)
                    dve.wait_ge(oproj_used, i * 3 + l + 1)
                    if l == 0:
                        dve.wait_ge(x_ld, i * 16 + 16)
                    step(V.tensor_tensor(y[:, :], y[:, :], x_res[:, :], ALU.add))
                    for h in range(2):
                        last = V.bn_stats(bst[:, h, :], y[:, h * 512:(h + 1) * 512])
                    step(last)
                    settle(dve)
                    V.bn_aggr(mv[:, :], bst[:, :, :].rearrange("p a b -> p (a b)")).then_inc(var_done, 1)
                    dve.wait_ge(std_done, i * 2 + b + 1)
                    step(V.reciprocal(rstd[:, :], std[:, :]))
                    V.tensor_scalar(y[:, :], y[:, :], mv[:, 0:1], rstd[:, 0:1], ALU.subtract, ALU.mult)\
                        .then_inc(xl_done, 1)

                dve.wait_ge(mask_ld, i * 48 + 48)
                step(V.tensor_scalar(mb[:, :], mb[:, :], 0.0, NEG, ALU.is_le, ALU.mult))
                chunk_attention(0, X0, X1)

                def front1(g, s):
                    sc = SC[g % 2][:, :].rearrange("p (r k) -> p r k", k=P)
                    step(V.reduce_max(mx[:, 0:8], sc, AX.X))
                    V.tensor_tensor(s[:, :].rearrange("p (r k) -> p r k", k=P), sc,
                                    mx[:, 0:8].unsqueeze(2).broadcast_to([P, 8, P]), ALU.subtract)\
                        .then_inc(front_done, 1)

                groups(1, front1, P)
                dve.wait_ge(oproj_ready, i * 3 + 2)
                V.tensor_tensor(X1[:, :], SC[0][:, :], X1[:, :], ALU.add).then_inc(xl_done, 1)
                dve.wait_ge(xl_done, i * 3 + 2)
                dve.sem_inc(oproj_used, 1)
                chunk_attention(2, X1, X0)

                dve.wait_ge(crd_done, i * NT + 2)
                dve.wait_ge(topk_done, i * NT + NT)
                V.tensor_copy(idxp[:, :, :], idx[:, :, :]).then_inc(idxp_done, 1)
                spherical(i, step)
                V.tensor_copy(own[:, :, :], ctxT[:, :, 0:4]).then_inc(own_saved, 1)
                assert chain[0] == DVE_STEPS, chain[0]
                dve.wait_ge(own_saved, i + 2)
            tail = [0]

            def step_tail(ins):
                tail[0] += 1
                ins.then_inc(dve_step, 1)
                dve.wait_ge(dve_step, NB * DVE_STEPS + tail[0])

            spherical(NB, step_tail)
            step = step_tail
            dve.wait_ge(mlp_ld, 64)
            step(V.reduce_sum(wsum, w1[:, :, 3:6], AX.X))
            step(V.tensor_scalar(wsum, wsum, -1.0 / 3.0, None, ALU.mult))
            we = weff.rearrange("p (j f) -> p j f", j=6)
            step(V.tensor_tensor(we, w1[:, :, 0:3], w1[:, :, 3:6], ALU.add))
            V.memset(zero, 0.0)
            step(V.tensor_tensor(we, we, wsum.unsqueeze(2).broadcast_to([P, 6, 3]), ALU.add))
            dve.sem_inc(coef_done, 1)

            norms = [0]

            def batch_norm(width, g, b):
                settle(dve)
                for j in range(width):
                    last = V.bn_aggr(hmv[:, j, :], hstat[:, j, :])
                step(last)
                step(V.tensor_copy(stat[:, 0:width], hmv[:, 0:width, 0]))
                dve.sem_inc(stat_in, 1)
                dve.wait_ge(stat_ps, 2 * norms[0] + 1)
                step(V.tensor_copy(mean[:, 0:width], PD[:, 0:width]))
                step(V.tensor_tensor(dev[:, 0:width], hmv[:, 0:width, 0], mean[:, 0:width], ALU.subtract))
                step(V.tensor_tensor(dev[:, 0:width], dev[:, 0:width], dev[:, 0:width], ALU.mult))
                step(V.tensor_tensor(stat[:, 0:width], dev[:, 0:width], hmv[:, 0:width, 1], ALU.add))
                dve.sem_inc(stat_in, 1)
                norms[0] += 1
                dve.wait_ge(tstd_done, norms[0])
                step(V.reciprocal(gain[:, 0:width], tstd[:, 0:width]))
                step(V.tensor_tensor(gain[:, 0:width], gain[:, 0:width], g, ALU.mult))
                step(V.tensor_tensor(dev[:, 0:width], gain[:, 0:width], mean[:, 0:width], ALU.mult))
                step(V.tensor_tensor(shift[:, 0:width], b, dev[:, 0:width], ALU.subtract))

            n = 0
            for p in range(2):
                w = weff if p == 0 else wnorm
                for c in range(NCH):
                    cols = slice(c * CW, (c + 1) * CW)
                    for j in range(6):
                        dve.wait_ge(lin_done, n + 1)
                        n += 1
                        for f in (1, 2):
                            step(V.scalar_tensor_tensor(hid[j], chan[f][:, cols], w[:, 3 * j + f:3 * j + f + 1], hid[j],
                                                        ALU.mult, ALU.add))
                        if p == 0:
                            for h in range(2):
                                last = V.bn_stats(hstat[:, j, (2 * c + h) * 6:(2 * c + h + 1) * 6],
                                                  hid[j][:, h * SUB:(h + 1) * SUB])
                            last.then_inc(h_used, 1)
                        else:
                            step(V.scalar_tensor_tensor(hid[j], hid[j], 0.2, hid[j], ALU.mult, ALU.max))
                    if p:
                        for m in range(3):
                            step(V.tensor_scalar(chan[m][:, cols], hid[0], w2[:, 6 * m:6 * m + 1], None, ALU.mult))
                            for j in range(1, 6):
                                last = V.scalar_tensor_tensor(chan[m][:, cols], hid[j], w2[:, 6 * m + j:6 * m + j + 1],
                                                              chan[m][:, cols], ALU.mult, ALU.add)
                                step(last)
                        dve.sem_inc(h_used, 6)
                        for m in range(3):
                            for h in range(2):
                                step(V.bn_stats(hstat[:, m, (2 * c + h) * 6:(2 * c + h + 1) * 6],
                                                chan[m][:, c * CW + h * SUB:c * CW + (h + 1) * SUB]))
                if p == 0:
                    dve.wait_ge(h_used, n)
                    batch_norm(6, g1, b1)
                    step(V.tensor_tensor(wnorm.rearrange("p (j f) -> p j f", j=6), we,
                                         gain.unsqueeze(2).broadcast_to([P, 6, 3]), ALU.mult))
                else:
                    batch_norm(3, g2, b2)
                dve.sem_inc(coef_done, 1)
            for c in range(NCH):
                cols = slice(c * CW, (c + 1) * CW)
                for m in range(3):
                    dve.wait_ge(lin_done, n + 1)
                    n += 1
                    step(V.scalar_tensor_tensor(hid[m], hid[m], 0.2, hid[m], ALU.mult, ALU.max))
                step(V.tensor_scalar(chan[0][:, cols], hid[0], w3[:, 0:1], None, ALU.mult))
                for m in (1, 2):
                    step(V.scalar_tensor_tensor(chan[0][:, cols], hid[m], w3[:, m:m + 1], chan[0][:, cols],
                                                ALU.mult, ALU.add))
                dve.sem_inc(h_used, 3)
                for h in range(2):
                    step(V.bn_stats(hstat[:, 0, (2 * c + h) * 6:(2 * c + h + 1) * 6],
                                    chan[0][:, c * CW + h * SUB:c * CW + (h + 1) * SUB]))
            batch_norm(1, g3, b3)
            dve.sem_inc(coef_done, 1)
            dve.wait_ge(lin_done, n + 1)
            step(V.scalar_tensor_tensor(chan[0], chan[1], 0.2, chan[1], ALU.mult, ALU.max))
            a = chan[0].rearrange("p (r k) -> p r k", k=KNN)
            over = [P, NB * NT, KNN]
            step(V.reduce_max(att_mx, a, AX.X))
            V.tensor_tensor(a, a, att_mx.unsqueeze(2).broadcast_to(over), ALU.subtract).then_inc(att_in, 1)
            dve.wait_ge(att_exp, 1)
            step(V.reduce_sum(att_mx, a, AX.X))
            step(V.reciprocal(att_mx, att_mx))
            V.tensor_tensor(a, a, att_mx.unsqueeze(2).broadcast_to(over), ALU.mult).then_inc(att_done, 1)
            dve.wait_ge(att_done, 1)
            with dve.Fori(0, NB) as i:
                for t in range(NT):
                    b = rbuf[t % NBUF]
                    dve.wait_ge(rows_ld[t % NBUF], i * (NT // NBUF * 16) + (t // NBUF + 1) * 16)
                    weights = arena[:, bass.ds(i * PAIRS + t * KNN, KNN)]
                    V.tensor_tensor(b[:, :, 0:C], b[:, :, 0:C], weights.unsqueeze(2).broadcast_to([P, KNN, C]),
                                    ALU.mult).then_inc(weighted, 1)


def constants():
    p = np.arange(P)
    c = np.zeros((P, 528), np.float32)
    c[:, 0:128] = np.eye(P)
    c[:, 128:256] = (p[:, None] // 64) == (p[None, :] // D0) % 2
    c[:, 256:264] = (p[:, None] // D0) == np.arange(H0)[None, :]
    c[:, 264:268] = (p[:, None] // HD) == np.arange(4)[None, :]
    c[:, 268] = -0.5
    c[:, 269] = -1.0
    c[:, 270] = EPS
    c[:, 271:399] = 1.0
    c[:, 399:527] = 1.0 / P
    return c


def layout(d):
    g = lambda n: np.asarray(d[n])
    t = lambda a: np.ascontiguousarray(a)
    heads = np.arange(T).reshape(2, 4, NH // NKV, HD).transpose(0, 2, 1, 3).reshape(-1)
    bias = np.stack([np.concatenate([g(f"L{l}_xattn_b_in").reshape(3, C), g(f"L{l}_xattn_b_out").reshape(1, C)])
                     for l in (0, 2)])
    return {
        "x": t(g("x")), "ctx": t(g("ctx_4096")), "mask": t(g("mask_Bx1x4096_ff1")),
        "w_in": t(np.stack([g(f"L{l}_xattn_W_in").T for l in (0, 2)])),
        "b_qkv": t(bias.transpose(2, 0, 1)),
        "w_out": t(np.stack([g(f"L{l}_xattn_W_out").T for l in (0, 2)])),
        "wq": t(g("L1_xattn_Wq")[:, heads]), "wk": t(g("L1_xattn_Wk")), "wv": t(g("L1_xattn_Wv")), "wo": t(g("L1_xattn_Wo")[heads]),
        "at": t(np.stack([g(f"L1_xattn_A{n}").T for n in "qkv"] + [g("L1_xattn_Ao")[heads].T])),
        "bq": t(g("L1_xattn_Bq")[:, heads]), "bk": t(g("L1_xattn_Bk")), "bv": t(g("L1_xattn_Bv")), "bo": t(g("L1_xattn_Bo")),
        "mlp_w": t(np.concatenate([g(f"L3_xattn_{n}{l}").reshape(-1) for l in (1, 2, 3) for n in ("W", "g", "b")])),
        "consts": constants(),
    }


def kernel(**inputs):
    import concourse.bacc as bacc
    from concourse.bass_utils import run_bass_kernel_spmd

    nc = bacc.Bacc("TRN2", target_bir_lowering=False, num_devices=1)
    arrays = layout(inputs)
    aps = [nc.dram_tensor(f"in_{n}", a.shape, mybir.dt.from_np(a.dtype), kind="ExternalInput").ap()
           for n, a in arrays.items()]
    out = nc.dram_tensor("out", (B, C, T), mybir.dt.float32, kind="ExternalOutput").ap()
    program(nc, *aps, out)
    r = run_bass_kernel_spmd(nc, [{f"in_{n}": a for n, a in arrays.items()}], core_ids=[0])
    return r.results[0]["out"]
```

```python
import numpy as np
import concourse.bass as bass
from concourse import mybir
from contextlib import ExitStack

B, C, T = 32, 128, 1024
H0, CHUNK = 8, 64
D0 = C // H0
NH, NKV = 32, 8
HD = T // NH
R = 16
LORA = 32.0 / 16.0
KNN = 30
EPS = 1e-5
NEG = -1.0e9
TINY = 1e-20
P = 128
NT = T // P
KC = T // P
ROW = C + 4
ROUNDS = 4
PAIRS = NT * KNN
FOLD = 7
COPY_AFTER = 8
DVE_STEPS = 125


def program(nc, x_in, ctx_in, mask_in, w_in, b_qkv, w_out, wq, wk, wv, wo, at, bq, bk, bv, bo,
            mlp_w, consts, out, NB=B):
    f32, u32 = mybir.dt.float32, mybir.dt.uint32
    ALU, ACT, AX = mybir.AluOpType, mybir.ActivationFunctionType, mybir.AxisListType
    TOTAL = NB * PAIRS

    stack = ExitStack()
    with stack:
        def sb(name, shape, dt=f32):
            return stack.enter_context(nc.sbuf_tensor(name, shape, dt))

        def sem(name):
            return stack.enter_context(nc.semaphore(name))

        table = [nc.dram_tensor(f"gather_table{n}", [T, ROW], f32).ap() for n in range(2)]
        x3_dram = nc.dram_tensor("x3_scratch", [NB, P, T], f32).ap()
        sph_dram = nc.dram_tensor("sph_scratch", [NB + 2, P, 3, PAIRS], f32).ap()
        rows_dram = [nc.dram_tensor(f"neighbour_rows{t}", [NB, P, KNN * ROW], f32).ap() for t in range(NT)]

        arena = sb("arena", [P, 3 * B * PAIRS])
        o = 0
        Wq = arena[:, o:o + KC * T].rearrange("p (k n) -> p k n", k=KC); o += KC * T
        Wo = arena[:, o:o + KC * T].rearrange("p (k n) -> p k n", k=KC); o += KC * T
        Wk = arena[:, o:o + KC * 256].rearrange("p (k n) -> p k n", k=KC); o += KC * 256
        Wv = arena[:, o:o + KC * 256].rearrange("p (k n) -> p k n", k=KC); o += KC * 256
        tab = arena[:, o:o + NT * ROW].rearrange("p (t r) -> p t r", t=NT); o += NT * ROW
        xxrow = arena[:, o:o + T]; o += T
        ctx = sb("ctx", [P, T])
        X0 = sb("X0", [P, T])
        X1 = sb("X1", [P, T])
        reg = sb("reg", [P, 4 * T])
        q_sb, kT, V2 = reg[:, 0:T], reg[:, T:2 * T], reg[:, 2 * T:4 * T].rearrange("p (c n) -> p c n", c=16)
        V2flat = reg[:, 2 * T:4 * T].rearrange("p (c e d) -> p c e d", e=2, d=D0)
        hT = reg[:, 2 * T:3 * T].rearrange("p (k n) -> p k n", k=KC)
        V1 = reg[:, 3 * T:3 * T + 256]
        kexp = sb("kexp", [P, 2048])
        OT = sb("OT", [P, T])
        ctxT = sb("ctxT", [P, NT, P])
        S = [sb(f"S{n}", [P, T]) for n in range(2)]
        ET = sb("ET", [P, T])
        rel = OT[:, 0:3 * PAIRS].rearrange("p (a n) -> p a n", a=3)
        tmp = [w[:, 2 * PAIRS * n:2 * PAIRS * (n + 1)].rearrange("p (a n) -> p a n", a=2)
               for w, n in ((S[0], 0), (S[0], 1), (S[1], 0), (S[1], 1), (X1, 0))]
        pd = [sb(f"pd{n}", [P, T]) for n in range(2)]
        gbuf = [sb(f"gbuf{n}", [P, KNN, ROW]) for n in range(2)]
        mb = sb("mb", [P, 512])
        maskT = sb("maskT", [P, T])
        m8 = sb("m8", [P, 8 * ROUNDS])
        idx = sb("idx", [P, NT, 8 * ROUNDS], u32)
        idxp = sb("idxp", [P, 2, NT, KNN], u32)
        crd = sb("crd", [P, NT, KNN, 4])
        own = sb("own", [P, NT, 4])
        sph = sb("sph", [P, 3, PAIRS])
        WL = [sb(f"WL{n}", [P, 4 * P]) for n in range(2)]
        bL = sb("bL", [P, 2, 4])
        bqs = sb("bqs", [P, 2])
        bof = sb("bof", [P, 2])
        con = sb("con", [P, consts.shape[1]])
        ident = con[:, 0:128]
        parity = con[:, 128:256]
        headmask = con[:, 256:264]
        quadmask = con[:, 264:268]
        neghalf = con[:, 268:269]
        negone = con[:, 269:270]
        eps = con[:, 270:271]
        ones_row = con[0:1, 271:399]
        mean_w = con[:, 399:527]
        xxcol = sb("xxcol", [P, NT])
        mx = sb("mx", [P, 16])
        sm = sb("sm", [P, 16])
        bst = sb("bst", [P, 2, 6])
        mv = sb("mv", [P, 2])
        std = sb("std", [P, 1])
        rstd = sb("rstd", [P, 1])
        small = sb("small", [P, 180])
        att_mx = X1[:, 0:NB * NT]
        loraA = gbuf[0][0:R, :, :].rearrange("p a b -> p (a b)")[:, 0:3072]
        loraO = gbuf[1][0:R, :, :].rearrange("p a b -> p (a b)")[:, 0:1024]
        loraB = gbuf[1][0:R, :, :].rearrange("p a b -> p (a b)")[:, 1024:3584]

        def pb(name, n):
            return stack.enter_context(nc.psum_tensor(name, [P, 512 * n], f32))
        SC = [pb("SCA", 2), pb("SCB", 2)]
        TP = pb("TP", 2)
        PD = pb("PD", 1)
        MISC = pb("MISC", 1)

        w_ld, lora_ps, lora_done, bo_ps, prep_done = (sem(n) for n in (
            "w_ld", "lora_ps", "lora_done", "bo_ps", "prep_done"))
        ctx_ld, x_ld, mask_ld, x3_st, table_st, sph_st = (sem(n) for n in (
            "ctx_ld", "x_ld", "mask_ld", "x3_st", "table_st", "sph_st"))
        rows_in = [sem(f"rows_in{n}") for n in range(2)]
        rows_st = [sem(f"rows_st{n}") for n in range(2)]
        ctxT_ready, xx_ready, pd_ready, q_ready, k_ready, v_ready, v1_ready, hT_ready = (sem(n) for n in (
            "ctxT_ready", "xx_ready", "pd_ready", "q_ready", "k_ready", "v_ready", "v1_ready", "hT_ready"))
        scores_ready, probsT_ready, av_ready, oproj_ready, x3T_ready = (sem(n) for n in (
            "scores_ready", "probsT_ready", "av_ready", "oproj_ready", "x3T_ready"))
        sq_done, xx_evac, ctxT_evac, pd_evac, q_evac, k_evac, v1_evac, hT_evac = (sem(n) for n in (
            "sq_done", "xx_evac", "ctxT_evac", "pd_evac", "q_evac", "k_evac", "v1_evac", "hT_evac"))
        kexp_done, exp_done, et_evac, ot_evac, std_done, tab_done, sqrt_done, atan_done = (sem(n) for n in (
            "kexp_done", "exp_done", "et_evac", "ot_evac", "std_done", "tab_done", "sqrt_done", "atan_done"))
        dve_step, v2_evac, front_done, probs_done, topk_done, oproj_used, xl_done, var_done = (sem(n) for n in (
            "dve_step", "v2_evac", "front_done", "probs_done", "topk_done", "oproj_used", "xl_done", "var_done"))
        idxp_done, own_saved, rel_done, sq_in, atan_in, sph_done, crd_done = (sem(n) for n in (
            "idxp_done", "own_saved", "rel_done", "sq_in", "atan_in", "sph_done", "crd_done"))
        rows_ld = [sem(f"rows_ld{n}") for n in range(4)]
        mlp_ld, lin_done, h_used, stat_in, stat_ps, tstd_done, coef_done, att_in, att_exp, att_done = (sem(n) for n in (
            "mlp_ld", "lin_done", "h_used", "stat_in", "stat_ps", "tstd_done", "coef_done", "att_in", "att_exp", "att_done"))
        x3_ld, products, weighted, agg_ready, agg_used, out_st = (sem(n) for n in (
            "x3_ld", "products", "weighted", "agg_ready", "agg_used", "out_st"))

        CW = min(960, TOTAL)
        NCH = TOTAL // CW
        SUB = CW // 2
        chan = [arena[:, c * TOTAL:(c + 1) * TOTAL] for c in range(3)]
        hid = [gbuf[j // 4][:, :, :].rearrange("p k r -> p (k r)")[:, (j % 4) * CW:(j % 4 + 1) * CW] for j in range(6)]
        hstat = reg[:, 0:6 * 6 * 2 * NCH].rearrange("p (j n) -> p j n", j=6)
        free = arena[:, TOTAL:3 * TOTAL] if NB == B else arena[:, 3 * TOTAL:3 * TOTAL + 2 * KNN * ROW]
        NBUF = 4
        rbuf = [gbuf[0][:, :, :], gbuf[1][:, :, :]] + [
            free[:, n * KNN * ROW:(n + 1) * KNN * ROW].rearrange("p (k r) -> p k r", k=KNN) for n in range(2)]
        w1, g1, b1 = small[:, 0:36].rearrange("p (j f) -> p j f", j=6), small[:, 36:42], small[:, 42:48]
        w2, g2, b2 = small[:, 48:66], small[:, 66:69], small[:, 69:72]
        w3, g3, b3 = small[:, 72:75], small[:, 75:76], small[:, 76:77]
        weff = small[:, 80:98]
        wnorm = small[:, 98:116]
        wsum = small[:, 116:122]
        hmv = small[:, 124:136].rearrange("p (j s) -> p j s", j=6)
        stat = small[:, 136:142]
        mean = small[:, 142:148]
        tstd = small[:, 148:154]
        gain = small[:, 154:160]
        shift = small[:, 160:166]
        zero = small[:, 166:167]
        dev = small[:, 168:174]

        def spherical_act(act, i):
            A = nc.scalar.activation
            act.wait_ge(sq_in, i + 1)
            A(tmp[0][:, :, :], tmp[0][:, :, :], ACT.Sqrt).then_inc(sqrt_done, 1)
            act.wait_ge(atan_in, i + 1)
            A(tmp[2][:, :, :], tmp[2][:, :, :], ACT.Arctan).then_inc(atan_done, 1)

        ROUNDS_AT = (1, 1, 1, 1, 1, 1, 1, 1, 0, 1, 1, 0)
        DIST_AT = {0: (2, 0), 1: (2, 1), 4: (4, 1), 5: (5, 0), 6: (5, 1), 7: (6, 0), 8: (7, 1)}
        NORMS_AT = {9: 0, 10: 1, 11: 2}
        BLK = stack.enter_context(nc.Block())
        waited = sem("waited")

        def settle(eng):
            eng.sem_inc(waited, 1)

        WCHUNKS = [(W, kc, w) for W, w in ((Wq, T), (Wk, NKV * HD), (Wv, NKV * HD), (Wo, T)) for kc in range(KC)]
        A_OF = {id(Wq): loraA[:, 0:1024], id(Wk): loraA[:, 1024:2048], id(Wv): loraA[:, 2048:3072], id(Wo): loraO}
        B_OF = {id(Wq): loraB[:, 0:1024], id(Wk): loraB[:, 1024:1280], id(Wv): loraB[:, 1280:1536],
                id(Wo): loraB[:, 1536:2560]}
        N_WLD = 16 * (4 + 4 + 3 + 4 + 2 + 1)

        @BLK.sync
        def _(sp):
            for W, d in ((Wq, wq), (Wk, wk), (Wv, wv), (Wo, wo)):
                sp.dma_start(W, d.rearrange("(k p) n -> p k n", p=P)).then_inc(w_ld, 16)
            for n in range(4):
                sp.dma_start((loraA[:, 1024 * n:1024 * n + 1024] if n < 3 else loraO), at[n, :, :]).then_inc(w_ld, 16)
            for (lo, hi), d in (((0, 1024), bq), ((1024, 1280), bk), ((1280, 1536), bv), ((1536, 2560), bo)):
                sp.dma_start(loraB[:, lo:hi], d).then_inc(w_ld, 16)
            for n in range(2):
                sp.dma_start(WL[n][:, 0:384], w_in[n, :, :]).then_inc(w_ld, 16)
            sp.dma_start(WL[0][:, 384:512], w_out[0, :, :]).then_inc(w_ld, 16)
            sp.dma_start(WL[1][:, 384:512], w_out[1, :, :]).then_inc(w_ld, 16)
            sp.dma_start(bL[:, :, :], b_qkv).then_inc(w_ld, 16)
            sp.dma_start(con[:, :], consts).then_inc(w_ld, 16)
            with sp.Fori(0, NB) as i:
                sp.wait_ge(sph_done, i + 2)
                sp.dma_start(sph_dram[i, :, :, :], sph[:, :, :]).then_inc(sph_st, 16)
                for t in range(NT):
                    sp.wait_ge(rows_in[t % 2], i * (NT // 2 * KNN * 16) + (t // 2 + 1) * KNN * 16)
                    sp.dma_start(rows_dram[t][i, :, :],
                                 gbuf[t % 2][:, :, :].rearrange("p k r -> p (k r)")).then_inc(rows_st[t % 2], 16)
            for b in (NB, NB + 1):
                sp.wait_ge(sph_done, b + 2)
                sp.dma_start(sph_dram[b, :, :, :], sph[:, :, :]).then_inc(sph_st, 16)
            for n in range(2):
                sp.wait_ge(rows_st[n], 16 * NB * NT // 2 + 16)
            sp.wait_ge(sph_st, 16 * (NB + 3))
            sp.wait_ge(x3_st, 16 * (NB + 1))
            sp.wait_ge(table_st, 16 * (NB + 1))
            for c in range(3):
                sp.dma_start(chan[c].rearrange("p (b n) -> p b n", b=NB),
                             sph_dram[2:NB + 2, :, c, :].rearrange("b p n -> p b n")).then_inc(mlp_ld, 16)
            sp.dma_start(small[:, 0:mlp_w.shape[0]], mlp_w.partition_broadcast(P)).then_inc(mlp_ld, 16)
            sp.wait_ge(att_done, 1)
            with sp.Fori(0, NB) as i:
                for t in range(NT):
                    if t == NBUF - 1:
                        sp.wait_ge(agg_ready, i * NT + NBUF)
                        sp.dma_start(X0[:, :], x3_dram[i, :, :]).then_inc(x3_ld, 16)
                    sp.wait_ge(agg_ready, i * NT + t + 1)
                    sp.dma_start(rbuf[t % NBUF].rearrange("p k r -> p (k r)"),
                                 rows_dram[t][i, :, :]).then_inc(rows_ld[t % NBUF], 16)
            sp.wait_ge(out_st, 16 * (NB + 1))

        @BLK.gpsimd
        def _(pool):
            nc.gpsimd.memset(crd[:, :, :, :], 0.0).then_inc(crd_done, 1)
            for n in range(2):
                pool.sem_inc(rows_st[n], 16)
            pool.wait_ge(prep_done, 1)
            nc.gpsimd.memset(gbuf[1][:, :, C:ROW], 0.0).then_inc(crd_done, 1)
            pool.wait_ge(crd_done, 2)
            pool.sem_inc(crd_done, NT)
            with pool.Fori(0, NB // 2) as pair:
                for odd in range(2):
                    i = pair * 2 + odd
                    pool.wait_ge(table_st, i * 16 + 32)
                    pool.wait_ge(idxp_done, i + 1)
                    for t in range(NT):
                        n = t % 2
                        pool.wait_ge(rows_st[n], i * (16 * NT // 2) + 16 * (t // 2) + 16)
                        pool.wait_ge(crd_done, i * NT + t + NT + 2)
                        settle(pool)
                        for k in range(KNN):
                            nc.gpsimd.indirect_dma_start(
                                gbuf[n][:, k, :], None, table[odd],
                                bass.IndirectOffsetOnAxis(ap=idxp[:, odd, t, k:k + 1], axis=0)).then_inc(rows_in[n], 16)
                            if k == COPY_AFTER:
                                if t == 0:
                                    pool.wait_ge(rows_st[1], i * (16 * NT // 2) + 16)
                                else:
                                    pool.wait_ge(rows_in[1 - n], i * (NT // 2 * KNN * 16) + (t + 1) // 2 * KNN * 16)
                                if t == 1:
                                    pool.wait_ge(rel_done, i + 2)
                                settle(pool)
                                nc.gpsimd.tensor_copy(crd[:, (t - 1) % NT, :, :],
                                                      gbuf[1 - n][:, :, C:ROW]).then_inc(crd_done, 1)
            pool.wait_ge(rows_in[1], NB * NT // 2 * KNN * 16)
            settle(pool)
            nc.gpsimd.tensor_copy(crd[:, NT - 1, :, :], gbuf[1][:, :, C:ROW]).then_inc(crd_done, 1)

        @BLK.tensor
        def _(pe):
            mm = nc.tensor.matmul
            pe.wait_ge(w_ld, N_WLD)
            for n, (W, kc, w) in enumerate(WCHUNKS):
                if n >= 2:
                    pe.wait_ge(lora_done, n - 1)
                for c in range(0, w, 512):
                    last = mm(SC[n % 2][:, c:min(c + 512, w)], A_OF[id(W)][:, kc * P:(kc + 1) * P],
                              B_OF[id(W)][:, c:min(c + 512, w)], start=True, stop=True)
                last.then_inc(lora_ps, 1)
            for n in range(2):
                last = mm(MISC[:, n:n + 1], WL[n][:, 384:512], bL[:, n, 2:3], start=True, stop=True)
            last.then_inc(bo_ps, 1)
            pe.wait_ge(prep_done, 1)

            def norms(b, part):
                pe.wait_ge(sq_done, b + 1)
                if part < 2:
                    if part:
                        pe.wait_ge(xx_evac, b * 3 + 1)
                    last = mm(PD[0:1, :], neghalf, X0[:, part * 512:(part + 1) * 512], start=True, stop=True)
                else:
                    pe.wait_ge(xx_evac, b * 3 + 2)
                    for t in range(NT):
                        last = mm(PD[:, t:t + 1], X0[:, t * P:(t + 1) * P], negone, start=True, stop=True)
                last.then_inc(xx_ready, 1)

            def distance(b, t, h):
                if t or h:
                    pe.wait_ge(pd_evac, b * 16 + 2 * t + h)
                else:
                    pe.wait_ge(xx_evac, b * 3 + 3)
                mm(PD[:, :], ctx[:, t * P:(t + 1) * P], ctx[:, h * 512:(h + 1) * 512], start=True, stop=False)
                mm(PD[:, :], ones_row, xxrow[0:1, h * 512:(h + 1) * 512], start=False, stop=True).then_inc(pd_ready, 1)

            for part in range(3):
                norms(0, part)
            for h in range(2):
                distance(0, 0, h)
            with pe.Fori(0, NB) as i:
                def groups(l, scores, values):
                    pe.wait_ge(q_evac, i * 3 + l + 1)
                    scores(0)
                    for g in range(4):
                        n = 4 * l + g
                        if g < 3:
                            scores(g + 1)
                        if n in DIST_AT:
                            distance(i, *DIST_AT[n])
                        if n in NORMS_AT:
                            norms(i + 1, NORMS_AT[n])
                        pe.wait_ge(probs_done, i * 12 + n + 1)
                        if n == 0:
                            pe.wait_ge(ctxT_evac, i + 1)
                        for b in range(2):
                            for j in range(4):
                                last = nc.tensor.transpose(TP[:, b * 512 + j * P:b * 512 + (j + 1) * P],
                                                           S[g % 2][:, b * 512 + j * P:b * 512 + (j + 1) * P], ident)
                        last.then_inc(probsT_ready, 1)
                        pe.wait_ge(et_evac, i * 12 + n + 1)
                        if n:
                            pe.wait_ge(ot_evac, i * 12 + n)
                        values(g)
                    pe.wait_ge(ot_evac, i * 12 + 4 * l + 4)

                def score_bank(l, g):
                    n = 4 * l + g
                    if g == 1 and l == 1:
                        pe.wait_ge(k_evac, i * 3 + l + 1)
                    if g >= 2:
                        pe.wait_ge(front_done, i * 12 + n - 1)
                    pe.wait_ge(kexp_done, i * 12 + n + 1)

                def chunk_attention(l):
                    w = WL[l // 2]
                    for h in range(2):
                        last = mm(SC[1][:, h * 512:(h + 1) * 512], w[:, 128:256], ctx[:, h * 512:(h + 1) * 512],
                                  start=True, stop=True)
                    last.then_inc(k_ready, 1)
                    distance(i, *((6, 1) if l else (1, 0)))
                    pe.wait_ge(k_evac, i * 3 + l + 1)
                    for half in range(2):
                        if half:
                            if l:
                                pe.wait_ge(oproj_used, i * 3 + l)
                            for h in range(2):
                                last = mm(SC[0][:, h * 512:(h + 1) * 512], w[:, 0:128],
                                          ctx[:, h * 512:(h + 1) * 512], start=True, stop=True)
                            last.then_inc(q_ready, 1)
                            pe.wait_ge(v2_evac, i * 4 + l + 1)
                        for c in range(8):
                            n = half * 8 + c
                            for h in range(2):
                                last = mm(TP[64 * h:64 * h + 64, c * P:(c + 1) * P],
                                          ctx[:, n * CHUNK:(n + 1) * CHUNK], w[:, 256:384], start=True, stop=True)
                        last.then_inc(v_ready, 1)
                    distance(i, *((7, 0) if l else (1, 1)))
                    pe.wait_ge(v2_evac, i * 4 + l + 2)
                    if l == 0:
                        for t in range(NT):
                            last = nc.tensor.transpose(TP[:, t * P:(t + 1) * P], ctx[:, t * P:(t + 1) * P], ident)
                        last.then_inc(ctxT_ready, 1)

                    def scores(g):
                        score_bank(l, g)
                        for j in range(4):
                            c = 4 * g + j
                            last = mm(SC[g % 2][64 * (j % 2):64 * (j % 2) + 64, (j // 2) * 512:(j // 2 + 1) * 512],
                                      q_sb[:, c * CHUNK:(c + 1) * CHUNK],
                                      kexp.rearrange("p (h t) -> p h t", h=H0)[:, :, j * CHUNK:(j + 1) * CHUNK],
                                      start=True, stop=True)
                        last.then_inc(scores_ready, 1)

                    def values(g):
                        for b in range(2):
                            for half in range(2):
                                for j in range(4):
                                    last = mm(MISC[32 * j:32 * j + 32, (2 * b + half) * 64:(2 * b + half + 1) * 64],
                                              V2[:, 4 * g + 2 * b + half, 32 * j:32 * j + 32],
                                              ET[:, b * 512 + j * P + 64 * half:b * 512 + j * P + 64 * half + 64],
                                              start=True, stop=True)
                        last.then_inc(av_ready, 1)

                    groups(l, scores, values)
                    for h in range(2):
                        last = mm(SC[0][:, h * 512:(h + 1) * 512], w[:, 384:512], OT[:, h * 512:(h + 1) * 512],
                                  start=True, stop=True)
                    last.then_inc(oproj_ready, 1)

                chunk_attention(0)

                distance(i, 3, 0)
                for c in range(2):
                    for kc in range(KC):
                        last = mm(SC[1][:, c * P:(c + 1) * P], Wk[:, kc, c * P:(c + 1) * P], ctxT[:, kc, :],
                                  start=(kc == 0), stop=(kc == KC - 1))
                last.then_inc(k_ready, 1)
                for kc in range(KC):
                    last = mm(MISC[:, 0:256], ctxT[:, kc, :], Wv[:, kc, :], start=(kc == 0), stop=(kc == KC - 1))
                last.then_inc(v1_ready, 1)
                distance(i, 3, 1)
                pe.wait_ge(xl_done, i * 3 + 1)
                for kc in range(KC):
                    last = nc.tensor.transpose(TP[:, kc * P:(kc + 1) * P], X1[:, kc * P:(kc + 1) * P], ident)
                last.then_inc(hT_ready, 1)
                pe.wait_ge(hT_evac, i + 1)
                for c in range(KC):
                    for kc in range(KC):
                        last = mm(SC[0][:, c * P:(c + 1) * P], Wq[:, kc, c * P:(c + 1) * P], hT[:, kc, :],
                                  start=(kc == 0), stop=(kc == KC - 1))
                last.then_inc(q_ready, 1)
                distance(i, 4, 0)
                pe.wait_ge(v1_evac, i + 1)

                def scores1(g):
                    score_bank(1, g)
                    for b in range(2):
                        c = 2 * g + b
                        last = mm(SC[g % 2][:, b * 512:(b + 1) * 512], q_sb[:, c * P:(c + 1) * P],
                                  kexp[:, (c // 4) * 512:(c // 4 + 1) * 512], start=True, stop=True)
                    last.then_inc(scores_ready, 1)

                def values1(g):
                    for b in range(2):
                        c = 2 * g + b
                        for j in range(4):
                            h = c // 4 * 4 + j
                            last = mm(MISC[32 * j:32 * j + 32, b * P:(b + 1) * P], V1[:, h * HD:(h + 1) * HD],
                                      ET[:, b * 512 + j * P:b * 512 + (j + 1) * P], start=True, stop=True)
                    last.then_inc(av_ready, 1)

                groups(1, scores1, values1)
                for h in range(2):
                    for c in range(KC):
                        last = mm(SC[0][:, h * 512:(h + 1) * 512], OT[:, c * P:(c + 1) * P],
                                  Wo[:, c, h * 512:(h + 1) * 512], start=(c == 0), stop=(c == KC - 1))
                last.then_inc(oproj_ready, 1)

                chunk_attention(2)
                for h in range(2):
                    distance(i + 1, 0, h)
                pe.wait_ge(xl_done, i * 3 + 3)
                for t in range(NT):
                    last = nc.tensor.transpose(TP[:, t * P:(t + 1) * P], X0[:, t * P:(t + 1) * P], ident)
                last.then_inc(x3T_ready, 1)

            pe.wait_ge(pd_evac, NB * 16 + 2)
            for n in range(6):
                pe.wait_ge(stat_in, n + 1)
                w = 6 if n < 2 else 3 if n < 4 else 1
                mm(PD[:, 0:w], mean_w, stat[:, 0:w], start=True, stop=True).then_inc(stat_ps, 1)
            pe.sem_inc(agg_ready, NBUF)
            with pe.Fori(0, NB) as i:
                for t in range(NT):
                    pe.wait_ge(weighted, i * NT + t + 1)
                    pe.wait_ge(agg_used, i * NT + t + 1)
                    for k in range(KNN - FOLD):
                        mm(SC[t % 2][:, 0:P], rbuf[t % NBUF][:, k, 0:C], ident, start=(k == 0), stop=False)
                    if t == 0:
                        pe.wait_ge(x3_ld, i * 16 + 16)
                    mm(SC[t % 2][:, 0:P], ident, X0[:, t * P:(t + 1) * P], start=False, stop=True)\
                        .then_inc(agg_ready, 1)

        @BLK.scalar
        def _(act):
            A = nc.scalar.activation
            act.sem_inc(x3_st, 16)
            act.sem_inc(table_st, 16)
            act.wait_ge(w_ld, N_WLD)
            for n in range(2):
                A(bqs[:, n:n + 1], bL[:, n, 0:1], ACT.Copy, scale=0.25)
            act.dma_start(ctx[:, :], ctx_in[0, :, :]).then_inc(ctx_ld, 16)

            def norms(b, part):
                act.wait_ge(xx_ready, b * 3 + part + 1)
                if part < 2:
                    A(xxrow[0:1, part * 512:(part + 1) * 512], PD[0:1, :], ACT.Copy).then_inc(xx_evac, 1)
                else:
                    A(xxcol[:, :], PD[:, 0:NT], ACT.Copy).then_inc(xx_evac, 1)
                    act.wait_ge(xx_evac, b * 3 + 3)

            def distance(b, t, h):
                act.wait_ge(pd_ready, b * 16 + 2 * t + h + 1)
                if t >= 2 and h == 0:
                    act.wait_ge(topk_done, b * NT + t - 1)
                A(pd[t % 2][:, h * 512:(h + 1) * 512], PD[:, :], ACT.Identity,
                  bias=xxcol[:, t:t + 1], scale=2.0).then_inc(pd_evac, 1)

            act.wait_ge(ctx_ld, 16)
            A(X0[:, :], ctx[:, :], ACT.Square).then_inc(sq_done, 1)
            for part in range(3):
                norms(0, part)
            for h in range(2):
                distance(0, 0, h)
            with act.Fori(0, NB // 2) as pair:
                for odd in range(2):
                    i = pair * 2 + odd

                    def groups(l, expand, scale):
                        for g in range(4):
                            n = 4 * l + g
                            if g < 3:
                                if l != 1:
                                    act.wait_ge(scores_ready, i * 12 + n + 1)
                                expand(g + 1)
                            act.wait_ge(front_done, i * 12 + n + 1)
                            A(S[g % 2][:, :], S[g % 2][:, :], ACT.Exp, scale=scale).then_inc(exp_done, 1)
                            if n in DIST_AT:
                                distance(i, *DIST_AT[n])
                            if n == 8:
                                act.dma_start(ctx[:, :], ctx_in[(i + 1) % NB, :, :]).then_inc(ctx_ld, 16)
                            if n == 9:
                                act.wait_ge(ctx_ld, i * 16 + 32)
                                act.wait_ge(pd_evac, i * 16 + 16)
                                A(X0[:, :], ctx[:, :], ACT.Square).then_inc(sq_done, 1)
                            if n in NORMS_AT:
                                norms(i + 1, NORMS_AT[n])
                            act.wait_ge(probsT_ready, i * 12 + n + 1)
                            A(ET[:, :], TP[:, :], ACT.Copy).then_inc(et_evac, 1)
                            act.wait_ge(av_ready, i * 12 + n + 1)
                            A(OT[:, g * 256:(g + 1) * 256], MISC[:, 0:256], ACT.Copy).then_inc(ot_evac, 1)

                    def chunk_attention(l):
                        b = l // 2
                        act.wait_ge(k_ready, i * 3 + l + 1)
                        A(kT, SC[1][:, :], ACT.Identity, bias=bL[:, b, 1:2]).then_inc(k_evac, 1)
                        distance(i, *((6, 1) if l else (1, 0)))
                        act.wait_ge(k_evac, i * 3 + l + 1)

                        def expand(g):
                            for h in range(H0):
                                last = A(kexp[:, h * 256:(h + 1) * 256], kT[:, g * 256:(g + 1) * 256], ACT.Copy,
                                         scale=headmask[:, h:h + 1])
                            last.then_inc(kexp_done, 1)

                        expand(0)
                        for half in range(2):
                            act.wait_ge(v_ready, i * 4 + l + half + 1)
                            for e in range(2):
                                last = A(V2flat[:, half * 32:half * 32 + 32, e, :],
                                         TP[:, :].rearrange("p (c e d) -> p c e d", e=2, d=D0)[:, :, e, :],
                                         ACT.Copy, scale=parity[:, e * D0:e * D0 + 1])
                            last.then_inc(v2_evac, 1)
                            if half == 0:
                                act.wait_ge(q_ready, i * 3 + l + 1)
                                A(q_sb, SC[0][:, :], ACT.Identity, bias=bqs[:, b:b + 1], scale=0.25).then_inc(q_evac, 1)
                        distance(i, *((7, 0) if l else (1, 1)))
                        if l == 0:
                            act.wait_ge(x3_st, i * 16 + 16)
                            act.dma_start(X0[:, :], x_in[i, :, :]).then_inc(x_ld, 16)
                            act.wait_ge(ctxT_ready, i + 1)
                            act.wait_ge(own_saved, i + 1)
                            A(ctxT[:, :, :].rearrange("p t c -> p (t c)"), TP[:, :], ACT.Copy).then_inc(ctxT_evac, 1)
                            spherical_act(act, i)
                        groups(l, expand, 1.0)
                        if l == 0:
                            distance(i, 3, 0)
                        else:
                            distance(i + 1, 0, 0)
                        act.wait_ge(var_done, i * 2 + b + 1)
                        A(std[:, :], mv[:, 1:2], ACT.Sqrt, bias=eps).then_inc(std_done, 1)

                    mrow = mask_in[i, :, :]
                    halves = mrow.rearrange("a (c h k) -> a c h k", h=2, k=CHUNK)
                    for h in range(2):
                        act.dma_start(mb[64 * h:64 * h + 64, :].rearrange("p (c k) -> p c k", k=CHUNK),
                                      halves[0, :, h, :].partition_broadcast(64)).then_inc(mask_ld, 16)
                    act.dma_start(maskT[:, :], mrow[0, :].partition_broadcast(P)).then_inc(mask_ld, 16)
                    chunk_attention(0)

                    act.wait_ge(k_ready, i * 3 + 2)
                    halves = kexp.rearrange("p (c j t) -> p c j t", c=4, j=4)[:, 0:2, :, :]
                    for j in range(4):
                        last = A(halves[:, :, j, :], SC[1][:, 0:256].rearrange("p (c t) -> p c t", c=2), ACT.Copy,
                                 scale=quadmask[:, j:j + 1])
                    last.then_inc(k_evac, 1)
                    act.wait_ge(v1_ready, i + 1)
                    A(V1, MISC[:, 0:256], ACT.Copy).then_inc(v1_evac, 1)
                    distance(i, 3, 1)
                    act.wait_ge(hT_ready, i + 1)
                    A(hT.rearrange("p k n -> p (k n)"), TP[:, :], ACT.Copy).then_inc(hT_evac, 1)
                    act.wait_ge(q_ready, i * 3 + 2)
                    A(q_sb, SC[0][:, :], ACT.Copy).then_inc(q_evac, 1)
                    distance(i, 4, 0)
                    act.wait_ge(k_evac, i * 3 + 2)

                    def expand1(g):
                        act.sem_inc(kexp_done, 1)

                    expand1(0)
                    groups(1, expand1, float(HD) ** -0.5)

                    chunk_attention(2)

                    distance(i + 1, 0, 1)

                    act.wait_ge(xl_done, i * 3 + 3)
                    act.dma_start(x3_dram[i, :, :], X0[:, :]).then_inc(x3_st, 16)
                    act.wait_ge(table_st, i * 16 + 16)
                    act.wait_ge(x3T_ready, i + 1)
                    A(tab[:, :, 0:C], TP[:, :].rearrange("p (t c) -> p t c", t=NT), ACT.Copy).then_inc(tab_done, 1)
                    A(tab[:, :, C:ROW], ctxT[:, :, 0:4], ACT.Copy).then_inc(tab_done, 1)
                    act.wait_ge(tab_done, i * 2 + 2)
                    act.dma_start(table[odd].rearrange("(t p) r -> p t r", p=P), tab).then_inc(table_st, 16)
            spherical_act(act, NB)
            spherical_act(act, NB + 1)

            act.wait_ge(mlp_ld, 64)
            n = 0
            act.wait_ge(coef_done, 1)
            for p in range(2):
                if p:
                    act.wait_ge(stat_ps, 2)
                    A(tstd[:, 0:6], PD[:, 0:6], ACT.Sqrt, bias=eps).then_inc(tstd_done, 1)
                    act.wait_ge(coef_done, 2)
                for c in range(NCH):
                    for j in range(6):
                        if n >= 6:
                            act.wait_ge(h_used, n - 5)
                        w = weff if p == 0 else wnorm
                        A(hid[j], chan[0][:, c * CW:(c + 1) * CW], ACT.Identity, scale=w[:, 3 * j:3 * j + 1],
                          bias=(zero if p == 0 else shift[:, j:j + 1])).then_inc(lin_done, 1)
                        n += 1
            act.wait_ge(stat_ps, 4)
            A(tstd[:, 0:3], PD[:, 0:3], ACT.Sqrt, bias=eps).then_inc(tstd_done, 1)
            act.wait_ge(coef_done, 3)
            for c in range(NCH):
                for m in range(3):
                    act.wait_ge(h_used, n - (5 if c == 0 else 2))
                    A(hid[m], chan[m][:, c * CW:(c + 1) * CW], ACT.Identity, scale=gain[:, m:m + 1],
                      bias=shift[:, m:m + 1]).then_inc(lin_done, 1)
                    n += 1
            act.wait_ge(stat_ps, 6)
            A(tstd[:, 0:1], PD[:, 0:1], ACT.Sqrt, bias=eps).then_inc(tstd_done, 1)
            act.wait_ge(coef_done, 4)
            A(chan[1], chan[0], ACT.Identity, scale=gain[:, 0:1], bias=shift[:, 0:1]).then_inc(lin_done, 1)
            act.wait_ge(att_in, 1)
            A(chan[0], chan[0], ACT.Exp).then_inc(att_exp, 1)
            act.sem_inc(agg_used, 2)
            act.sem_inc(out_st, 16)
            with act.Fori(0, NB) as i:
                act.wait_ge(out_st, i * 16 + 16)
                for t in range(NT):
                    act.wait_ge(agg_ready, i * NT + t + 1 + NBUF)
                    A(X1[:, t * P:(t + 1) * P], SC[t % 2][:, 0:P], ACT.Copy).then_inc(agg_used, 1)
                act.wait_ge(agg_used, i * NT + NT + 2)
                act.dma_start(out[i, :, :], X1[:, :]).then_inc(out_st, 16)

        @BLK.vector
        def _(dve):
            V = nc.vector
            dve.sem_inc(sph_done, 1)
            V.memset(ctxT[:, :, 0:4], 0.0)
            V.memset(own[:, :, :], 0.0)
            dve.wait_ge(w_ld, N_WLD)
            for n, (W, kc, w) in enumerate(WCHUNKS):
                dve.wait_ge(lora_ps, n + 1)
                V.scalar_tensor_tensor(W[:, kc, :], SC[n % 2][:, 0:w], LORA, W[:, kc, :],
                                       ALU.mult, ALU.add).then_inc(lora_done, 1)
            dve.wait_ge(lora_done, len(WCHUNKS))
            dve.wait_ge(bo_ps, 1)
            V.tensor_tensor(bof[:, :], MISC[:, 0:2], bL[:, :, 3], ALU.add).then_inc(prep_done, 1)
            dve.wait_ge(prep_done, 1)

            def relative(i):
                dve.wait_ge(crd_done, i * NT + 3)
                for c in range(3):
                    last = V.tensor_tensor(rel[:, c, :].rearrange("p (t k) -> p t k", t=NT), crd[:, :, :, c],
                                           own[:, :, c].unsqueeze(2).broadcast_to([P, NT, KNN]), ALU.subtract)
                last.then_inc(rel_done, 1)
                dve.wait_ge(rel_done, i + 1)
                V.tensor_copy(own[:, :, :], ctxT[:, :, 0:4]).then_inc(own_saved, 1)
                dve.wait_ge(own_saved, i + 1)

            def spherical(i, step):
                r_xy, den, t2, t3, corr = tmp
                step(V.tensor_tensor(t2[:, :, :], rel[:, 0:2, :], rel[:, 0:2, :], ALU.mult))
                V.tensor_tensor(t3[:, 0, :], rel[:, 2, :], rel[:, 2, :], ALU.mult)
                step(V.tensor_tensor(den[:, 0, :], t2[:, 0, :], t2[:, 1, :], ALU.add))
                step(V.tensor_tensor(den[:, 1, :], den[:, 0, :], t3[:, 0, :], ALU.add))
                V.tensor_scalar(t3[:, :, :], den[:, :, :], TINY, None, ALU.is_ge)
                V.tensor_scalar(r_xy[:, :, :], den[:, :, :], TINY, None, ALU.max).then_inc(sq_in, 1)
                dve.wait_ge(sqrt_done, i + 1)
                dve.wait_ge(sph_st, i * 16 + 16)
                V.tensor_copy(sph[:, 0, :], r_xy[:, 1, :])
                V.scalar_tensor_tensor(den[:, 0, :], rel[:, 0, :], -1.0, rel[:, 0, :], ALU.mult, ALU.max)
                V.tensor_copy(den[:, 1, :], r_xy[:, 0, :])
                step(V.scalar_tensor_tensor(t2[:, :, :], rel[:, 1:3, :], -1.0, rel[:, 1:3, :], ALU.mult, ALU.max))
                num = t2
                step(V.tensor_tensor(r_xy[:, :, :], num[:, :, :], den[:, :, :], ALU.max))
                step(V.tensor_scalar(r_xy[:, :, :], r_xy[:, :, :], 1e-30, None, ALU.max))
                step(V.reciprocal(r_xy[:, :, :], r_xy[:, :, :]))
                big = X1[:, 2 * PAIRS:4 * PAIRS].rearrange("p (a n) -> p a n", a=2)
                V.tensor_tensor(big, num[:, :, :], den[:, :, :], ALU.is_gt)
                step(V.tensor_tensor(num[:, :, :], num[:, :, :], den[:, :, :], ALU.min))
                V.tensor_tensor(num[:, :, :], num[:, :, :], r_xy[:, :, :], ALU.mult).then_inc(atan_in, 1)
                dve.wait_ge(atan_in, i + 1)
                V.tensor_scalar(r_xy[:, :, :], rel[:, 1:3, :], 0.0, -2.0, ALU.is_lt, ALU.mult)
                step(V.tensor_scalar(den[:, 0, :], rel[:, 0, :], 0.0, None, ALU.is_lt))
                step(V.tensor_scalar(r_xy[:, :, :], r_xy[:, :, :], 1.0, None, ALU.add))
                dve.wait_ge(atan_done, i + 1)
                a = num
                step(V.tensor_scalar(corr, a[:, :, :], -2.0, float(np.pi / 2), ALU.mult, ALU.add))
                step(V.tensor_tensor(corr, corr, big, ALU.mult))
                step(V.tensor_tensor(a[:, :, :], a[:, :, :], corr, ALU.add))
                step(V.tensor_scalar(corr[:, 0, :], a[:, 0, :], -2.0, float(np.pi), ALU.mult, ALU.add))
                step(V.tensor_tensor(corr[:, 0, :], corr[:, 0, :], den[:, 0, :], ALU.mult))
                step(V.tensor_tensor(a[:, 0, :], a[:, 0, :], corr[:, 0, :], ALU.add))
                step(V.tensor_tensor(a[:, :, :], a[:, :, :], r_xy[:, :, :], ALU.mult))
                V.tensor_tensor(sph[:, 1, :], a[:, 1, :], t3[:, 1, :], ALU.mult)
                step(V.tensor_tensor(sph[:, 2, :], a[:, 0, :], t3[:, 0, :], ALU.mult))
                dve.sem_inc(sph_done, 1)

            dve.sem_inc(sph_st, 16)
            with dve.Fori(0, NB) as i:
                chain = [0]

                def step(ins):
                    chain[0] += 1
                    ins.then_inc(dve_step, 1)
                    dve.wait_ge(dve_step, i * DVE_STEPS + chain[0])

                rounds = [0]

                def search_round():
                    t, r = divmod(rounds[0], ROUNDS)
                    rounds[0] += 1
                    buf = pd[t % 2]
                    if r == 0:
                        dve.wait_ge(pd_evac, i * 16 + 2 * t + 2)
                    m = m8[:, 8 * r:8 * r + 8]
                    settle(dve)
                    step(V.max(m, buf[:, :]))
                    settle(dve)
                    last = V.max_index(idx[:, t, 8 * r:8 * r + 8], m, buf[:, :])
                    if r < ROUNDS - 1:
                        step(V.match_replace(buf[:, :], m, buf[:, :], -3.0e38))
                    else:
                        last.then_inc(topk_done, 1)

                def groups(l, front, keys):
                    for g in range(4):
                        n = 4 * l + g
                        s = S[g % 2]
                        dve.wait_ge(scores_ready, i * 12 + n + 1)
                        if n >= 2:
                            dve.wait_ge(probsT_ready, i * 12 + n - 1)
                        front(g, s)
                        dve.wait_ge(front_done, i * 12 + n + 1)
                        for _ in range(ROUNDS_AT[n]):
                            search_round()
                        dve.wait_ge(exp_done, i * 12 + n + 1)
                        rows = T // keys
                        e = s[:, :].rearrange("p (r k) -> p r k", k=keys)
                        step(V.reduce_sum(sm[:, 0:rows], e, AX.X))
                        step(V.reciprocal(sm[:, 0:rows], sm[:, 0:rows]))
                        V.tensor_tensor(e, e, sm[:, 0:rows].unsqueeze(2).broadcast_to([P, rows, keys]), ALU.mult)\
                            .then_inc(probs_done, 1)

                def chunk_attention(l, x_res, y):
                    b = l // 2
                    def front(g, s):
                        rows = s[:, :].rearrange("p (b h k) -> p b h k", b=2, h=H0)
                        bias = mb[:, g * 128:(g + 1) * 128].rearrange("p (b k) -> p b k", b=2)
                        for b_ in range(2):
                            last = V.tensor_tensor(rows[:, b_, :, :],
                                                   SC[g % 2][:, b_ * 512:(b_ + 1) * 512].rearrange("p (h k) -> p h k", h=H0),
                                                   bias[:, b_, :].unsqueeze(1).broadcast_to([P, H0, CHUNK]), ALU.add)
                        step(last)
                        e = s[:, :].rearrange("p (r k) -> p r k", k=CHUNK)
                        step(V.reduce_max(mx[:, :], e, AX.X))
                        V.tensor_tensor(e, e, mx[:, :].unsqueeze(2).broadcast_to([P, 16, CHUNK]), ALU.subtract)\
                            .then_inc(front_done, 1)

                    groups(l, front, CHUNK)
                    for _ in range(2):
                        search_round()
                    if l:
                        dve.wait_ge(topk_done, i * NT + NT)
                        V.tensor_copy(idxp[:, i % 2, :, :], idx[:, :, 0:KNN]).then_inc(idxp_done, 1)
                    dve.wait_ge(oproj_ready, i * 3 + l + 1)
                    V.scalar_tensor_tensor(y[:, :], SC[0][:, :], bof[:, b:b + 1], maskT[:, :], ALU.add, ALU.mult)\
                        .then_inc(oproj_used, 1)
                    dve.wait_ge(oproj_used, i * 3 + l + 1)
                    if l == 0:
                        dve.wait_ge(x_ld, i * 16 + 16)
                    step(V.tensor_tensor(y[:, :], y[:, :], x_res[:, :], ALU.add))
                    for h in range(2):
                        last = V.bn_stats(bst[:, h, :], y[:, h * 512:(h + 1) * 512])
                    step(last)
                    settle(dve)
                    V.bn_aggr(mv[:, :], bst[:, :, :].rearrange("p a b -> p (a b)")).then_inc(var_done, 1)
                    dve.wait_ge(std_done, i * 2 + b + 1)
                    step(V.reciprocal(rstd[:, :], std[:, :]))
                    V.tensor_scalar(y[:, :], y[:, :], mv[:, 0:1], rstd[:, 0:1], ALU.subtract, ALU.mult)\
                        .then_inc(xl_done, 1)

                for _ in range(3):
                    search_round()
                relative(i)
                spherical(i, step)
                dve.wait_ge(mask_ld, i * 48 + 48)
                step(V.tensor_scalar(mb[:, :], mb[:, :], 0.0, NEG, ALU.is_le, ALU.mult))
                chunk_attention(0, X0, X1)
                for _ in range(7):
                    search_round()

                def front1(g, s):
                    sc = SC[g % 2][:, :].rearrange("p (r k) -> p r k", k=P)
                    step(V.reduce_max(mx[:, 0:8], sc, AX.X))
                    V.tensor_tensor(s[:, :].rearrange("p (r k) -> p r k", k=P), sc,
                                    mx[:, 0:8].unsqueeze(2).broadcast_to([P, 8, P]), ALU.subtract)\
                        .then_inc(front_done, 1)

                groups(1, front1, P)
                for _ in range(4):
                    search_round()
                dve.wait_ge(oproj_ready, i * 3 + 2)
                V.tensor_tensor(X1[:, :], SC[0][:, :], X1[:, :], ALU.add).then_inc(xl_done, 1)
                dve.wait_ge(xl_done, i * 3 + 2)
                dve.sem_inc(oproj_used, 1)
                for _ in range(4):
                    search_round()
                chunk_attention(2, X1, X0)
                assert rounds[0] == NT * ROUNDS
                assert chain[0] == DVE_STEPS, chain[0]
            tail = [0]

            def step_tail(ins):
                tail[0] += 1
                ins.then_inc(dve_step, 1)
                dve.wait_ge(dve_step, NB * DVE_STEPS + tail[0])

            relative(NB)
            spherical(NB, step_tail)
            relative(NB + 1)
            spherical(NB + 1, step_tail)
            step = step_tail
            dve.wait_ge(mlp_ld, 64)
            step(V.reduce_sum(wsum, w1[:, :, 3:6], AX.X))
            step(V.tensor_scalar(wsum, wsum, -1.0 / 3.0, None, ALU.mult))
            we = weff.rearrange("p (j f) -> p j f", j=6)
            step(V.tensor_tensor(we, w1[:, :, 0:3], w1[:, :, 3:6], ALU.add))
            V.memset(zero, 0.0)
            step(V.tensor_tensor(we, we, wsum.unsqueeze(2).broadcast_to([P, 6, 3]), ALU.add))
            dve.sem_inc(coef_done, 1)

            norms = [0]

            def batch_norm(width, g, b):
                settle(dve)
                for j in range(width):
                    last = V.bn_aggr(hmv[:, j, :], hstat[:, j, :])
                step(last)
                step(V.tensor_copy(stat[:, 0:width], hmv[:, 0:width, 0]))
                dve.sem_inc(stat_in, 1)
                dve.wait_ge(stat_ps, 2 * norms[0] + 1)
                step(V.tensor_copy(mean[:, 0:width], PD[:, 0:width]))
                step(V.tensor_tensor(dev[:, 0:width], hmv[:, 0:width, 0], mean[:, 0:width], ALU.subtract))
                step(V.tensor_tensor(dev[:, 0:width], dev[:, 0:width], dev[:, 0:width], ALU.mult))
                step(V.tensor_tensor(stat[:, 0:width], dev[:, 0:width], hmv[:, 0:width, 1], ALU.add))
                dve.sem_inc(stat_in, 1)
                norms[0] += 1
                dve.wait_ge(tstd_done, norms[0])
                step(V.reciprocal(gain[:, 0:width], tstd[:, 0:width]))
                step(V.tensor_tensor(gain[:, 0:width], gain[:, 0:width], g, ALU.mult))
                step(V.tensor_tensor(dev[:, 0:width], gain[:, 0:width], mean[:, 0:width], ALU.mult))
                step(V.tensor_tensor(shift[:, 0:width], b, dev[:, 0:width], ALU.subtract))

            n = 0
            for p in range(2):
                w = weff if p == 0 else wnorm
                for c in range(NCH):
                    cols = slice(c * CW, (c + 1) * CW)
                    for j in range(6):
                        dve.wait_ge(lin_done, n + 1)
                        n += 1
                        for f in (1, 2):
                            step(V.scalar_tensor_tensor(hid[j], chan[f][:, cols], w[:, 3 * j + f:3 * j + f + 1], hid[j],
                                                        ALU.mult, ALU.add))
                        if p == 0:
                            for h in range(2):
                                last = V.bn_stats(hstat[:, j, (2 * c + h) * 6:(2 * c + h + 1) * 6],
                                                  hid[j][:, h * SUB:(h + 1) * SUB])
                            last.then_inc(h_used, 1)
                        else:
                            step(V.scalar_tensor_tensor(hid[j], hid[j], 0.2, hid[j], ALU.mult, ALU.max))
                    if p:
                        for m in range(3):
                            step(V.tensor_scalar(chan[m][:, cols], hid[0], w2[:, 6 * m:6 * m + 1], None, ALU.mult))
                            for j in range(1, 6):
                                last = V.scalar_tensor_tensor(chan[m][:, cols], hid[j], w2[:, 6 * m + j:6 * m + j + 1],
                                                              chan[m][:, cols], ALU.mult, ALU.add)
                                step(last)
                        dve.sem_inc(h_used, 6)
                        for m in range(3):
                            for h in range(2):
                                step(V.bn_stats(hstat[:, m, (2 * c + h) * 6:(2 * c + h + 1) * 6],
                                                chan[m][:, c * CW + h * SUB:c * CW + (h + 1) * SUB]))
                if p == 0:
                    dve.wait_ge(h_used, n)
                    batch_norm(6, g1, b1)
                    step(V.tensor_tensor(wnorm.rearrange("p (j f) -> p j f", j=6), we,
                                         gain.unsqueeze(2).broadcast_to([P, 6, 3]), ALU.mult))
                else:
                    batch_norm(3, g2, b2)
                dve.sem_inc(coef_done, 1)
            for c in range(NCH):
                cols = slice(c * CW, (c + 1) * CW)
                for m in range(3):
                    dve.wait_ge(lin_done, n + 1)
                    n += 1
                    step(V.scalar_tensor_tensor(hid[m], hid[m], 0.2, hid[m], ALU.mult, ALU.max))
                step(V.tensor_scalar(chan[0][:, cols], hid[0], w3[:, 0:1], None, ALU.mult))
                for m in (1, 2):
                    step(V.scalar_tensor_tensor(chan[0][:, cols], hid[m], w3[:, m:m + 1], chan[0][:, cols],
                                                ALU.mult, ALU.add))
                dve.sem_inc(h_used, 3)
                for h in range(2):
                    step(V.bn_stats(hstat[:, 0, (2 * c + h) * 6:(2 * c + h + 1) * 6],
                                    chan[0][:, c * CW + h * SUB:c * CW + (h + 1) * SUB]))
            batch_norm(1, g3, b3)
            dve.sem_inc(coef_done, 1)
            dve.wait_ge(lin_done, n + 1)
            step(V.scalar_tensor_tensor(chan[0], chan[1], 0.2, chan[1], ALU.mult, ALU.max))
            a = chan[0].rearrange("p (r k) -> p r k", k=KNN)
            over = [P, NB * NT, KNN]
            step(V.reduce_max(att_mx, a, AX.X))
            V.tensor_tensor(a, a, att_mx.unsqueeze(2).broadcast_to(over), ALU.subtract).then_inc(att_in, 1)
            dve.wait_ge(att_exp, 1)
            step(V.reduce_sum(att_mx, a, AX.X))
            step(V.reciprocal(att_mx, att_mx))
            V.tensor_tensor(a, a, att_mx.unsqueeze(2).broadcast_to(over), ALU.mult).then_inc(att_done, 1)
            dve.wait_ge(att_done, 1)
            with dve.Fori(0, NB) as i:
                for t in range(NT):
                    b = rbuf[t % NBUF]
                    dve.wait_ge(rows_ld[t % NBUF], i * (NT // NBUF * 16) + (t // NBUF + 1) * 16)
                    weights = arena[:, bass.ds(i * PAIRS + t * KNN, KNN)]
                    V.tensor_tensor(b[:, :, 0:C], b[:, :, 0:C], weights.unsqueeze(2).broadcast_to([P, KNN, C]),
                                    ALU.mult).then_inc(products, 1)
                    dve.wait_ge(products, i * NT + t + 1)
                    V.tensor_tensor(b[:, 0:FOLD, 0:C], b[:, 0:FOLD, 0:C], b[:, KNN - FOLD:KNN, 0:C],
                                    ALU.add).then_inc(weighted, 1)


def constants():
    p = np.arange(P)
    c = np.zeros((P, 528), np.float32)
    c[:, 0:128] = np.eye(P)
    c[:, 128:256] = (p[:, None] // 64) == (p[None, :] // D0) % 2
    c[:, 256:264] = (p[:, None] // D0) == np.arange(H0)[None, :]
    c[:, 264:268] = (p[:, None] // HD) == np.arange(4)[None, :]
    c[:, 268] = -0.5
    c[:, 269] = -1.0
    c[:, 270] = EPS
    c[:, 271:399] = 1.0
    c[:, 399:527] = 1.0 / P
    return c


def layout(d):
    g = lambda n: np.asarray(d[n])
    t = lambda a: np.ascontiguousarray(a)
    heads = np.arange(T).reshape(2, 4, NH // NKV, HD).transpose(0, 2, 1, 3).reshape(-1)
    bias = np.stack([np.concatenate([g(f"L{l}_xattn_b_in").reshape(3, C), g(f"L{l}_xattn_b_out").reshape(1, C)])
                     for l in (0, 2)])
    return {
        "x": t(g("x")), "ctx": t(g("ctx_4096")), "mask": t(g("mask_Bx1x4096_ff1")),
        "w_in": t(np.stack([g(f"L{l}_xattn_W_in").T for l in (0, 2)])),
        "b_qkv": t(bias.transpose(2, 0, 1)),
        "w_out": t(np.stack([g(f"L{l}_xattn_W_out").T for l in (0, 2)])),
        "wq": t(g("L1_xattn_Wq")[:, heads]), "wk": t(g("L1_xattn_Wk")), "wv": t(g("L1_xattn_Wv")), "wo": t(g("L1_xattn_Wo")[heads]),
        "at": t(np.stack([g(f"L1_xattn_A{n}").T for n in "qkv"] + [g("L1_xattn_Ao")[heads].T])),
        "bq": t(g("L1_xattn_Bq")[:, heads]), "bk": t(g("L1_xattn_Bk")), "bv": t(g("L1_xattn_Bv")), "bo": t(g("L1_xattn_Bo")),
        "mlp_w": t(np.concatenate([g(f"L3_xattn_{n}{l}").reshape(-1) for l in (1, 2, 3) for n in ("W", "g", "b")])),
        "consts": constants(),
    }


def kernel(**inputs):
    import concourse.bacc as bacc
    from concourse.bass_utils import run_bass_kernel_spmd

    nc = bacc.Bacc("TRN2", target_bir_lowering=False, num_devices=1)
    arrays = layout(inputs)
    aps = [nc.dram_tensor(f"in_{n}", a.shape, mybir.dt.from_np(a.dtype), kind="ExternalInput").ap()
           for n, a in arrays.items()]
    out = nc.dram_tensor("out", (B, C, T), mybir.dt.float32, kind="ExternalOutput").ap()
    program(nc, *aps, out)
    r = run_bass_kernel_spmd(nc, [{f"in_{n}": a for n, a in arrays.items()}], core_ids=[0])
    return r.results[0]["out"]
```

```python
import numpy as np
import concourse.bass as bass
from concourse import mybir
from contextlib import ExitStack

B, C, T = 32, 128, 1024
H0, CHUNK = 8, 64
D0 = C // H0
NH, NKV = 32, 8
HD = T // NH
R = 16
LORA = 32.0 / 16.0
KNN = 30
EPS = 1e-5
NEG = -1.0e9
TINY = 1e-20
P = 128
NT = T // P
KC = T // P
ROW = C + 4
ROUNDS = 4
PAIRS = NT * KNN
PIECES, PW = 5, PAIRS // 5
NBUF = 4
FOLD = 7
DVE_STEPS = 125


def program(nc, x_in, ctx_in, mask_in, w_in, b_qkv, w_out, wq, wk, wv, wo, at, bq, bk, bv, bo,
            mlp_k, consts, out, NB=B):
    f32, u32 = mybir.dt.float32, mybir.dt.uint32
    ALU, ACT, AX = mybir.AluOpType, mybir.ActivationFunctionType, mybir.AxisListType
    TOTAL = NB * PAIRS
    GB = min(8, NB)
    PARTS = NB // GB
    G = PIECES * GB
    GR = 3 * G
    PCOLS = P * PW
    COLS = PARTS * PCOLS
    CW = 512
    NCH = COLS // CW
    PCH = PCOLS // CW

    stack = ExitStack()
    with stack:
        def sb(name, shape, dt=f32):
            return stack.enter_context(nc.sbuf_tensor(name, shape, dt))

        def sem(name):
            return stack.enter_context(nc.semaphore(name))

        table = [nc.dram_tensor(f"gather_table{n}", [T, ROW], f32).ap() for n in range(2)]
        x3_dram = nc.dram_tensor("x3_scratch", [NB, P, T], f32).ap()
        sph_dram = nc.dram_tensor("sph_scratch", [PARTS, 3, PIECES, GB, P, PW], f32).ap()
        h3_dram = nc.dram_tensor("logit_scratch", [PARTS, PIECES, GB, P, PW], f32).ap()
        rows_dram = [nc.dram_tensor(f"neighbour_rows{t}", [NB, P, KNN * C], f32).ap() for t in range(NT)]

        arena = sb("arena", [P, 3 * B * PAIRS + 2 * T])
        o = 0
        Wq = arena[:, o:o + KC * T].rearrange("p (k n) -> p k n", k=KC); o += KC * T
        Wo = arena[:, o:o + KC * T].rearrange("p (k n) -> p k n", k=KC); o += KC * T
        Wk = arena[:, o:o + KC * 256].rearrange("p (k n) -> p k n", k=KC); o += KC * 256
        Wv = arena[:, o:o + KC * 256].rearrange("p (k n) -> p k n", k=KC); o += KC * 256
        tab = arena[:, o:o + NT * ROW].rearrange("p (t r) -> p t r", t=NT); o += NT * ROW
        xxrow = arena[:, o:o + T]; o += T
        o = 3 * B * PAIRS
        ctx = arena[:, o:o + T]
        X0 = arena[:, o + T:o + 2 * T]
        X1 = sb("X1", [P, T])
        reg = sb("reg", [P, 4 * T])
        q_sb, kT, V2 = reg[:, 0:T], reg[:, T:2 * T], reg[:, 2 * T:4 * T].rearrange("p (c n) -> p c n", c=16)
        V2flat = reg[:, 2 * T:4 * T].rearrange("p (c e d) -> p c e d", e=2, d=D0)
        hT = reg[:, 2 * T:3 * T].rearrange("p (k n) -> p k n", k=KC)
        V1 = reg[:, 3 * T:3 * T + 256]
        kexp = sb("kexp", [P, 2048])
        OT = sb("OT", [P, T])
        ctxT = sb("ctxT", [P, NT, P])
        S = [sb(f"S{n}", [P, T]) for n in range(2)]
        ET = sb("ET", [P, T])
        rel = OT[:, 0:3 * PAIRS].rearrange("p (a n) -> p a n", a=3)
        tmp = [w[:, 2 * PAIRS * n:2 * PAIRS * (n + 1)].rearrange("p (a n) -> p a n", a=2)
               for w, n in ((S[0], 0), (S[0], 1), (S[1], 0), (S[1], 1), (X1, 0))]
        pd = [sb(f"pd{n}", [P, T]) for n in range(2)]
        gbuf = [sb(f"gbuf{n}", [P, KNN, ROW]) for n in range(2)]
        mb = sb("mb", [P, 512])
        maskT = sb("maskT", [P, T])
        m8 = sb("m8", [P, 8 * ROUNDS])
        idx = sb("idx", [P, NT, 8 * ROUNDS], u32)
        idxp = sb("idxp", [P, 2, NT, KNN], u32)
        crd = sb("crd", [P, NT, KNN, 4])
        own = sb("own", [P, NT, 4])
        sph = sb("sph", [P, 3, PAIRS])
        WL = [sb(f"WL{n}", [P, 4 * P]) for n in range(2)]
        bL = sb("bL", [P, 2, 4])
        bqs = sb("bqs", [P, 2])
        bof = sb("bof", [P, 2])
        con = sb("con", [P, consts.shape[1]])
        ident = con[:, 0:128]
        parity = con[:, 128:256]
        headmask = con[:, 256:264]
        quadmask = con[:, 264:268]
        neghalf = con[:, 268:269]
        negone = con[:, 269:270]
        eps = con[:, 270:271]
        ones_row = con[0:1, 271:399]
        xxcol = sb("xxcol", [P, NT])
        mx = sb("mx", [P, 16])
        sm = sb("sm", [P, 16])
        bst = sb("bst", [P, 2, 6])
        mv = sb("mv", [P, 2])
        std = sb("std", [P, 1])
        rstd = sb("rstd", [P, 1])
        small = sb("small", [P, 20])
        att_mx = mb[:, 0:NB * NT]
        loraA = gbuf[0][0:R, :, :].rearrange("p a b -> p (a b)")[:, 0:3072]
        loraO = gbuf[1][0:R, :, :].rearrange("p a b -> p (a b)")[:, 0:1024]
        loraB = gbuf[1][0:R, :, :].rearrange("p a b -> p (a b)")[:, 1024:3584]

        def pb(name, n):
            return stack.enter_context(nc.psum_tensor(name, [P, 512 * n], f32))
        SC = [pb("SCA", 2), pb("SCB", 2)]
        TP = pb("TP", 2)
        PD = pb("PD", 1)
        MISC = pb("MISC", 1)

        w_ld, lora_ps, lora_done, bo_ps, prep_done = (sem(n) for n in (
            "w_ld", "lora_ps", "lora_done", "bo_ps", "prep_done"))
        lora_ld = sem("lora_ld")
        w1_ld = [sem(f"w1_ld{n}") for n in range(4)]
        ctx_ld, x_ld, mask_ld, x3_st, table_st, sph_st = (sem(n) for n in (
            "ctx_ld", "x_ld", "mask_ld", "x3_st", "table_st", "sph_st"))
        rows_in = [sem(f"rows_in{n}") for n in range(2)]
        arrived = sem("arrived")
        rows_st = [sem(f"rows_st{n}") for n in range(2)]
        ctxT_ready, xx_ready, pd_ready, q_ready, k_ready, v_ready, v1_ready, hT_ready = (sem(n) for n in (
            "ctxT_ready", "xx_ready", "pd_ready", "q_ready", "k_ready", "v_ready", "v1_ready", "hT_ready"))
        scores_ready, probsT_ready, av_ready, oproj_ready, x3T_ready = (sem(n) for n in (
            "scores_ready", "probsT_ready", "av_ready", "oproj_ready", "x3T_ready"))
        sq_done, xx_evac, ctxT_evac, pd_evac, q_evac, k_evac, v1_evac, hT_evac = (sem(n) for n in (
            "sq_done", "xx_evac", "ctxT_evac", "pd_evac", "q_evac", "k_evac", "v1_evac", "hT_evac"))
        kexp_done, exp_done, et_evac, ot_evac, std_done, tab_done, sqrt_done, atan_done = (sem(n) for n in (
            "kexp_done", "exp_done", "et_evac", "ot_evac", "std_done", "tab_done", "sqrt_done", "atan_done"))
        dve_step, v2_evac, front_done, probs_done, topk_done, oproj_used, xl_done, var_done = (sem(n) for n in (
            "dve_step", "v2_evac", "front_done", "probs_done", "topk_done", "oproj_used", "xl_done", "var_done"))
        idxp_done, own_saved, rel_done, sq_in, atan_in, sph_done, crd_done = (sem(n) for n in (
            "idxp_done", "own_saved", "rel_done", "sq_in", "atan_in", "sph_done", "crd_done"))
        rows_ld = [sem(f"rows_ld{n}") for n in range(NBUF)]
        mlp_ld, stat_in, stat_ps, tstd_done, coef_done, h3_st, att_ld, att_lin, att_in, att_exp = (sem(n) for n in (
            "mlp_ld", "stat_in", "stat_ps", "tstd_done", "coef_done", "h3_st", "att_ld", "att_lin", "att_in", "att_exp"))
        l1_ready, l1_seen, h1_lin, h1_done, l2_ready, h2_done, a2_lin, a2_done, l3_ready, l3_seen, h3_done = (
            sem(n) for n in ("l1_ready", "l1_seen", "h1_lin", "h1_done", "l2_ready", "h2_done", "a2_lin", "a2_done",
                             "l3_ready", "l3_seen", "h3_done"))
        x3_ld, products, weighted, agg_ready, agg_used, out_st = (sem(n) for n in (
            "x3_ld", "products", "weighted", "agg_ready", "agg_used", "out_st"))

        chan = lambda rows, n, width: arena[0:rows, bass.ds(n * width, width)]
        hstat = reg[:, 0:2 * 6 * NCH].rearrange("p (j n) -> p j n", j=2)
        MK = kexp[:, 0:mlp_k.shape[1]]
        o = 0
        k1 = MK[0:GR, o:o + 5 * 2 * GR].rearrange("p (a n) -> p a n", a=5); o += 5 * 2 * GR
        k2 = MK[0:GR, o:o + 2 * GR].rearrange("p (h n) -> p h n", h=2); o += 2 * GR
        k3 = MK[0:GR, o:o + G]; o += G
        group_mean = MK[0:GR, o:o + GR]; o += GR
        all_mean = MK[0:G, o:o + P]; o += P
        g1, b1, g2, b2, g3, b3 = (MK[:, o + a:o + b] for a, b in ((0, 2), (2, 4), (4, 5), (5, 6), (6, 7), (7, 8)))
        L1w = ET[0:GR, 0:2 * GR]
        act2 = [S[0], S[1], pd[0]]
        att = arena[:, 0:TOTAL]
        att_part = lambda q: att[:, q * GB * PAIRS:(q + 1) * GB * PAIRS]

        def load_part(eng, q):
            eng.dma_start(arena[0:GR, q * PCOLS:(q + 1) * PCOLS],
                          sph_dram[q, :, :, :, :, :].rearrange("c f g p w -> (c f g) (p w)")).then_inc(mlp_ld, 16)

        free = arena[:, B * PAIRS:B * PAIRS + 2 * KNN * C]
        rbuf = [w.rearrange("p (k c) -> p k c", k=KNN) for w in (
            [gbuf[n][:, :, :].rearrange("p k r -> p (k r)")[:, 0:KNN * C] for n in range(2)]
            + [free[:, n * KNN * C:(n + 1) * KNN * C] for n in range(2)])]
        hmv = small[:, 0:4].rearrange("p (j s) -> p j s", j=2)
        stat, mean, tstd, dev = (small[:, o:o + 2] for o in (4, 6, 8, 10))
        gain, shift = small[:, 12:16], small[:, 16:20]

        def spherical_act(act, i):
            A = nc.scalar.activation
            act.wait_ge(sq_in, i + 1)
            A(tmp[0][:, :, :], tmp[0][:, :, :], ACT.Sqrt).then_inc(sqrt_done, 1)
            act.wait_ge(atan_in, i + 1)
            A(tmp[2][:, :, :], tmp[2][:, :, :], ACT.Arctan).then_inc(atan_done, 1)

        ROUNDS_AT = (0, 1, 1, 1, 1, 1, 1, 1, 0, 1, 1, 0)
        DIST_AT = {0: (2, 0), 1: (2, 1), 4: (4, 1), 5: (5, 0), 6: (5, 1), 7: (6, 0), 8: (7, 1)}
        COORDS_AT = {1: 0, 6: 3, 9: 5, 11: 6}
        NORMS_AT = {9: 0, 10: 1, 11: 2}
        BLK = stack.enter_context(nc.Block())
        waited = sem("waited")

        def settle(eng):
            eng.sem_inc(waited, 1)

        WCHUNKS = [(W, kc, w) for W, w in ((Wk, NKV * HD), (Wv, NKV * HD), (Wq, T), (Wo, T)) for kc in range(KC)]
        A_OF = {id(Wq): loraA[:, 0:1024], id(Wk): loraA[:, 1024:2048], id(Wv): loraA[:, 2048:3072], id(Wo): loraO}
        B_OF = {id(Wq): loraB[:, 0:1024], id(Wk): loraB[:, 1024:1280], id(Wv): loraB[:, 1280:1536],
                id(Wo): loraB[:, 1536:2560]}
        N_WLD = 16 * 6

        @BLK.sync
        def _(sp):
            for n in range(4):
                sp.dma_start((loraA[:, 1024 * n:1024 * n + 1024] if n < 3 else loraO), at[n, :, :]).then_inc(lora_ld, 16)
            for (lo, hi), d in (((0, 1024), bq), ((1024, 1280), bk), ((1280, 1536), bv), ((1536, 2560), bo)):
                sp.dma_start(loraB[:, lo:hi], d).then_inc(lora_ld, 16)
            for n, (W, d) in enumerate(((Wk, wk), (Wv, wv), (Wq, wq), (Wo, wo))):
                sp.dma_start(W, d.rearrange("(k p) n -> p k n", p=P)).then_inc(w1_ld[n], 16)
            for n in range(2):
                sp.dma_start(WL[n][:, 0:384], w_in[n, :, :]).then_inc(w_ld, 16)
            sp.dma_start(WL[0][:, 384:512], w_out[0, :, :]).then_inc(w_ld, 16)
            sp.dma_start(WL[1][:, 384:512], w_out[1, :, :]).then_inc(w_ld, 16)
            sp.dma_start(bL[:, :, :], b_qkv).then_inc(w_ld, 16)
            sp.dma_start(con[:, :], consts).then_inc(w_ld, 16)
            with sp.Fori(0, NB) as i:
                sp.wait_ge(sph_done, i + 2)
                b = (i + NB - 2) % NB
                sp.dma_start(sph_dram[b // GB, :, :, b % GB, :, :].rearrange("c f p w -> p (c f) w"),
                             sph[:, :, :].rearrange("p c (f w) -> p (c f) w", w=PW)).then_inc(sph_st, 16)
                for t in range(NT):
                    sp.wait_ge(rows_in[t % 2], i * (NT // 2 * KNN * 16) + (t // 2 + 1) * KNN * 16)
                    sp.sem_inc(arrived, 1)
                    sp.dma_start(rows_dram[t][i, :, :].rearrange("p (k c) -> p k c", k=KNN),
                                 gbuf[t % 2][:, :, 0:C]).then_inc(rows_st[t % 2], 16)
            for b in (NB, NB + 1):
                sp.wait_ge(sph_done, b + 2)
                sp.dma_start(sph_dram[(b - 2) // GB, :, :, (b - 2) % GB, :, :].rearrange("c f p w -> p (c f) w"),
                             sph[:, :, :].rearrange("p c (f w) -> p (c f) w", w=PW)).then_inc(sph_st, 16)
            for n in range(2):
                sp.wait_ge(rows_st[n], 16 * NB * NT // 2 + 16)
            sp.wait_ge(sph_st, 16 * (NB + 3))
            sp.wait_ge(x3_st, 16 * (NB + 1))
            sp.wait_ge(table_st, 16 * (NB + 1))
            load_part(sp, PARTS - 1)
            for q in range(PARTS):
                sp.wait_ge(l3_seen, (q + 1) * PCH // 2)
                sp.dma_start(h3_dram[q, :, :, :, :].rearrange("f g p w -> (f g) (p w)"),
                             arena[0:G, q * PCOLS:(q + 1) * PCOLS]).then_inc(h3_st, 16)
                sp.wait_ge(h3_st, 16 * (q + 1))
                for f in range(PIECES):
                    sp.dma_start(att_part(q).rearrange("p (b f w) -> p b f w", f=PIECES, w=PW)[:, :, f, :],
                                 h3_dram[q, f, :, :, :].rearrange("b p w -> p b w")).then_inc(att_ld, 16)
            with sp.Fori(0, NB) as i:
                for t in range(NT):
                    if t == NBUF - 1:
                        sp.wait_ge(agg_ready, i * NT + NBUF)
                        sp.dma_start(X0[:, :], x3_dram[i, :, :]).then_inc(x3_ld, 16)
                    sp.wait_ge(agg_ready, i * NT + t + 1)
                    sp.dma_start(rbuf[t % NBUF].rearrange("p k r -> p (k r)"),
                                 rows_dram[t][i, :, :]).then_inc(rows_ld[t % NBUF], 16)
            sp.wait_ge(out_st, 16 * (NB + 1))

        @BLK.gpsimd
        def _(pool):
            for n in range(2):
                pool.sem_inc(rows_st[n], 16)
            pool.wait_ge(prep_done, 1)
            for n in (1, 0):
                nc.gpsimd.memset(gbuf[n][:, :, C:ROW], 0.0).then_inc(arrived, NT)
            with pool.Fori(0, NB // 2) as pair:
                for odd in range(2):
                    i = pair * 2 + odd
                    pool.wait_ge(table_st, i * 16 + 32)
                    pool.wait_ge(idxp_done, i + 1)
                    for t in range(NT):
                        n = t % 2
                        pool.wait_ge(rows_st[n], i * (16 * NT // 2) + 16 * (t // 2) + 16)
                        pool.wait_ge(crd_done, i * NT + NT + t)
                        settle(pool)
                        for k in range(KNN):
                            nc.gpsimd.indirect_dma_start(
                                gbuf[n][:, k, :], None, table[odd],
                                bass.IndirectOffsetOnAxis(ap=idxp[:, odd, t, k:k + 1], axis=0)).then_inc(rows_in[n], 16)

        @BLK.tensor
        def _(pe):
            mm = nc.tensor.matmul
            pe.wait_ge(lora_ld, 16 * 8)
            for n, (W, kc, w) in enumerate(WCHUNKS):
                if n >= 2:
                    pe.wait_ge(lora_done, n - 1)
                for c in range(0, w, 512):
                    last = mm(SC[n % 2][:, c:min(c + 512, w)], A_OF[id(W)][:, kc * P:(kc + 1) * P],
                              B_OF[id(W)][:, c:min(c + 512, w)], start=True, stop=True)
                last.then_inc(lora_ps, 1)
            pe.wait_ge(w_ld, N_WLD)
            for n in range(2):
                last = mm(MISC[:, n:n + 1], WL[n][:, 384:512], bL[:, n, 2:3], start=True, stop=True)
            last.then_inc(bo_ps, 1)
            pe.wait_ge(prep_done, 1)

            def norms(b, part):
                pe.wait_ge(sq_done, b + 1)
                if part < 2:
                    if part:
                        pe.wait_ge(xx_evac, b * 3 + 1)
                    last = mm(PD[0:1, :], neghalf, X0[:, part * 512:(part + 1) * 512], start=True, stop=True)
                else:
                    pe.wait_ge(xx_evac, b * 3 + 2)
                    for t in range(NT):
                        last = mm(PD[:, t:t + 1], X0[:, t * P:(t + 1) * P], negone, start=True, stop=True)
                last.then_inc(xx_ready, 1)

            def distance(b, t, h):
                if t or h:
                    pe.wait_ge(pd_evac, b * 16 + 2 * t + h)
                else:
                    pe.wait_ge(xx_evac, b * 3 + 3)
                mm(PD[:, :], ctx[:, t * P:(t + 1) * P], ctx[:, h * 512:(h + 1) * 512], start=True, stop=False)
                mm(PD[:, :], ones_row, xxrow[0:1, h * 512:(h + 1) * 512], start=False, stop=True).then_inc(pd_ready, 1)

            for part in range(3):
                norms(0, part)
            for h in range(2):
                distance(0, 0, h)
            with pe.Fori(0, NB) as i:
                def groups(l, scores, values):
                    pe.wait_ge(q_evac, i * 3 + l + 1)
                    scores(0)
                    for g in range(4):
                        n = 4 * l + g
                        if g < 3:
                            scores(g + 1)
                        if n in DIST_AT:
                            distance(i, *DIST_AT[n])
                        if n in NORMS_AT:
                            norms(i + 1, NORMS_AT[n])
                        pe.wait_ge(probs_done, i * 12 + n + 1)
                        if n == 0:
                            pe.wait_ge(ctxT_evac, i + 1)
                        for b in range(2):
                            for j in range(4):
                                last = nc.tensor.transpose(TP[:, b * 512 + j * P:b * 512 + (j + 1) * P],
                                                           S[g % 2][:, b * 512 + j * P:b * 512 + (j + 1) * P], ident)
                        last.then_inc(probsT_ready, 1)
                        pe.wait_ge(et_evac, i * 12 + n + 1)
                        if n:
                            pe.wait_ge(ot_evac, i * 12 + n)
                        values(g)
                    pe.wait_ge(ot_evac, i * 12 + 4 * l + 4)

                def score_bank(l, g):
                    n = 4 * l + g
                    if g == 1 and l == 1:
                        pe.wait_ge(k_evac, i * 3 + l + 1)
                    if g >= 2:
                        pe.wait_ge(front_done, i * 12 + n - 1)
                    pe.wait_ge(kexp_done, i * 12 + n + 1)

                def chunk_attention(l):
                    w = WL[l // 2]
                    for h in range(2):
                        last = mm(SC[1][:, h * 512:(h + 1) * 512], w[:, 128:256], ctx[:, h * 512:(h + 1) * 512],
                                  start=True, stop=True)
                    last.then_inc(k_ready, 1)
                    if l == 0:
                        distance(i, 1, 0)
                    pe.wait_ge(k_evac, i * 3 + l + 1)
                    for half in range(2):
                        if half:
                            if l:
                                pe.wait_ge(oproj_used, i * 3 + l)
                            for h in range(2):
                                last = mm(SC[0][:, h * 512:(h + 1) * 512], w[:, 0:128],
                                          ctx[:, h * 512:(h + 1) * 512], start=True, stop=True)
                            last.then_inc(q_ready, 1)
                            pe.wait_ge(v2_evac, i * 4 + l + 1)
                        for c in range(8):
                            n = half * 8 + c
                            for h in range(2):
                                last = mm(TP[64 * h:64 * h + 64, c * P:(c + 1) * P],
                                          ctx[:, n * CHUNK:(n + 1) * CHUNK], w[:, 256:384], start=True, stop=True)
                        last.then_inc(v_ready, 1)
                    distance(i, *((7, 0) if l else (1, 1)))
                    pe.wait_ge(v2_evac, i * 4 + l + 2)
                    if l == 0:
                        for t in range(NT):
                            last = nc.tensor.transpose(TP[:, t * P:(t + 1) * P], ctx[:, t * P:(t + 1) * P], ident)
                        last.then_inc(ctxT_ready, 1)

                    def scores(g):
                        score_bank(l, g)
                        for j in range(4):
                            c = 4 * g + j
                            last = mm(SC[g % 2][64 * (j % 2):64 * (j % 2) + 64, (j // 2) * 512:(j // 2 + 1) * 512],
                                      q_sb[:, c * CHUNK:(c + 1) * CHUNK],
                                      kexp.rearrange("p (h t) -> p h t", h=H0)[:, :, j * CHUNK:(j + 1) * CHUNK],
                                      start=True, stop=True)
                        last.then_inc(scores_ready, 1)

                    def values(g):
                        for b in range(2):
                            for half in range(2):
                                for j in range(4):
                                    last = mm(MISC[32 * j:32 * j + 32, (2 * b + half) * 64:(2 * b + half + 1) * 64],
                                              V2[:, 4 * g + 2 * b + half, 32 * j:32 * j + 32],
                                              ET[:, b * 512 + j * P + 64 * half:b * 512 + j * P + 64 * half + 64],
                                              start=True, stop=True)
                        last.then_inc(av_ready, 1)

                    groups(l, scores, values)
                    for h in range(2):
                        last = mm(SC[0][:, h * 512:(h + 1) * 512], w[:, 384:512], OT[:, h * 512:(h + 1) * 512],
                                  start=True, stop=True)
                    last.then_inc(oproj_ready, 1)

                chunk_attention(0)

                distance(i, 3, 0)
                for c in range(2):
                    for kc in range(KC):
                        last = mm(SC[1][:, c * P:(c + 1) * P], Wk[:, kc, c * P:(c + 1) * P], ctxT[:, kc, :],
                                  start=(kc == 0), stop=(kc == KC - 1))
                last.then_inc(k_ready, 1)
                for kc in range(KC):
                    last = mm(MISC[:, 0:256], ctxT[:, kc, :], Wv[:, kc, :], start=(kc == 0), stop=(kc == KC - 1))
                last.then_inc(v1_ready, 1)
                distance(i, 3, 1)
                pe.wait_ge(xl_done, i * 3 + 1)
                for kc in range(KC):
                    last = nc.tensor.transpose(TP[:, kc * P:(kc + 1) * P], X1[:, kc * P:(kc + 1) * P], ident)
                last.then_inc(hT_ready, 1)
                pe.wait_ge(hT_evac, i + 1)
                for c in range(KC):
                    for kc in range(KC):
                        last = mm(SC[0][:, c * P:(c + 1) * P], Wq[:, kc, c * P:(c + 1) * P], hT[:, kc, :],
                                  start=(kc == 0), stop=(kc == KC - 1))
                last.then_inc(q_ready, 1)
                distance(i, 4, 0)
                pe.wait_ge(v1_evac, i + 1)

                def scores1(g):
                    score_bank(1, g)
                    for b in range(2):
                        c = 2 * g + b
                        last = mm(SC[g % 2][:, b * 512:(b + 1) * 512], q_sb[:, c * P:(c + 1) * P],
                                  kexp[:, (c // 4) * 512:(c // 4 + 1) * 512], start=True, stop=True)
                    last.then_inc(scores_ready, 1)

                def values1(g):
                    for b in range(2):
                        c = 2 * g + b
                        for j in range(4):
                            h = c // 4 * 4 + j
                            last = mm(MISC[32 * j:32 * j + 32, b * P:(b + 1) * P], V1[:, h * HD:(h + 1) * HD],
                                      ET[:, b * 512 + j * P:b * 512 + (j + 1) * P], start=True, stop=True)
                    last.then_inc(av_ready, 1)

                groups(1, scores1, values1)
                distance(i, 6, 1)
                for h in range(2):
                    for c in range(KC):
                        last = mm(SC[0][:, h * 512:(h + 1) * 512], OT[:, c * P:(c + 1) * P],
                                  Wo[:, c, h * 512:(h + 1) * 512], start=(c == 0), stop=(c == KC - 1))
                last.then_inc(oproj_ready, 1)

                chunk_attention(2)
                for h in range(2):
                    distance(i + 1, 0, h)
                pe.wait_ge(xl_done, i * 3 + 3)
                for t in range(NT):
                    last = nc.tensor.transpose(TP[:, t * P:(t + 1) * P], X0[:, t * P:(t + 1) * P], ident)
                last.then_inc(x3T_ready, 1)

            pe.wait_ge(pd_evac, NB * 16 + 2)
            def first_layer(n, u):
                for h in range(2):
                    last = mm(SC[u][0:GR, h * CW:(h + 1) * CW], L1w[:, h * GR:(h + 1) * GR], chan(GR, n, CW),
                              start=True, stop=True)
                last.then_inc(l1_ready, 1)

            def second_layer(n, u):
                pe.wait_ge(h1_done, n + 1)
                pe.wait_ge(h2_done, n + 1)
                for h in range(2):
                    last = mm(TP[0:GR, u * CW:(u + 1) * CW], k2[:, h, :], S[u][0:GR, h * CW:(h + 1) * CW],
                              start=(h == 0), stop=(h == 1))
                last.then_inc(l2_ready, 1)

            def norm_sums(l):
                for n in range(2):
                    pe.wait_ge(stat_in, 2 * l + n + 1)
                    if l < 2:
                        w = 2 - l
                        mm(PD[0:GR, 0:w], group_mean, stat[0:GR, 0:w], start=True, stop=True).then_inc(stat_ps, 1)
                    else:
                        mm(PD[:, 0:1], all_mean, stat[0:G, 0:1], start=True, stop=True).then_inc(stat_ps, 1)

            pe.sem_inc(l2_ready, 2)
            pe.sem_inc(l3_ready, 3)

            def first_pass(lo, hi):
                with pe.Fori(lo, hi) as i:
                    for u in range(2):
                        pe.wait_ge(l1_seen, i * 2 + u + 1)
                        first_layer(i * 2 + u, u)

            pe.wait_ge(coef_done, 1)
            if PARTS > 1:
                pe.wait_ge(mlp_ld, 16 * PARTS)
                first_pass(0, (NCH - PCH) // 2)
            pe.wait_ge(mlp_ld, 16 * (PARTS + 1))
            first_pass((NCH - PCH) // 2, NCH // 2)
            norm_sums(0)
            pe.wait_ge(coef_done, 2)
            first_layer(0, 0)
            with pe.Fori(0, NCH // 2 - 1) as i:
                for u in range(2):
                    n = i * 2 + u
                    pe.wait_ge(h1_lin, n + 2)
                    first_layer(n + 1, 1 - u)
                    second_layer(n, u)
            pe.wait_ge(h1_lin, NCH)
            first_layer(NCH - 1, 1)
            second_layer(NCH - 2, 0)
            second_layer(NCH - 1, 1)
            norm_sums(1)
            with pe.Fori(0, PARTS) as i:
                for u in range(PCH // 2):
                    n = i * (PCH // 2) + u
                    pe.wait_ge(a2_done, n + 1)
                    pe.wait_ge(h3_done, n + 1)
                    for h in range(2):
                        last = mm(SC[u % 2][0:G, h * CW:(h + 1) * CW], k3, act2[u % 3][0:GR, h * CW:(h + 1) * CW],
                                  start=True, stop=True)
                    last.then_inc(l3_ready, 1)
            norm_sums(2)
            pe.sem_inc(agg_ready, NBUF)
            with pe.Fori(0, NB) as i:
                for t in range(NT):
                    pe.wait_ge(weighted, i * NT + t + 1)
                    pe.wait_ge(agg_used, i * NT + t + 1)
                    for k in range(KNN - FOLD):
                        mm(SC[t % 2][:, 0:P], rbuf[t % NBUF][:, k, :], ident, start=(k == 0), stop=False)
                    if t == 0:
                        pe.wait_ge(x3_ld, i * 16 + 16)
                    mm(SC[t % 2][:, 0:P], ident, X0[:, t * P:(t + 1) * P], start=False, stop=True)\
                        .then_inc(agg_ready, 1)

        @BLK.scalar
        def _(act):
            A = nc.scalar.activation
            act.sem_inc(x3_st, 16)
            act.sem_inc(table_st, 16)
            act.wait_ge(w_ld, N_WLD)
            for n in range(2):
                A(bqs[:, n:n + 1], bL[:, n, 0:1], ACT.Copy, scale=0.25)
            act.dma_start(ctx[:, :], ctx_in[0, :, :]).then_inc(ctx_ld, 16)

            def norms(b, part):
                act.wait_ge(xx_ready, b * 3 + part + 1)
                if part < 2:
                    A(xxrow[0:1, part * 512:(part + 1) * 512], PD[0:1, :], ACT.Copy).then_inc(xx_evac, 1)
                else:
                    A(xxcol[:, :], PD[:, 0:NT], ACT.Copy).then_inc(xx_evac, 1)
                    act.wait_ge(xx_evac, b * 3 + 3)

            def distance(b, t, h):
                act.wait_ge(pd_ready, b * 16 + 2 * t + h + 1)
                if t >= 2 and h == 0:
                    act.wait_ge(topk_done, b * NT + t - 1)
                A(pd[t % 2][:, h * 512:(h + 1) * 512], PD[:, :], ACT.Identity,
                  bias=xxcol[:, t:t + 1], scale=2.0).then_inc(pd_evac, 1)

            def coordinates(b, t):
                act.wait_ge(arrived, b * NT + NT + t + 1)
                A(crd[:, t, :, :], gbuf[t % 2][:, :, C:ROW], ACT.Copy).then_inc(crd_done, 1)

            act.wait_ge(ctx_ld, 16)
            A(X0[:, :], ctx[:, :], ACT.Square).then_inc(sq_done, 1)
            for part in range(3):
                norms(0, part)
            for h in range(2):
                distance(0, 0, h)
            with act.Fori(0, NB // 2) as pair:
                for odd in range(2):
                    i = pair * 2 + odd

                    def groups(l, expand, scale):
                        for g in range(4):
                            n = 4 * l + g
                            if g < 3:
                                if l != 1:
                                    act.wait_ge(scores_ready, i * 12 + n + 1)
                                expand(g + 1)
                            act.wait_ge(front_done, i * 12 + n + 1)
                            A(S[g % 2][:, :], S[g % 2][:, :], ACT.Exp, scale=scale).then_inc(exp_done, 1)
                            if n in DIST_AT:
                                distance(i, *DIST_AT[n])
                            if n == 8:
                                act.dma_start(ctx[:, :], ctx_in[(i + 1) % NB, :, :]).then_inc(ctx_ld, 16)
                            if n == 9:
                                act.wait_ge(ctx_ld, i * 16 + 32)
                                act.wait_ge(pd_evac, i * 16 + 16)
                                A(X0[:, :], ctx[:, :], ACT.Square).then_inc(sq_done, 1)
                            if n in NORMS_AT:
                                norms(i + 1, NORMS_AT[n])
                            act.wait_ge(probsT_ready, i * 12 + n + 1)
                            A(ET[:, :], TP[:, :], ACT.Copy).then_inc(et_evac, 1)
                            act.wait_ge(av_ready, i * 12 + n + 1)
                            A(OT[:, g * 256:(g + 1) * 256], MISC[:, 0:256], ACT.Copy).then_inc(ot_evac, 1)
                            if n in COORDS_AT:
                                coordinates(i, COORDS_AT[n])

                    def chunk_attention(l):
                        b = l // 2
                        act.wait_ge(k_ready, i * 3 + l + 1)
                        A(kT, SC[1][:, :], ACT.Identity, bias=bL[:, b, 1:2]).then_inc(k_evac, 1)
                        if l == 0:
                            distance(i, 1, 0)
                        else:
                            coordinates(i, 4)
                        act.wait_ge(k_evac, i * 3 + l + 1)

                        def expand(g):
                            for h in range(H0):
                                last = A(kexp[:, h * 256:(h + 1) * 256], kT[:, g * 256:(g + 1) * 256], ACT.Copy,
                                         scale=headmask[:, h:h + 1])
                            last.then_inc(kexp_done, 1)

                        expand(0)
                        for half in range(2):
                            act.wait_ge(v_ready, i * 4 + l + half + 1)
                            for e in range(2):
                                last = A(V2flat[:, half * 32:half * 32 + 32, e, :],
                                         TP[:, :].rearrange("p (c e d) -> p c e d", e=2, d=D0)[:, :, e, :],
                                         ACT.Copy, scale=parity[:, e * D0:e * D0 + 1])
                            last.then_inc(v2_evac, 1)
                            if half == 0:
                                act.wait_ge(q_ready, i * 3 + l + 1)
                                A(q_sb, SC[0][:, :], ACT.Identity, bias=bqs[:, b:b + 1], scale=0.25).then_inc(q_evac, 1)
                        distance(i, *((7, 0) if l else (1, 1)))
                        if l == 0:
                            act.wait_ge(x3_st, i * 16 + 16)
                            act.dma_start(X0[:, :], x_in[i, :, :]).then_inc(x_ld, 16)
                            coordinates(i - 1, NT - 1)
                            act.wait_ge(ctxT_ready, i + 1)
                            act.wait_ge(own_saved, i + 1)
                            A(ctxT[:, :, :].rearrange("p t c -> p (t c)"), TP[:, :], ACT.Copy).then_inc(ctxT_evac, 1)
                            spherical_act(act, i)
                        groups(l, expand, 1.0)
                        if l == 0:
                            distance(i, 3, 0)
                        else:
                            distance(i + 1, 0, 0)
                        act.wait_ge(var_done, i * 2 + b + 1)
                        A(std[:, :], mv[:, 1:2], ACT.Sqrt, bias=eps).then_inc(std_done, 1)

                    mrow = mask_in[i, :, :]
                    halves = mrow.rearrange("a (c h k) -> a c h k", h=2, k=CHUNK)
                    for h in range(2):
                        act.dma_start(mb[64 * h:64 * h + 64, :].rearrange("p (c k) -> p c k", k=CHUNK),
                                      halves[0, :, h, :].partition_broadcast(64)).then_inc(mask_ld, 16)
                    act.dma_start(maskT[:, :], mrow[0, :].partition_broadcast(P)).then_inc(mask_ld, 16)
                    chunk_attention(0)

                    coordinates(i, 1)
                    act.wait_ge(k_ready, i * 3 + 2)
                    halves = kexp.rearrange("p (c j t) -> p c j t", c=4, j=4)[:, 0:2, :, :]
                    for j in range(4):
                        last = A(halves[:, :, j, :], SC[1][:, 0:256].rearrange("p (c t) -> p c t", c=2), ACT.Copy,
                                 scale=quadmask[:, j:j + 1])
                    last.then_inc(k_evac, 1)
                    act.wait_ge(v1_ready, i + 1)
                    A(V1, MISC[:, 0:256], ACT.Copy).then_inc(v1_evac, 1)
                    distance(i, 3, 1)
                    act.wait_ge(hT_ready, i + 1)
                    A(hT.rearrange("p k n -> p (k n)"), TP[:, :], ACT.Copy).then_inc(hT_evac, 1)
                    act.wait_ge(q_ready, i * 3 + 2)
                    A(q_sb, SC[0][:, :], ACT.Copy).then_inc(q_evac, 1)
                    distance(i, 4, 0)
                    coordinates(i, 2)
                    act.wait_ge(k_evac, i * 3 + 2)

                    def expand1(g):
                        act.sem_inc(kexp_done, 1)

                    expand1(0)
                    groups(1, expand1, float(HD) ** -0.5)
                    distance(i, 6, 1)

                    chunk_attention(2)

                    distance(i + 1, 0, 1)

                    act.wait_ge(xl_done, i * 3 + 3)
                    act.dma_start(x3_dram[i, :, :], X0[:, :]).then_inc(x3_st, 16)
                    act.wait_ge(table_st, i * 16 + 16)
                    act.wait_ge(x3T_ready, i + 1)
                    A(tab[:, :, 0:C], TP[:, :].rearrange("p (t c) -> p t c", t=NT), ACT.Copy).then_inc(tab_done, 1)
                    A(tab[:, :, C:ROW], ctxT[:, :, 0:4], ACT.Copy).then_inc(tab_done, 1)
                    act.wait_ge(tab_done, i * 2 + 2)
                    act.dma_start(table[odd].rearrange("(t p) r -> p t r", p=P), tab).then_inc(table_st, 16)
            coordinates(NB - 1, NT - 1)
            act.wait_ge(x3_st, 16 * (NB + 1))
            act.wait_ge(table_st, 16 * (NB + 1))
            act.wait_ge(sph_st, 16 * (NB + 1))
            act.dma_start(MK, mlp_k).then_inc(mlp_ld, 16)
            for q in range(PARTS - 1):
                load_part(act, q)
            spherical_act(act, NB)
            act.wait_ge(own_saved, NB + 1)
            for t in range(NT):
                coordinates(NB, t)
            spherical_act(act, NB + 1)

            act.sem_inc(h1_lin, 2)
            act.sem_inc(h3_done, 2)

            def norm_root(l, rows):
                act.wait_ge(stat_ps, 2 * l + 2)
                w = 2 if l == 0 else 1
                A(tstd[0:rows, 0:w], PD[0:rows, 0:w], ACT.Sqrt, bias=eps[0:rows, :]).then_inc(tstd_done, 1)
                act.wait_ge(coef_done, l + 2)

            norm_root(0, GR)
            with act.Fori(0, NCH // 2) as i:
                for u in range(2):
                    n = i * 2 + u
                    act.wait_ge(l1_ready, n + NCH + 1)
                    act.wait_ge(l2_ready, n + 1)
                    for h in range(2):
                        last = A(S[u][0:GR, h * CW:(h + 1) * CW], SC[u][0:GR, h * CW:(h + 1) * CW], ACT.Identity,
                                 scale=gain[0:GR, h:h + 1], bias=shift[0:GR, h:h + 1])
                    last.then_inc(h1_lin, 1)
            norm_root(1, GR)

            def second_norm(n, u):
                act.wait_ge(l3_ready, n + 1)
                settle(act)
                A(act2[u % 3][0:GR, :], chan(GR, n, 2 * CW), ACT.Identity,
                  scale=gain[0:GR, 2:3], bias=shift[0:GR, 2:3]).then_inc(a2_lin, 1)

            def logits(n, u):
                act.wait_ge(l3_ready, n + 4)
                settle(act)
                A(chan(G, n, 2 * CW), SC[u % 2][0:G, :], ACT.Copy).then_inc(h3_done, 1)

            def third_part(first, last):
                for u in range(PCH // 2):
                    if not last or u + 2 < PCH // 2:
                        second_norm(first + u + 2, u + 2)
                    logits(first + u, u)

            for n in range(2):
                second_norm(n, n)
            if PARTS > 1:
                with act.Fori(0, PARTS - 1) as i:
                    third_part(i * (PCH // 2), False)
            third_part((PARTS - 1) * (PCH // 2), True)
            norm_root(2, P)
            act.wait_ge(att_ld, 16 * PIECES * PARTS)
            for q in range(PARTS):
                A(att_part(q), att_part(q), ACT.Identity, scale=gain[:, 3:4], bias=shift[:, 3:4]).then_inc(att_lin, 1)

            def exponentials(q):
                act.wait_ge(att_in, q + 1)
                A(att_part(q), att_part(q), ACT.Exp).then_inc(att_exp, 1)

            act.sem_inc(agg_used, 2)
            act.sem_inc(out_st, 16)
            exponentials(0)
            for q in range(PARTS):
                if q + 1 < PARTS:
                    exponentials(q + 1)
                with act.Fori(q * GB, (q + 1) * GB) as i:
                    act.wait_ge(out_st, i * 16 + 16)
                    for t in range(NT):
                        act.wait_ge(agg_ready, i * NT + t + 1 + NBUF)
                        A(X1[:, t * P:(t + 1) * P], SC[t % 2][:, 0:P], ACT.Copy).then_inc(agg_used, 1)
                    act.wait_ge(agg_used, i * NT + NT + 2)
                    act.dma_start(out[i, :, :], X1[:, :]).then_inc(out_st, 16)

        @BLK.vector
        def _(dve):
            V = nc.vector
            dve.sem_inc(sph_done, 1)
            V.memset(ctxT[:, :, 0:4], 0.0)
            V.memset(crd[:, :, :, :], 0.0)
            V.memset(own[:, :, :], 0.0)
            for n, (W, kc, w) in enumerate(WCHUNKS):
                if kc == 0:
                    dve.wait_ge(w1_ld[n // KC], 16)
                dve.wait_ge(lora_ps, n + 1)
                V.scalar_tensor_tensor(W[:, kc, :], SC[n % 2][:, 0:w], LORA, W[:, kc, :],
                                       ALU.mult, ALU.add).then_inc(lora_done, 1)
            dve.wait_ge(lora_done, len(WCHUNKS))
            dve.wait_ge(w_ld, N_WLD)
            dve.wait_ge(bo_ps, 1)
            V.tensor_tensor(bof[:, :], MISC[:, 0:2], bL[:, :, 3], ALU.add).then_inc(prep_done, 1)
            dve.wait_ge(prep_done, 1)

            def relative(i):
                dve.wait_ge(crd_done, i * NT + 1)
                for c in range(3):
                    last = V.tensor_tensor(rel[:, c, :].rearrange("p (t k) -> p t k", t=NT), crd[:, :, :, c],
                                           own[:, :, c].unsqueeze(2).broadcast_to([P, NT, KNN]), ALU.subtract)
                last.then_inc(rel_done, 1)
                dve.wait_ge(rel_done, i + 1)
                V.tensor_copy(own[:, :, :], ctxT[:, :, 0:4]).then_inc(own_saved, 1)
                dve.wait_ge(own_saved, i + 1)

            def spherical(i, step):
                r_xy, den, t2, t3, corr = tmp
                step(V.tensor_tensor(t2[:, :, :], rel[:, 0:2, :], rel[:, 0:2, :], ALU.mult))
                V.tensor_tensor(t3[:, 0, :], rel[:, 2, :], rel[:, 2, :], ALU.mult)
                step(V.tensor_tensor(den[:, 0, :], t2[:, 0, :], t2[:, 1, :], ALU.add))
                step(V.tensor_tensor(den[:, 1, :], den[:, 0, :], t3[:, 0, :], ALU.add))
                V.tensor_scalar(t3[:, :, :], den[:, :, :], TINY, None, ALU.is_ge)
                V.tensor_scalar(r_xy[:, :, :], den[:, :, :], TINY, None, ALU.max).then_inc(sq_in, 1)
                dve.wait_ge(sqrt_done, i + 1)
                dve.wait_ge(sph_st, i * 16 + 16)
                V.tensor_copy(sph[:, 0, :], r_xy[:, 1, :])
                V.scalar_tensor_tensor(den[:, 0, :], rel[:, 0, :], -1.0, rel[:, 0, :], ALU.mult, ALU.max)
                V.tensor_copy(den[:, 1, :], r_xy[:, 0, :])
                step(V.scalar_tensor_tensor(t2[:, :, :], rel[:, 1:3, :], -1.0, rel[:, 1:3, :], ALU.mult, ALU.max))
                num = t2
                step(V.tensor_tensor(r_xy[:, :, :], num[:, :, :], den[:, :, :], ALU.max))
                step(V.tensor_scalar(r_xy[:, :, :], r_xy[:, :, :], 1e-30, None, ALU.max))
                step(V.reciprocal(r_xy[:, :, :], r_xy[:, :, :]))
                big = X1[:, 2 * PAIRS:4 * PAIRS].rearrange("p (a n) -> p a n", a=2)
                V.tensor_tensor(big, num[:, :, :], den[:, :, :], ALU.is_gt)
                step(V.tensor_tensor(num[:, :, :], num[:, :, :], den[:, :, :], ALU.min))
                V.tensor_tensor(num[:, :, :], num[:, :, :], r_xy[:, :, :], ALU.mult).then_inc(atan_in, 1)
                dve.wait_ge(atan_in, i + 1)
                V.tensor_scalar(r_xy[:, :, :], rel[:, 1:3, :], 0.0, -2.0, ALU.is_lt, ALU.mult)
                step(V.tensor_scalar(den[:, 0, :], rel[:, 0, :], 0.0, None, ALU.is_lt))
                step(V.tensor_scalar(r_xy[:, :, :], r_xy[:, :, :], 1.0, None, ALU.add))
                dve.wait_ge(atan_done, i + 1)
                a = num
                step(V.tensor_scalar(corr, a[:, :, :], -2.0, float(np.pi / 2), ALU.mult, ALU.add))
                step(V.tensor_tensor(corr, corr, big, ALU.mult))
                step(V.tensor_tensor(a[:, :, :], a[:, :, :], corr, ALU.add))
                step(V.tensor_scalar(corr[:, 0, :], a[:, 0, :], -2.0, float(np.pi), ALU.mult, ALU.add))
                step(V.tensor_tensor(corr[:, 0, :], corr[:, 0, :], den[:, 0, :], ALU.mult))
                step(V.tensor_tensor(a[:, 0, :], a[:, 0, :], corr[:, 0, :], ALU.add))
                step(V.tensor_tensor(a[:, :, :], a[:, :, :], r_xy[:, :, :], ALU.mult))
                V.tensor_tensor(sph[:, 1, :], a[:, 1, :], t3[:, 1, :], ALU.mult)
                step(V.tensor_tensor(sph[:, 2, :], a[:, 0, :], t3[:, 0, :], ALU.mult))
                dve.sem_inc(sph_done, 1)

            dve.sem_inc(sph_st, 16)
            with dve.Fori(0, NB) as i:
                chain = [0]

                def step(ins):
                    chain[0] += 1
                    ins.then_inc(dve_step, 1)
                    dve.wait_ge(dve_step, i * DVE_STEPS + chain[0])

                rounds = [0]

                def search_round():
                    t, r = divmod(rounds[0], ROUNDS)
                    rounds[0] += 1
                    buf = pd[t % 2]
                    if r == 0:
                        dve.wait_ge(pd_evac, i * 16 + 2 * t + 2)
                    m = m8[:, 8 * r:8 * r + 8]
                    settle(dve)
                    step(V.max(m, buf[:, :]))
                    settle(dve)
                    last = V.max_index(idx[:, t, 8 * r:8 * r + 8], m, buf[:, :])
                    if r < ROUNDS - 1:
                        step(V.match_replace(buf[:, :], m, buf[:, :], -3.0e38))
                    else:
                        last.then_inc(topk_done, 1)

                def groups(l, front, keys):
                    for g in range(4):
                        n = 4 * l + g
                        s = S[g % 2]
                        dve.wait_ge(scores_ready, i * 12 + n + 1)
                        if n >= 2:
                            dve.wait_ge(probsT_ready, i * 12 + n - 1)
                        front(g, s)
                        dve.wait_ge(front_done, i * 12 + n + 1)
                        for _ in range(ROUNDS_AT[n]):
                            search_round()
                        dve.wait_ge(exp_done, i * 12 + n + 1)
                        rows = T // keys
                        e = s[:, :].rearrange("p (r k) -> p r k", k=keys)
                        step(V.reduce_sum(sm[:, 0:rows], e, AX.X))
                        step(V.reciprocal(sm[:, 0:rows], sm[:, 0:rows]))
                        V.tensor_tensor(e, e, sm[:, 0:rows].unsqueeze(2).broadcast_to([P, rows, keys]), ALU.mult)\
                            .then_inc(probs_done, 1)

                def chunk_attention(l, x_res, y):
                    b = l // 2
                    def front(g, s):
                        rows = s[:, :].rearrange("p (b h k) -> p b h k", b=2, h=H0)
                        bias = mb[:, g * 128:(g + 1) * 128].rearrange("p (b k) -> p b k", b=2)
                        for b_ in range(2):
                            last = V.tensor_tensor(rows[:, b_, :, :],
                                                   SC[g % 2][:, b_ * 512:(b_ + 1) * 512].rearrange("p (h k) -> p h k", h=H0),
                                                   bias[:, b_, :].unsqueeze(1).broadcast_to([P, H0, CHUNK]), ALU.add)
                        step(last)
                        e = s[:, :].rearrange("p (r k) -> p r k", k=CHUNK)
                        step(V.reduce_max(mx[:, :], e, AX.X))
                        V.tensor_tensor(e, e, mx[:, :].unsqueeze(2).broadcast_to([P, 16, CHUNK]), ALU.subtract)\
                            .then_inc(front_done, 1)

                    groups(l, front, CHUNK)
                    for _ in range(2):
                        search_round()
                    if l:
                        dve.wait_ge(topk_done, i * NT + NT)
                        V.tensor_copy(idxp[:, i % 2, :, :], idx[:, :, 0:KNN]).then_inc(idxp_done, 1)
                    dve.wait_ge(oproj_ready, i * 3 + l + 1)
                    V.scalar_tensor_tensor(y[:, :], SC[0][:, :], bof[:, b:b + 1], maskT[:, :], ALU.add, ALU.mult)\
                        .then_inc(oproj_used, 1)
                    dve.wait_ge(oproj_used, i * 3 + l + 1)
                    if l == 0:
                        dve.wait_ge(x_ld, i * 16 + 16)
                    step(V.tensor_tensor(y[:, :], y[:, :], x_res[:, :], ALU.add))
                    for h in range(2):
                        last = V.bn_stats(bst[:, h, :], y[:, h * 512:(h + 1) * 512])
                    step(last)
                    settle(dve)
                    V.bn_aggr(mv[:, :], bst[:, :, :].rearrange("p a b -> p (a b)")).then_inc(var_done, 1)
                    dve.wait_ge(std_done, i * 2 + b + 1)
                    step(V.reciprocal(rstd[:, :], std[:, :]))
                    V.tensor_scalar(y[:, :], y[:, :], mv[:, 0:1], rstd[:, 0:1], ALU.subtract, ALU.mult)\
                        .then_inc(xl_done, 1)

                for _ in range(4):
                    search_round()
                relative(i)
                spherical(i, step)
                dve.wait_ge(mask_ld, i * 48 + 48)
                step(V.tensor_scalar(mb[:, :], mb[:, :], 0.0, NEG, ALU.is_le, ALU.mult))
                chunk_attention(0, X0, X1)
                for _ in range(7):
                    search_round()

                def front1(g, s):
                    sc = SC[g % 2][:, :].rearrange("p (r k) -> p r k", k=P)
                    step(V.reduce_max(mx[:, 0:8], sc, AX.X))
                    V.tensor_tensor(s[:, :].rearrange("p (r k) -> p r k", k=P), sc,
                                    mx[:, 0:8].unsqueeze(2).broadcast_to([P, 8, P]), ALU.subtract)\
                        .then_inc(front_done, 1)

                groups(1, front1, P)
                for _ in range(6):
                    search_round()
                dve.wait_ge(oproj_ready, i * 3 + 2)
                V.tensor_tensor(X1[:, :], SC[0][:, :], X1[:, :], ALU.add).then_inc(xl_done, 1)
                dve.wait_ge(xl_done, i * 3 + 2)
                dve.sem_inc(oproj_used, 1)
                for _ in range(2):
                    search_round()
                chunk_attention(2, X1, X0)
                assert rounds[0] == NT * ROUNDS
                assert chain[0] == DVE_STEPS, chain[0]
            tail = [0]

            def step_tail(ins):
                tail[0] += 1
                ins.then_inc(dve_step, 1)
                dve.wait_ge(dve_step, NB * DVE_STEPS + tail[0])

            relative(NB)
            spherical(NB, step_tail)
            step = step_tail
            dve.sem_inc(l1_seen, 2)
            dve.sem_inc(h2_done, 2)
            dve.wait_ge(mlp_ld, 16 * PARTS)
            V.tensor_tensor(L1w, k1[:, 0, :], k1[:, 1, :], ALU.add)
            step(V.tensor_tensor(k1[:, 2, :], k1[:, 2, :], k1[:, 3, :], ALU.add))
            step(V.tensor_tensor(k1[:, 2, :], k1[:, 2, :], k1[:, 4, :], ALU.add))
            step(V.scalar_tensor_tensor(L1w, k1[:, 2, :], -1.0 / 3.0, L1w, ALU.mult, ALU.add))
            dve.sem_inc(coef_done, 1)

            def batch_norm(l, rows, out_rows, g, b):
                w, o = ((2, 0), (1, 2), (1, 3))[l]
                settle(dve)
                for j in range(w):
                    last = V.bn_aggr(hmv[0:rows, j, :], hstat[0:rows, j, :])
                step(last)
                step(V.tensor_copy(stat[0:rows, 0:w], hmv[0:rows, 0:w, 0]))
                dve.sem_inc(stat_in, 1)
                dve.wait_ge(stat_ps, 2 * l + 1)
                step(V.tensor_copy(mean[0:out_rows, 0:w], PD[0:out_rows, 0:w]))
                step(V.tensor_tensor(dev[0:rows, 0:w], hmv[0:rows, 0:w, 0], mean[0:rows, 0:w], ALU.subtract))
                step(V.tensor_tensor(dev[0:rows, 0:w], dev[0:rows, 0:w], dev[0:rows, 0:w], ALU.mult))
                step(V.tensor_tensor(stat[0:rows, 0:w], dev[0:rows, 0:w], hmv[0:rows, 0:w, 1], ALU.add))
                dve.sem_inc(stat_in, 1)
                dve.wait_ge(tstd_done, l + 1)
                gain_l, shift_l = gain[0:out_rows, o:o + w], shift[0:out_rows, o:o + w]
                step(V.reciprocal(gain_l, tstd[0:out_rows, 0:w]))
                step(V.tensor_tensor(gain_l, gain_l, g[0:out_rows, :], ALU.mult))
                step(V.tensor_tensor(dev[0:out_rows, 0:w], gain_l, mean[0:out_rows, 0:w], ALU.mult))
                step(V.tensor_tensor(shift_l, b[0:out_rows, :], dev[0:out_rows, 0:w], ALU.subtract))
                dve.sem_inc(coef_done, 1)

            def first_stats(lo, hi):
                with dve.Fori(lo, hi) as i:
                    for u in range(2):
                        n = i * 2 + u
                        dve.wait_ge(l1_ready, n + 1)
                        settle(dve)
                        for h in range(2):
                            last = V.bn_stats(hstat[0:GR, h, bass.ds(n * 6, 6)], SC[u][0:GR, h * CW:(h + 1) * CW])
                        last.then_inc(l1_seen, 1)

            if PARTS > 1:
                first_stats(0, (NCH - PCH) // 2)
            relative(NB + 1)
            spherical(NB + 1, step)
            first_stats((NCH - PCH) // 2, NCH // 2)
            dve.wait_ge(l1_seen, NCH + 2)
            batch_norm(0, GR, GR, g1, b1)

            def leaky(buf, n, lin, done):
                s = buf[0:GR, :]
                dve.wait_ge(lin, n)
                V.scalar_tensor_tensor(s, s, 0.2, s, ALU.mult, ALU.max).then_inc(done, 1)

            def second_stats(n, u):
                dve.wait_ge(l2_ready, n + 3)
                settle(dve)
                V.bn_stats(hstat[0:GR, 0, bass.ds(n * 6, 6)], TP[0:GR, u * CW:(u + 1) * CW])
                V.tensor_copy(chan(GR, n, CW), TP[0:GR, u * CW:(u + 1) * CW]).then_inc(h2_done, 1)

            leaky(S[0], 3, h1_lin, h1_done)
            with dve.Fori(0, NCH // 2 - 1) as i:
                for u in range(2):
                    leaky(S[1 - u], i * 2 + u + 4, h1_lin, h1_done)
                    second_stats(i * 2 + u, u)
            leaky(S[1], NCH + 2, h1_lin, h1_done)
            second_stats(NCH - 2, 0)
            second_stats(NCH - 1, 1)
            dve.wait_ge(h2_done, NCH + 2)
            batch_norm(1, GR, GR, g2, b2)

            def third_stats(n):
                dve.wait_ge(h3_done, n + 3)
                settle(dve)
                for h in range(2):
                    last = V.bn_stats(hstat[0:G, 0, bass.ds(n * 12 + h * 6, 6)], chan(G, n * 2 + h, CW))
                last.then_inc(l3_seen, 1)

            def third_part(first, last):
                for u in range(PCH // 2):
                    if not last or u + 2 < PCH // 2:
                        leaky(act2[(u + 2) % 3], first + u + 3, a2_lin, a2_done)
                    third_stats(first + u)

            for n in range(2):
                leaky(act2[n], n + 1, a2_lin, a2_done)
            if PARTS > 1:
                with dve.Fori(0, PARTS - 1) as i:
                    third_part(i * (PCH // 2), False)
            third_part((PARTS - 1) * (PCH // 2), True)
            dve.wait_ge(l3_seen, NCH // 2)
            batch_norm(2, G, P, g3, b3)
            rows = GB * NT
            parts = [(att_part(q).rearrange("p (r k) -> p r k", k=KNN), att_mx[:, q * rows:(q + 1) * rows])
                     for q in range(PARTS)]

            def shifted(q):
                a, m = parts[q]
                dve.wait_ge(att_lin, q + 1)
                step(V.scalar_tensor_tensor(a, a, 0.2, a, ALU.mult, ALU.max))
                step(V.reduce_max(m, a, AX.X))
                V.tensor_tensor(a, a, m.unsqueeze(2).broadcast_to([P, rows, KNN]), ALU.subtract).then_inc(att_in, 1)

            shifted(0)
            for q in range(PARTS):
                if q + 1 < PARTS:
                    shifted(q + 1)
                a, m = parts[q]
                dve.wait_ge(att_exp, q + 1)
                step(V.reduce_sum(m, a, AX.X))
                step(V.reciprocal(m, m))
                step(V.tensor_tensor(a, a, m.unsqueeze(2).broadcast_to([P, rows, KNN]), ALU.mult))
                with dve.Fori(q * GB, (q + 1) * GB) as i:
                    for t in range(NT):
                        b = rbuf[t % NBUF]
                        dve.wait_ge(rows_ld[t % NBUF], i * (NT // NBUF * 16) + (t // NBUF + 1) * 16)
                        weights = att[:, bass.ds(i * PAIRS + t * KNN, KNN)]
                        V.tensor_tensor(b, b, weights.unsqueeze(2).broadcast_to([P, KNN, C]),
                                        ALU.mult).then_inc(products, 1)
                        dve.wait_ge(products, i * NT + t + 1)
                        V.tensor_tensor(b[:, 0:FOLD, :], b[:, 0:FOLD, :], b[:, KNN - FOLD:KNN, :],
                                        ALU.add).then_inc(weighted, 1)


def constants():
    p = np.arange(P)
    c = np.zeros((P, 399), np.float32)
    c[:, 0:128] = np.eye(P)
    c[:, 128:256] = (p[:, None] // 64) == (p[None, :] // D0) % 2
    c[:, 256:264] = (p[:, None] // D0) == np.arange(H0)[None, :]
    c[:, 264:268] = (p[:, None] // HD) == np.arange(4)[None, :]
    c[:, 268] = -0.5
    c[:, 269] = -1.0
    c[:, 270] = EPS
    c[:, 271:399] = 1.0
    return c


def mlp_layout(d):
    g = lambda n: np.asarray(d[f"L3_xattn_{n}"])
    groups = PIECES * min(8, np.asarray(d["x"]).shape[0])

    def blocks(w):
        k = np.zeros((w.shape[0], groups, w.shape[1], groups), w.dtype)
        for n in range(groups):
            k[:, n, :, n] = w
        return k.reshape(w.shape[0] * groups, -1)

    w1, w2, w3 = g("W1"), g("W2"), g("W3")
    rep = lambda v: np.repeat(v, groups)[:, None]
    parts = [blocks(w1[:, 0:3].T), blocks(w1[:, 3:6].T)]
    parts += [blocks(np.stack([w1[:, 3 + c]] * 3)) for c in range(3)]
    parts += [blocks(w2[:, 0:3].T), blocks(w2[:, 3:6].T), blocks(w3.T)]
    parts += [np.repeat(np.repeat(np.eye(3, dtype=np.float32), groups, 0), groups, 1) / np.float32(groups)]
    full = np.zeros((P, P), np.float32)
    full[0:groups, :] = 1.0 / groups
    parts += [full] + [rep(v) for n in ("g1", "b1") for v in (g(n)[0:3], g(n)[3:6])] + [rep(g("g2")), rep(g("b2"))]
    parts += [np.full((P, 1), g(n)[0], np.float32) for n in ("g3", "b3")]
    return np.concatenate([np.pad(a, ((0, P - a.shape[0]), (0, 0))) for a in parts], axis=1)


def layout(d):
    g = lambda n: np.asarray(d[n])
    t = lambda a: np.ascontiguousarray(a)
    heads = np.arange(T).reshape(2, 4, NH // NKV, HD).transpose(0, 2, 1, 3).reshape(-1)
    bias = np.stack([np.concatenate([g(f"L{l}_xattn_b_in").reshape(3, C), g(f"L{l}_xattn_b_out").reshape(1, C)])
                     for l in (0, 2)])
    return {
        "x": t(g("x")), "ctx": t(g("ctx_4096")), "mask": t(g("mask_Bx1x4096_ff1")),
        "w_in": t(np.stack([g(f"L{l}_xattn_W_in").T for l in (0, 2)])),
        "b_qkv": t(bias.transpose(2, 0, 1)),
        "w_out": t(np.stack([g(f"L{l}_xattn_W_out").T for l in (0, 2)])),
        "wq": t(g("L1_xattn_Wq")[:, heads]), "wk": t(g("L1_xattn_Wk")), "wv": t(g("L1_xattn_Wv")), "wo": t(g("L1_xattn_Wo")[heads]),
        "at": t(np.stack([g(f"L1_xattn_A{n}").T for n in "qkv"] + [g("L1_xattn_Ao")[heads].T])),
        "bq": t(g("L1_xattn_Bq")[:, heads]), "bk": t(g("L1_xattn_Bk")), "bv": t(g("L1_xattn_Bv")), "bo": t(g("L1_xattn_Bo")),
        "mlp_k": mlp_layout(d),
        "consts": constants(),
    }


def kernel(**inputs):
    import concourse.bacc as bacc
    from concourse.bass_utils import run_bass_kernel_spmd

    nc = bacc.Bacc("TRN2", target_bir_lowering=False, num_devices=1)
    arrays = layout(inputs)
    aps = [nc.dram_tensor(f"in_{n}", a.shape, mybir.dt.from_np(a.dtype), kind="ExternalInput").ap()
           for n, a in arrays.items()]
    out = nc.dram_tensor("out", (B, C, T), mybir.dt.float32, kind="ExternalOutput").ap()
    program(nc, *aps, out)
    r = run_bass_kernel_spmd(nc, [{f"in_{n}": a for n, a in arrays.items()}], core_ids=[0])
    return r.results[0]["out"]
```
